# Optimizing a Trainium2 kernel written in Bass

```python
import numpy as np
import jax
import jax.numpy as jnp

def _softmax(x, axis=-1):
    return jax.nn.softmax(x, axis=axis)

def _gelu(x):
    return jax.nn.gelu(x, approximate=True)

def _silu(x):
    return jax.nn.silu(x)

def _sigmoid(x):
    return jax.nn.sigmoid(x)

def _layernorm(x, axis=-1, eps=1e-05):
    m = jnp.mean(x, axis=axis, keepdims=True)
    v = jnp.var(x, axis=axis, keepdims=True)
    return (x - m) / jnp.sqrt(v + eps)

def _scatter_add(tgt, idx, src, axis=0):
    return tgt.at[idx].add(src)

def _segment_sum(src, seg, n):
    return jax.ops.segment_sum(src, seg, n)
kernel_name = 'mk_decoder_preln_d2_seqx_r4_423d8f'

def setup_inputs(seed: int=0):
    np.random.seed(seed)
    _w = jnp.asarray

    def _rec_inputs():
        import jax
        import jax.numpy as jnp
        _rk = jax.random.key(seed)
        x = -0.000125 + 0.9999 * jax.random.normal(jax.random.fold_in(_rk, 1), (4, 512, 512), jnp.float32)
        _lenS = 512 - jax.random.randint(jax.random.fold_in(_rk, 7), (4,), 0, max(1, 512 // 4) + 1, jnp.int32)
        _lenS2 = 512 - jax.random.randint(jax.random.fold_in(_rk, 8), (4,), 0, max(1, 512 // 4) + 1, jnp.int32)
        _ctx_2048P = jax.random.normal(jax.random.fold_in(_rk, 11), (4, 16, 512), jnp.float32)
        _ctx_2048c = jax.random.dirichlet(jax.random.fold_in(_rk, 511), 0.3 * jnp.ones((16,), jnp.float32), (4, 512))
        _ctx_2048t = jnp.einsum('bsk,bkd->bsd', _ctx_2048c, _ctx_2048P)
        _ctx_2048t = _ctx_2048t * jax.lax.rsqrt(jnp.mean(jnp.square(_ctx_2048t)) + 1e-12) * 0.953939
        ctx_2048 = -0.000514642 + 1.00011 * (_ctx_2048t + 0.3 * jax.random.normal(jax.random.fold_in(_rk, 611), (4, 512, 512), jnp.float32))
        _validS = jnp.arange(512)[None, :] < _lenS[:, None]
        _validS2 = jnp.arange(512)[None, :] < _lenS2[:, None]
        _causal = jnp.tril(jnp.ones((512, 512), dtype=bool))
        mask_BxS2_bk0 = jnp.logical_not(jnp.broadcast_to(_validS2[:, :], (4, 512)))
        return (x, ctx_2048, mask_BxS2_bk0)
    x, ctx_2048, mask_BxS2_bk0 = _rec_inputs()

    def _L0_attn_setup():
        import jax, jax.numpy as jnp
        import numpy as np
        B, T, H = (8, 512, 512)
        LN_EPS = 1e-05

        def _timemix(x, ln_scale, ln_bias, mix_k, mix_v, mix_r, time_first, time_decay, Wk, Wv, Wr, Wo):
            mean = jnp.mean(x, axis=-1, keepdims=True)
            var = jnp.mean((x - mean) ** 2, axis=-1, keepdims=True)
            xn = (x - mean) * jax.lax.rsqrt(var + LN_EPS) * ln_scale + ln_bias
            prev = jnp.concatenate([jnp.zeros_like(xn[:, :1]), xn[:, :-1]], axis=1)
            kx = xn * mix_k + prev * (1.0 - mix_k)
            vx = xn * mix_v + prev * (1.0 - mix_v)
            rx = xn * mix_r + prev * (1.0 - mix_r)
            r = jax.nn.sigmoid(jnp.einsum('bth,hd->btd', rx, Wr))
            k = jnp.einsum('bth,hd->btd', kx, Wk)
            v = jnp.einsum('bth,hd->btd', vx, Wv)
            w = -jnp.exp(time_decay)
            kT = jnp.moveaxis(k, 1, 0)
            vT = jnp.moveaxis(v, 1, 0)

            def step(carry, kv):
                a, b, p = carry
                kt, vt = kv
                uk = kt + time_first
                q = jnp.maximum(uk, p)
                e1 = jnp.exp(p - q)
                e2 = jnp.exp(uk - q)
                num = e1 * a + e2 * vt
                den = e1 * b + e2
                den_safe = jnp.where(den == 0.0, 1.0, den)
                wkv = jnp.where(den == 0.0, 0.0, num / den_safe)
                cw = w + p
                q2 = jnp.maximum(cw, kt)
                ce1 = jnp.exp(cw - q2)
                ce2 = jnp.exp(kt - q2)
                return ((ce1 * a + ce2 * vt, ce1 * b + ce2, q2), wkv)
            bz = x.shape[0]
            init = (jnp.zeros((bz, H), jnp.float32), jnp.zeros((bz, H), jnp.float32), jnp.full((bz, H), 1.0 - 1e+30, jnp.float32))
            _, wkvT = jax.lax.scan(step, init, (kT, vT))
            wkv = jnp.moveaxis(wkvT, 0, 1)
            out = x + jnp.einsum('bth,hd->btd', r * wkv, Wo)
            return out
        key = jax.random.key(seed)
        ks = jax.random.split(key, 12)
        x = jax.random.normal(ks[0], (B, T, H), dtype=jnp.float32)
        ln_scale = jnp.ones((H,), jnp.float32) + 0.1 * jax.random.normal(ks[1], (H,), jnp.float32)
        ln_bias = 0.1 * jax.random.normal(ks[2], (H,), jnp.float32)
        mix_k = jax.random.uniform(ks[3], (H,), jnp.float32)
        mix_v = jax.random.uniform(ks[4], (H,), jnp.float32)
        mix_r = jax.random.uniform(ks[5], (H,), jnp.float32)
        time_first = 0.3 * jax.random.normal(ks[6], (H,), jnp.float32)
        time_decay = 0.5 * jax.random.normal(ks[7], (H,), jnp.float32)
        std = 0.02
        Wk = std * jax.random.normal(ks[8], (H, H), jnp.float32)
        Wv = std * jax.random.normal(ks[9], (H, H), jnp.float32)
        Wr = std * jax.random.normal(ks[10], (H, H), jnp.float32)
        Wo = std * jax.random.normal(ks[11], (H, H), jnp.float32)
        return {'x': x, 'ln_scale': ln_scale, 'ln_bias': ln_bias, 'mix_k': mix_k, 'mix_v': mix_v, 'mix_r': mix_r, 'time_first': time_first, 'time_decay': time_decay, 'Wk': Wk, 'Wv': Wv, 'Wr': Wr, 'Wo': Wo}
    _L0_attn_all = _L0_attn_setup()
    _L0_attn_in = {k: v for k, v in _L0_attn_all.items() if k in ('ln_scale', 'ln_bias', 'mix_k', 'mix_v', 'mix_r', 'time_first', 'time_decay', 'Wk', 'Wv', 'Wr', 'Wo')}
    del _L0_attn_all

    def _L0_xattn_setup():
        import jax, jax.numpy as jnp
        import numpy as np
        key = jax.random.key(seed)
        k1, k2, k3 = jax.random.split(key, 3)
        B, S, D, M = (8, 512, 512, 128)
        hidden_states = jax.random.normal(k1, (B, S, D), dtype=jnp.float32)
        memory_tokens = jax.random.normal(k2, (B, M, D), dtype=jnp.float32)
        memory_mask = jax.random.randint(k3, (B, M), 0, 2).astype(jnp.bool_)
        return {'hidden_states': hidden_states, 'memory_tokens': memory_tokens, 'memory_mask': memory_mask}
    _L0_xattn_all = _L0_xattn_setup()
    _L0_xattn_in = {k: v for k, v in _L0_xattn_all.items() if k in ()}
    del _L0_xattn_all

    def _L0_ffn_setup():
        import jax, jax.numpy as jnp
        import numpy as np
        EPS = 1e-05

        def rms_norm(x):
            return x * jax.lax.rsqrt(jnp.mean(x * x, axis=-1, keepdims=True) + EPS)

        def act_quant(x):
            scale = 127.0 / jnp.clip(jnp.max(jnp.abs(x), axis=-1, keepdims=True), 1e-05)
            q = jnp.clip(jnp.round(x * scale), -128.0, 127.0) / scale
            return x + jax.lax.stop_gradient(q - x)

        def weight_quant(w):
            scale = 1.0 / jnp.clip(jnp.mean(jnp.abs(w)), 1e-05)
            q = jnp.clip(jnp.round(w * scale), -1.0, 1.0) / scale
            return w + jax.lax.stop_gradient(q - w)

        def bitlinear158(x, w, b):
            xq = act_quant(rms_norm(x))
            wq = weight_quant(w)
            return jnp.einsum('bsd,od->bso', xq, wq) + b

        def layer_norm(x, g, b):
            mu = jnp.mean(x, axis=-1, keepdims=True)
            var = jnp.mean((x - mu) ** 2, axis=-1, keepdims=True)
            return (x - mu) * jax.lax.rsqrt(var + EPS) * g + b
        key = jax.random.key(seed)
        ks = jax.random.split(key, 3)
        d, inner = (512, 2048)
        x = jax.random.normal(ks[0], (4, 512, d), dtype=jnp.float32)
        w1 = jax.random.normal(ks[1], (inner, d), dtype=jnp.float32) * 0.02
        b1 = jnp.zeros((inner,), jnp.float32)
        ln_g = jnp.ones((inner,), jnp.float32)
        ln_b = jnp.zeros((inner,), jnp.float32)
        w2 = jax.random.normal(ks[2], (d, inner), dtype=jnp.float32) * 0.02
        b2 = jnp.zeros((d,), jnp.float32)
        return {'x': x, 'w1': w1, 'b1': b1, 'ln_g': ln_g, 'ln_b': ln_b, 'w2': w2, 'b2': b2}
    _L0_ffn_all = _L0_ffn_setup()
    _L0_ffn_in = {k: v for k, v in _L0_ffn_all.items() if k in ('w1', 'b1', 'ln_g', 'ln_b', 'w2', 'b2')}
    del _L0_ffn_all

    def _L1_attn_setup():
        import jax, jax.numpy as jnp
        import numpy as np
        from functools import partial
        H = 512
        DI = 1024
        N = 16
        K = 4
        R = 128
        B = 2
        L = 256

        def _silu(v):
            return v * jax.nn.sigmoid(v)

        def _mamba_fwd(x, Win, Wconv, bconv, Wx, Wdt, bdt, Wout, A_log, D):
            sg = jax.lax.stop_gradient
            proj = jnp.einsum('blh,eh->bel', x, Win)
            hs, gate = (proj[:, :DI], proj[:, DI:])
            hs = jax.lax.conv_general_dilated(hs, Wconv, window_strides=(1,), padding=[(K - 1, 0)], dimension_numbers=('NCH', 'OIH', 'NCH'), feature_group_count=DI)
            hs = _silu(hs + bconv[None, :, None])
            ssm_p = jnp.einsum('bdl,pd->blp', hs, Wx)
            dt_in, Bm, Cm = (ssm_p[..., :R], ssm_p[..., R:R + N], ssm_p[..., R + N:])
            dt = jax.nn.softplus(jnp.einsum('blr,dr->bld', dt_in, Wdt) + bdt)
            dt = jnp.transpose(dt, (0, 2, 1))
            A = -jnp.exp(A_log)
            dA = jnp.exp(A[None, :, None, :] * dt[:, :, :, None])
            dBu = sg(dt[:, :, :, None] * Bm[:, None, :, :]) * hs[:, :, :, None]
            dA = sg(dA)
            Cm = sg(Cm)
            xs = (jnp.transpose(dA, (2, 0, 1, 3)), jnp.transpose(dBu, (2, 0, 1, 3)), jnp.transpose(Cm, (1, 0, 2)))
            h0 = jnp.zeros((x.shape[0], DI, N), jnp.float32)

            def step(h, inp):
                dA_t, dBu_t, C_t = inp
                h = dA_t * h + dBu_t
                y = jnp.einsum('bdn,bn->bd', h, C_t)
                return (h, y)
            _, ys = jax.lax.scan(step, h0, xs)
            y = jnp.transpose(ys, (1, 2, 0))
            y = y + hs * D[None, :, None]
            y = y * _silu(gate)
            y = y / 2.0 + sg(y / 2.0)
            return jnp.einsum('bdl,hd->blh', y, Wout)
        key = jax.random.key(seed)
        ks = jax.random.split(key, 10)
        s = 0.02
        return {'x': jax.random.normal(ks[0], (B, L, H), jnp.float32), 'Win': jax.random.normal(ks[1], (2 * DI, H), jnp.float32) * s, 'Wconv': jax.random.normal(ks[2], (DI, 1, K), jnp.float32) * 0.2, 'bconv': jax.random.normal(ks[3], (DI,), jnp.float32) * 0.1, 'Wx': jax.random.normal(ks[4], (R + 2 * N, DI), jnp.float32) * s, 'Wdt': jax.random.normal(ks[5], (DI, R), jnp.float32) * s, 'bdt': jax.random.normal(ks[6], (DI,), jnp.float32) * 0.1, 'Wout': jax.random.normal(ks[7], (H, DI), jnp.float32) * s, 'A_log': jnp.log(jnp.broadcast_to(jnp.arange(1, N + 1, dtype=jnp.float32), (DI, N))), 'D': jnp.ones((DI,), jnp.float32)}
    _L1_attn_all = _L1_attn_setup()
    _L1_attn_in = {k: v for k, v in _L1_attn_all.items() if k in ('Win', 'Wconv', 'bconv', 'Wx', 'Wdt', 'bdt', 'Wout', 'A_log', 'D')}
    del _L1_attn_all

    def _L1_xattn_setup():
        import jax, jax.numpy as jnp
        import numpy as np
        HIDDEN = 512
        NUM_HEADS = 16
        NUM_KV_HEADS = 4
        HEAD_DIM = 128
        ROPE_THETA = 10000.0
        EPS = 1e-06

        def rms_norm(x, w, eps=EPS):
            var = jnp.mean(jnp.square(x), axis=-1, keepdims=True)
            return x * jax.lax.rsqrt(var + eps) * w

        def rope_cache(L, head_dim, theta, dtype):
            inv_freq = 1.0 / theta ** (jnp.arange(0, head_dim, 2, dtype=jnp.float32) / head_dim)
            t = jnp.arange(L, dtype=jnp.float32)
            freqs = jnp.outer(t, inv_freq)
            emb = jnp.concatenate([freqs, freqs], -1)
            cos = jnp.cos(emb).astype(dtype)[None, :, None, :]
            sin = jnp.sin(emb).astype(dtype)[None, :, None, :]
            return (cos, sin)

        def rotate_half(x):
            x1, x2 = jnp.split(x, 2, axis=-1)
            return jnp.concatenate([-x2, x1], axis=-1)
        key = jax.random.key(seed)
        ks = jax.random.split(key, 10)
        B, L, T = (2, 512, 128)
        q_out = NUM_HEADS * HEAD_DIM
        kv_out = NUM_KV_HEADS * HEAD_DIM
        s = lambda fan_in: 1.0 / np.sqrt(fan_in)
        return {'x': jax.random.normal(ks[0], (B, L, HIDDEN), jnp.float32), 'h_ctx_kv': jax.random.normal(ks[1], (B, T, HIDDEN), jnp.float32), 'wq': jax.random.normal(ks[2], (HIDDEN, q_out), jnp.float32) * s(HIDDEN), 'wk': jax.random.normal(ks[3], (HIDDEN, kv_out), jnp.float32) * s(HIDDEN), 'wv': jax.random.normal(ks[4], (HIDDEN, kv_out), jnp.float32) * s(HIDDEN), 'wo': jax.random.normal(ks[5], (q_out, HIDDEN), jnp.float32) * s(q_out), 'wk_ctx': jax.random.normal(ks[6], (HIDDEN, kv_out), jnp.float32) * s(HIDDEN), 'wv_ctx': jax.random.normal(ks[7], (HIDDEN, kv_out), jnp.float32) * s(HIDDEN), 'q_norm_w': jnp.ones((HEAD_DIM,), jnp.float32), 'k_norm_w': jnp.ones((HEAD_DIM,), jnp.float32)}
    _L1_xattn_all = _L1_xattn_setup()
    _L1_xattn_in = {k: v for k, v in _L1_xattn_all.items() if k in ('wq', 'wk', 'wv', 'wo', 'wk_ctx', 'wv_ctx', 'q_norm_w', 'k_norm_w')}
    del _L1_xattn_all

    def _L1_ffn_setup():
        import jax, jax.numpy as jnp
        import numpy as np
        from jax import lax
        E = 64
        TOP_K = 8
        SEL_K = 4
        THRESH = 0.5
        H = 512
        F_INT = 192
        B, S = (1, 512)
        key = jax.random.key(seed)
        k0, k1, k2, k3, k4 = jax.random.split(key, 5)
        return {'hidden_states': jax.random.normal(k0, (B, S, H), jnp.float32), 'gate_weight': jax.random.normal(k1, (E, H), jnp.float32) * 0.02, 'gate_up_proj': jax.random.normal(k2, (E, 2 * F_INT, H), jnp.float32) * 0.02, 'down_proj': jax.random.normal(k3, (E, H, F_INT), jnp.float32) * 0.02, 'similarity': jax.random.uniform(k4, (E, E), jnp.float32)}
    _L1_ffn_all = _L1_ffn_setup()
    _L1_ffn_in = {k: v for k, v in _L1_ffn_all.items() if k in ('gate_weight', 'gate_up_proj', 'down_proj', 'similarity')}
    del _L1_ffn_all
    return {'x': x, 'ctx_2048': ctx_2048, 'mask_BxS2_bk0': mask_BxS2_bk0, 'L0_attn_ln_scale': _L0_attn_in['ln_scale'], 'L0_attn_ln_bias': _L0_attn_in['ln_bias'], 'L0_attn_mix_k': _L0_attn_in['mix_k'], 'L0_attn_mix_v': _L0_attn_in['mix_v'], 'L0_attn_mix_r': _L0_attn_in['mix_r'], 'L0_attn_time_first': _L0_attn_in['time_first'], 'L0_attn_time_decay': _L0_attn_in['time_decay'], 'L0_attn_Wk': _L0_attn_in['Wk'], 'L0_attn_Wv': _L0_attn_in['Wv'], 'L0_attn_Wr': _L0_attn_in['Wr'], 'L0_attn_Wo': _L0_attn_in['Wo'], 'L0_ffn_w1': _L0_ffn_in['w1'], 'L0_ffn_b1': _L0_ffn_in['b1'], 'L0_ffn_ln_g': _L0_ffn_in['ln_g'], 'L0_ffn_ln_b': _L0_ffn_in['ln_b'], 'L0_ffn_w2': _L0_ffn_in['w2'], 'L0_ffn_b2': _L0_ffn_in['b2'], 'L1_attn_Win': _L1_attn_in['Win'], 'L1_attn_Wconv': _L1_attn_in['Wconv'], 'L1_attn_bconv': _L1_attn_in['bconv'], 'L1_attn_Wx': _L1_attn_in['Wx'], 'L1_attn_Wdt': _L1_attn_in['Wdt'], 'L1_attn_bdt': _L1_attn_in['bdt'], 'L1_attn_Wout': _L1_attn_in['Wout'], 'L1_attn_A_log': _L1_attn_in['A_log'], 'L1_attn_D': _L1_attn_in['D'], 'L1_xattn_wq': _L1_xattn_in['wq'], 'L1_xattn_wk': _L1_xattn_in['wk'], 'L1_xattn_wv': _L1_xattn_in['wv'], 'L1_xattn_wo': _L1_xattn_in['wo'], 'L1_xattn_wk_ctx': _L1_xattn_in['wk_ctx'], 'L1_xattn_wv_ctx': _L1_xattn_in['wv_ctx'], 'L1_xattn_q_norm_w': _L1_xattn_in['q_norm_w'], 'L1_xattn_k_norm_w': _L1_xattn_in['k_norm_w'], 'L1_ffn_gate_weight': _L1_ffn_in['gate_weight'], 'L1_ffn_gate_up_proj': _L1_ffn_in['gate_up_proj'], 'L1_ffn_down_proj': _L1_ffn_in['down_proj'], 'L1_ffn_similarity': _L1_ffn_in['similarity']}

def reference(x, ctx_2048, mask_BxS2_bk0, L0_attn_ln_scale, L0_attn_ln_bias, L0_attn_mix_k, L0_attn_mix_v, L0_attn_mix_r, L0_attn_time_first, L0_attn_time_decay, L0_attn_Wk, L0_attn_Wv, L0_attn_Wr, L0_attn_Wo, L0_ffn_w1, L0_ffn_b1, L0_ffn_ln_g, L0_ffn_ln_b, L0_ffn_w2, L0_ffn_b2, L1_attn_Win, L1_attn_Wconv, L1_attn_bconv, L1_attn_Wx, L1_attn_Wdt, L1_attn_bdt, L1_attn_Wout, L1_attn_A_log, L1_attn_D, L1_xattn_wq, L1_xattn_wk, L1_xattn_wv, L1_xattn_wo, L1_xattn_wk_ctx, L1_xattn_wv_ctx, L1_xattn_q_norm_w, L1_xattn_k_norm_w, L1_ffn_gate_weight, L1_ffn_gate_up_proj, L1_ffn_down_proj, L1_ffn_similarity):
    import jax
    import jax.numpy as jnp

    def _L0_attn_ref(x, ln_scale, ln_bias, mix_k, mix_v, mix_r, time_first, time_decay, Wk, Wv, Wr, Wo):
        import jax, jax.numpy as jnp
        import numpy as np
        B, T, H = (8, 512, 512)
        LN_EPS = 1e-05

        def _timemix(x, ln_scale, ln_bias, mix_k, mix_v, mix_r, time_first, time_decay, Wk, Wv, Wr, Wo):
            mean = jnp.mean(x, axis=-1, keepdims=True)
            var = jnp.mean((x - mean) ** 2, axis=-1, keepdims=True)
            xn = (x - mean) * jax.lax.rsqrt(var + LN_EPS) * ln_scale + ln_bias
            prev = jnp.concatenate([jnp.zeros_like(xn[:, :1]), xn[:, :-1]], axis=1)
            kx = xn * mix_k + prev * (1.0 - mix_k)
            vx = xn * mix_v + prev * (1.0 - mix_v)
            rx = xn * mix_r + prev * (1.0 - mix_r)
            r = jax.nn.sigmoid(jnp.einsum('bth,hd->btd', rx, Wr))
            k = jnp.einsum('bth,hd->btd', kx, Wk)
            v = jnp.einsum('bth,hd->btd', vx, Wv)
            w = -jnp.exp(time_decay)
            kT = jnp.moveaxis(k, 1, 0)
            vT = jnp.moveaxis(v, 1, 0)

            def step(carry, kv):
                a, b, p = carry
                kt, vt = kv
                uk = kt + time_first
                q = jnp.maximum(uk, p)
                e1 = jnp.exp(p - q)
                e2 = jnp.exp(uk - q)
                num = e1 * a + e2 * vt
                den = e1 * b + e2
                den_safe = jnp.where(den == 0.0, 1.0, den)
                wkv = jnp.where(den == 0.0, 0.0, num / den_safe)
                cw = w + p
                q2 = jnp.maximum(cw, kt)
                ce1 = jnp.exp(cw - q2)
                ce2 = jnp.exp(kt - q2)
                return ((ce1 * a + ce2 * vt, ce1 * b + ce2, q2), wkv)
            bz = x.shape[0]
            init = (jnp.zeros((bz, H), jnp.float32), jnp.zeros((bz, H), jnp.float32), jnp.full((bz, H), 1.0 - 1e+30, jnp.float32))
            _, wkvT = jax.lax.scan(step, init, (kT, vT))
            wkv = jnp.moveaxis(wkvT, 0, 1)
            out = x + jnp.einsum('bth,hd->btd', r * wkv, Wo)
            return out
        return _timemix(x, ln_scale, ln_bias, mix_k, mix_v, mix_r, time_first, time_decay, Wk, Wv, Wr, Wo)

    def _L0_xattn_ref(hidden_states, memory_tokens, memory_mask):
        import jax, jax.numpy as jnp
        import numpy as np
        B, S, D = hidden_states.shape
        scale = 1.0 / jnp.sqrt(jnp.asarray(D, hidden_states.dtype))
        scores = jnp.einsum('bsd,bmd->bsm', hidden_states, memory_tokens) * scale
        neg_inf = jnp.asarray(-1e+30, scores.dtype)
        scores = jnp.where(memory_mask[:, None, :], scores, neg_inf)
        attn = jax.nn.softmax(scores, axis=-1)
        readout = jnp.einsum('bsm,bmd->bsd', attn, memory_tokens)
        valid_b = jnp.any(memory_mask, axis=-1)
        out = jnp.where(valid_b[:, None, None], readout, jnp.zeros_like(readout))
        return out

    def _L0_ffn_ref(x, w1, b1, ln_g, ln_b, w2, b2):
        import jax, jax.numpy as jnp
        import numpy as np
        EPS = 1e-05

        def rms_norm(x):
            return x * jax.lax.rsqrt(jnp.mean(x * x, axis=-1, keepdims=True) + EPS)

        def act_quant(x):
            scale = 127.0 / jnp.clip(jnp.max(jnp.abs(x), axis=-1, keepdims=True), 1e-05)
            q = jnp.clip(jnp.round(x * scale), -128.0, 127.0) / scale
            return x + jax.lax.stop_gradient(q - x)

        def weight_quant(w):
            scale = 1.0 / jnp.clip(jnp.mean(jnp.abs(w)), 1e-05)
            q = jnp.clip(jnp.round(w * scale), -1.0, 1.0) / scale
            return w + jax.lax.stop_gradient(q - w)

        def bitlinear158(x, w, b):
            xq = act_quant(rms_norm(x))
            wq = weight_quant(w)
            return jnp.einsum('bsd,od->bso', xq, wq) + b

        def layer_norm(x, g, b):
            mu = jnp.mean(x, axis=-1, keepdims=True)
            var = jnp.mean((x - mu) ** 2, axis=-1, keepdims=True)
            return (x - mu) * jax.lax.rsqrt(var + EPS) * g + b
        h = jax.nn.silu(bitlinear158(x, w1, b1))
        h = jax.nn.gelu(h, approximate=False)
        h = layer_norm(h, ln_g, ln_b)
        return bitlinear158(h, w2, b2)

    def _L1_attn_ref(x, Win, Wconv, bconv, Wx, Wdt, bdt, Wout, A_log, D):
        import jax, jax.numpy as jnp
        import numpy as np
        from functools import partial
        H = 512
        DI = 1024
        N = 16
        K = 4
        R = 128
        B = 2
        L = 256

        def _silu(v):
            return v * jax.nn.sigmoid(v)

        def _mamba_fwd(x, Win, Wconv, bconv, Wx, Wdt, bdt, Wout, A_log, D):
            sg = jax.lax.stop_gradient
            proj = jnp.einsum('blh,eh->bel', x, Win)
            hs, gate = (proj[:, :DI], proj[:, DI:])
            hs = jax.lax.conv_general_dilated(hs, Wconv, window_strides=(1,), padding=[(K - 1, 0)], dimension_numbers=('NCH', 'OIH', 'NCH'), feature_group_count=DI)
            hs = _silu(hs + bconv[None, :, None])
            ssm_p = jnp.einsum('bdl,pd->blp', hs, Wx)
            dt_in, Bm, Cm = (ssm_p[..., :R], ssm_p[..., R:R + N], ssm_p[..., R + N:])
            dt = jax.nn.softplus(jnp.einsum('blr,dr->bld', dt_in, Wdt) + bdt)
            dt = jnp.transpose(dt, (0, 2, 1))
            A = -jnp.exp(A_log)
            dA = jnp.exp(A[None, :, None, :] * dt[:, :, :, None])
            dBu = sg(dt[:, :, :, None] * Bm[:, None, :, :]) * hs[:, :, :, None]
            dA = sg(dA)
            Cm = sg(Cm)
            xs = (jnp.transpose(dA, (2, 0, 1, 3)), jnp.transpose(dBu, (2, 0, 1, 3)), jnp.transpose(Cm, (1, 0, 2)))
            h0 = jnp.zeros((x.shape[0], DI, N), jnp.float32)

            def step(h, inp):
                dA_t, dBu_t, C_t = inp
                h = dA_t * h + dBu_t
                y = jnp.einsum('bdn,bn->bd', h, C_t)
                return (h, y)
            _, ys = jax.lax.scan(step, h0, xs)
            y = jnp.transpose(ys, (1, 2, 0))
            y = y + hs * D[None, :, None]
            y = y * _silu(gate)
            y = y / 2.0 + sg(y / 2.0)
            return jnp.einsum('bdl,hd->blh', y, Wout)
        return _mamba_fwd(x, Win, Wconv, bconv, Wx, Wdt, bdt, Wout, A_log, D)

    def _L1_xattn_ref(x, h_ctx_kv, wq, wk, wv, wo, wk_ctx, wv_ctx, q_norm_w, k_norm_w):
        import jax, jax.numpy as jnp
        import numpy as np
        HIDDEN = 512
        NUM_HEADS = 16
        NUM_KV_HEADS = 4
        HEAD_DIM = 128
        ROPE_THETA = 10000.0
        EPS = 1e-06

        def rms_norm(x, w, eps=EPS):
            var = jnp.mean(jnp.square(x), axis=-1, keepdims=True)
            return x * jax.lax.rsqrt(var + eps) * w

        def rope_cache(L, head_dim, theta, dtype):
            inv_freq = 1.0 / theta ** (jnp.arange(0, head_dim, 2, dtype=jnp.float32) / head_dim)
            t = jnp.arange(L, dtype=jnp.float32)
            freqs = jnp.outer(t, inv_freq)
            emb = jnp.concatenate([freqs, freqs], -1)
            cos = jnp.cos(emb).astype(dtype)[None, :, None, :]
            sin = jnp.sin(emb).astype(dtype)[None, :, None, :]
            return (cos, sin)

        def rotate_half(x):
            x1, x2 = jnp.split(x, 2, axis=-1)
            return jnp.concatenate([-x2, x1], axis=-1)
        B, L, _ = x.shape
        T = h_ctx_kv.shape[1]
        rep = NUM_HEADS // NUM_KV_HEADS
        q = (x @ wq).reshape(B, L, NUM_HEADS, HEAD_DIM)
        k = (x @ wk).reshape(B, L, NUM_KV_HEADS, HEAD_DIM)
        v = (x @ wv).reshape(B, L, NUM_KV_HEADS, HEAD_DIM)
        q = rms_norm(q, q_norm_w)
        k = rms_norm(k, k_norm_w)
        k_ctx = (h_ctx_kv @ wk_ctx).reshape(B, T, NUM_KV_HEADS, HEAD_DIM)
        v_ctx = (h_ctx_kv @ wv_ctx).reshape(B, T, NUM_KV_HEADS, HEAD_DIM)
        k_ctx = rms_norm(k_ctx, k_norm_w)
        cos, sin = rope_cache(L, HEAD_DIM, ROPE_THETA, x.dtype)
        q = q * cos + rotate_half(q) * sin
        k = k * cos + rotate_half(k) * sin
        k_full = jnp.concatenate([k_ctx, k], axis=1)
        v_full = jnp.concatenate([v_ctx, v], axis=1)
        k_full = jnp.repeat(k_full, rep, axis=2)
        v_full = jnpp_repeat = jnp.repeat(v_full, rep, axis=2)
        i = jnp.arange(L)[:, None]
        j = jnp.arange(L)[None, :]
        causal = jnp.where(j > i, -jnp.inf, 0.0).astype(x.dtype)
        mask = jnp.concatenate([jnp.zeros((L, T), x.dtype), causal], axis=1)
        scale = 1.0 / np.sqrt(HEAD_DIM)
        scores = jnp.einsum('blhd,bmhd->bhlm', q, k_full) * scale + mask
        probs = jax.nn.softmax(scores, axis=-1)
        out = jnp.einsum('bhlm,bmhd->blhd', probs, v_full)
        out = out.reshape(B, L, NUM_HEADS * HEAD_DIM)
        return out @ wo

    def _L1_ffn_ref(hidden_states, gate_weight, gate_up_proj, down_proj, similarity):
        import jax, jax.numpy as jnp
        import numpy as np
        from jax import lax
        E = 64
        TOP_K = 8
        SEL_K = 4
        THRESH = 0.5
        H = 512
        F_INT = 192
        B, S = (1, 512)
        b, s, h = hidden_states.shape
        x = hidden_states.reshape(-1, h)
        logits = x @ gate_weight.T
        probs = jax.nn.softmax(logits.astype(jnp.float32), axis=-1).astype(logits.dtype)
        top_val, top_idx = lax.top_k(probs, TOP_K)
        top_val = top_val / jnp.clip(top_val.sum(-1, keepdims=True), 1e-12)
        sim = similarity.astype(jnp.float32)
        diag = jnp.arange(E)
        sim = sim.at[diag, diag].set(1.0)
        primary_mask = jnp.zeros((E,), bool).at[top_idx[:, :SEL_K].reshape(-1)].set(True)
        secondary_mask = jnp.zeros((E,), bool).at[top_idx[:, SEL_K:].reshape(-1)].set(True)
        cand = jnp.where(primary_mask[None, :], sim, -jnp.inf)
        best_primary = jnp.argmax(cand, axis=-1)
        best_sim = jnp.max(cand, axis=-1)
        replace = secondary_mask & ~primary_mask & (best_sim >= THRESH)
        mapping = jnp.where(replace, best_primary, jnp.arange(E))
        rerouted = mapping[top_idx]
        rerouted = rerouted.at[:, :SEL_K].set(top_idx[:, :SEL_K])
        flat_e = rerouted.reshape(-1)
        order = jnp.argsort(flat_e)
        tok = order // TOP_K
        xs = x[tok]
        group_sizes = jnp.zeros((E,), jnp.int32).at[flat_e].add(1)
        gu = lax.ragged_dot(xs, jnp.swapaxes(gate_up_proj, 1, 2), group_sizes)
        gate, up = jnp.split(gu, 2, axis=-1)
        hact = jax.nn.silu(gate) * up
        y = lax.ragged_dot(hact, jnp.swapaxes(down_proj, 1, 2), group_sizes)
        w = top_val.reshape(-1)[order]
        out = jnp.zeros_like(x).at[tok].add(y * w[:, None])
        return out.reshape(b, s, h)
    x = x + _L0_attn_ref(_layernorm(x, axis=-1), L0_attn_ln_scale, L0_attn_ln_bias, L0_attn_mix_k, L0_attn_mix_v, L0_attn_mix_r, L0_attn_time_first, L0_attn_time_decay, L0_attn_Wk, L0_attn_Wv, L0_attn_Wr, L0_attn_Wo)
    x = x + _L0_xattn_ref(_layernorm(x, axis=-1), ctx_2048, mask_BxS2_bk0)
    x = x + _L0_ffn_ref(_layernorm(x, axis=-1), L0_ffn_w1, L0_ffn_b1, L0_ffn_ln_g, L0_ffn_ln_b, L0_ffn_w2, L0_ffn_b2)
    x = x + _L1_attn_ref(_layernorm(x, axis=-1), L1_attn_Win, L1_attn_Wconv, L1_attn_bconv, L1_attn_Wx, L1_attn_Wdt, L1_attn_bdt, L1_attn_Wout, L1_attn_A_log, L1_attn_D)
    x = x + _L1_xattn_ref(_layernorm(x, axis=-1), ctx_2048, L1_xattn_wq, L1_xattn_wk, L1_xattn_wv, L1_xattn_wo, L1_xattn_wk_ctx, L1_xattn_wv_ctx, L1_xattn_q_norm_w, L1_xattn_k_norm_w)
    x = x + _L1_ffn_ref(_layernorm(x, axis=-1), L1_ffn_gate_weight, L1_ffn_gate_up_proj, L1_ffn_down_proj, L1_ffn_similarity)
    return x

_drawn_inputs = setup_inputs


def setup_inputs(seed=0):
    import zlib

    import numpy as np

    out = dict(_drawn_inputs(seed))
    spreads = {'L0_ffn_b1': (0.0, 0.1),
     'L0_ffn_ln_g': (1.0, 0.2),
     'L0_ffn_ln_b': (0.0, 0.1),
     'L0_ffn_b2': (0.0, 0.1),
     'L1_attn_D': (1.0, 0.2),
     'L1_xattn_q_norm_w': (1.0, 0.2),
     'L1_xattn_k_norm_w': (1.0, 0.2)}
    factors = {}
    for name, (base, spread) in spreads.items():
        noise = np.random.default_rng([zlib.crc32(name.encode()), seed]).standard_normal(out[name].shape)
        drawn = base * np.exp(spread * noise) if base else spread * noise
        out[name] = jnp.asarray(drawn.astype(out[name].dtype))
    for name, factor in factors.items():
        out[name] = (out[name] * factor).astype(out[name].dtype)
    return out
```

```python
from contextlib import ExitStack

import concourse.bass as bass
import numpy as np
from concourse import mybir

ALU = mybir.AluOpType
ACT = mybir.ActivationFunctionType
AX = mybir.AxisListType
F32 = mybir.dt.float32
BF16 = mybir.dt.bfloat16
U8 = mybir.dt.uint8
U32 = mybir.dt.uint32

P = 128
B, T, H = 4, 512, 512
HC = H // P
TT = T // P
NEG = -1e30
ROUND = 1.5 * 2.0**23


class Chain:

    def __init__(self, eng, sem, per=0):
        self.eng, self.sem, self.per, self.base, self.n, self.start = eng, sem, per, 0, 0, None

    def turn(self, i):
        if self.start is None:
            self.start = self.n
        self.base, self.n = self.start + i * self.per, 0

    def inc(self, instruction):
        instruction.then_inc(self.sem, 1)
        self.n += 1

    def wait(self):
        self.eng.wait_ge(self.sem, self.base + self.n)

    def end(self):
        assert self.n == self.per, f"{self.sem}: {self.n} marks in a turn, not {self.per}"


class Stage:

    def __init__(self, nc, ctx, name, sems=None):
        self.nc, self.ctx, self.name, self.sems = nc, ctx, name, sems
        if sems is None:
            self.sems = []
            ctx.callback(self.clear)

    def clear(self):
        if self.sems:
            self.nc.clear_and_free_semaphores(self.sems)
            self.nc.all_engine_barrier()

    def sb(self, name, shape, dt=F32):
        return self.ctx.enter_context(self.nc.sbuf_tensor(f"{self.name}_{name}", shape, dt))

    def sem(self, name):
        self.sems.append(self.nc.alloc_semaphore(f"{self.name}_{name}"))
        return self.sems[-1]


class Columns:

    def __init__(self, st, ps, ident, eps_col, xT, pad=0):
        st = Stage(st.nc, st.ctx, st.name + "_ln", st.sems)
        self.pause = st.sb("pause", [P, 1])
        self.ps, self.ident, self.eps_col, self.xT, self.pad = ps, ident, eps_col, xT, pad
        self.xn = st.sb("xn", [P, TT, H])
        self.stats = st.sb("stats", [P, TT, 6])
        self.mv = st.sb("mv", [P, TT, 2])
        self.sd = st.sb("sd", [P, TT])
        self.rstd = st.sb("rstd", [P, TT])
        self.var_ready = st.sem("var_ready")
        self.sd_ready = st.sem("sd_ready")
        self.xn_ready = st.sem("xn_ready")
        self.turned = st.sem("turned")
        self.xT_ready = st.sem("xT_ready")

    def statistics(self, dve, chain, rows):
        for i in range(TT):
            chain.inc(dve.bn_stats(self.stats[:, i, :], rows[:, i, :]))
        chain.wait()
        dve.memset(self.pause[:, :], 0.0)
        for i in range(TT):
            last = dve.bn_aggr(self.mv[:, i, :], self.stats[:, i, :])
        return last

    def normalise(self, dve, chain, rows, out):
        chain.inc(dve.reciprocal(self.rstd[:, :], self.sd[:, :]))
        chain.wait()
        for i in range(TT):
            last = dve.tensor_scalar(out[:, i, :], rows[:, i, :], self.mv[:, i, 0:1],
                                     self.rstd[:, i:i + 1], ALU.subtract, ALU.mult)
        return last

    def vector(self, dve, chain, b, rows):
        self.statistics(dve, chain, rows).then_inc(self.var_ready, 1)
        dve.wait_ge(self.sd_ready, b + 1)
        dve.wait_ge(self.turned, HC * b)
        self.normalise(dve, chain, rows, self.xn).then_inc(self.xn_ready, 1)

    def scalar_sd(self, act, n):
        act.wait_ge(self.var_ready, n + 1)
        act.activation(self.sd[:, :], self.mv[:, :, 1], ACT.Sqrt, bias=self.eps_col).then_inc(self.sd_ready, 1)

    def scalar_move(self, act, b, scale=None, bias=None):
        for c in range(HC):
            act.wait_ge(self.turned, HC * b + c + 1)
            args = {} if scale is None else {"scale": scale[:, c:c + 1], "bias": bias[:, c:c + 1]}
            act.activation(self.xT[:, c, self.pad:self.pad + T], self.ps[:, c % 2, :], ACT.Identity,
                           **args).then_inc(self.xT_ready, 1)

    def tensor(self, pe, b):
        pe.wait_ge(self.xn_ready, b + 1)
        for c in range(HC):
            pe.wait_ge(self.xT_ready, HC * b + max(c - 1, 0))
            for i in range(TT):
                last = pe.transpose(self.ps[:, c % 2, i * P:(i + 1) * P],
                                    self.xn[:, i, c * P:(c + 1) * P], self.ident)
            last.then_inc(self.turned, 1)


def rows_of(x, b):
    return x.rearrange("(b i p) h -> b p i h", b=B, p=P)[b]


def time_mix(nc, ps, ident, eps, x_in, x_out, cols, weights, load_extra=None):
    n_cols = cols.shape[1]
    with ExitStack() as ctx:
        st = Stage(nc, ctx, "tm")
        x = st.sb("x", [P, TT, H])
        xl = st.sb("xl", [P, TT, H])
        xT = st.sb("xT", [P, HC, 1 + T])
        step = st.sb("step", [P, HC, T])
        mixed = [st.sb(f"mixed_{n}", [P, HC, T]) for n in "rkv"]
        w = {n: st.sb(f"w{n}", [P, HC, H]) for n in "rkvo"}
        col = st.sb("col", [P, n_cols])
        decay = st.sb("decay", [P, HC])
        r = st.sb("r", [P, HC, T])
        kk = st.sb("kk", [P, 2, T])
        vv = st.sb("vv", [P, 2, T])
        peak = st.sb("peak", [P, 2, 1 + T])
        q = st.sb("q", [P, T])
        ex = st.sb("ex", [P, 2, 4, T])
        cv = st.sb("cv", [P, T])
        sa = st.sb("sa", [P, 1 + T])
        sb_ = st.sb("sbb", [P, 1 + T])
        t1 = st.sb("t1", [P, T])
        t2 = st.sb("t2", [P, T])
        rw = st.sb("rw", [P, HC, T])
        ln = Columns(st, ps, ident, eps, xT, pad=1)
        scale, bias, mix_k, mix_v, mix_r, first, dec = (col[:, HC * j:HC * (j + 1)] for j in range(7))

        weights_in, x_in_s, x_out_s = st.sem("weights_in"), st.sem("x_in"), st.sem("x_out")
        xl_added = st.sem("xl_added")
        decay_e = st.sem("decay_e")
        mixed_ready = st.sem("mixed_ready")
        proj = st.sem("proj")
        moved = st.sem("moved")
        diffs = st.sem("diffs")
        exps = st.sem("exps")
        rw_ready = st.sem("rw_ready")
        o_ready = st.sem("o_ready")
        added = st.sem("added")
        xl_ready = st.sem("xl_ready")
        v_own = st.sem("v_own")
        block = ctx.enter_context(nc.Block())
        order = [("r", d) for d in range(HC)] + [(n, d) for d in range(HC) for n in "kv"]
        NP = len(order)

        @block.sync
        def _(sp):
            sp.dma_start(col[:, :], cols).then_inc(weights_in, 16)
            for n in "rkvo":
                sp.dma_start(w[n][:, :, :], weights[n].rearrange("(c p) d -> p c d", p=P)).then_inc(weights_in, 16)
            with sp.Fori(0, B) as b:
                sp.wait_ge(x_out_s, 16 * b)
                sp.dma_start(x[:, :, :], rows_of(x_in, b)).then_inc(x_in_s, 16)
                sp.wait_ge(added, TT * b + TT)
                sp.dma_start(rows_of(x_out, b), x[:, :, :]).then_inc(x_out_s, 16)
            sp.wait_ge(x_out_s, 16 * B)

        @block.gpsimd
        def _(pool):
            with pool.Fori(0, B) as b:
                pool.wait_ge(xl_ready, b + 1)
                for i in range(TT):
                    pool.tensor_tensor(x[:, i, :], x[:, i, :], xl[:, i, :], ALU.add).then_inc(xl_added, 1)

        @block.scalar
        def _(act):
            act.wait_ge(weights_in, 16 * 5)
            act.activation(decay[:, :], dec, ACT.Exp).then_inc(decay_e, 1)
            with act.Fori(0, B) as b:
                ln.scalar_sd(act, 2 * b)
                ln.scalar_sd(act, 2 * b + 1)
                ln.scalar_move(act, b, scale, bias)
                for j, (n, d) in enumerate(order):
                    act.wait_ge(proj, NP * b + j + 1)
                    bank = ps[:, 2 + j % 6, :]
                    if n == "r":
                        if d == 0:
                            act.wait_ge(rw_ready, HC * b)
                        act.activation(r[:, d, :], bank, ACT.Sigmoid).then_inc(moved, 1)
                        continue
                    if n == "k" and d >= 2:
                        act.wait_ge(rw_ready, HC * b + d - 1)
                    act.activation((kk if n == "k" else vv)[:, d % 2, :], bank, ACT.Identity).then_inc(moved, 1)
                    if n == "v":
                        act.wait_ge(diffs, HC * b + d + 1)
                        act.activation(ex[:, d % 2, :, :], ex[:, d % 2, :, :], ACT.Exp).then_inc(exps, 1)

        @block.tensor
        def _(pe):
            pe.wait_ge(weights_in, 16 * 5)
            with pe.Fori(0, B) as b:
                pe.wait_ge(added, TT * b)
                ln.tensor(pe, b)
                for j, (n, d) in enumerate(order):
                    pe.wait_ge(moved, NP * b + max(j - 5, 0))
                    pe.wait_ge(mixed_ready, 3 * b + 1 + "rkv".index(n))
                    for c in range(HC):
                        last = pe.matmul(ps[:, 2 + j % 6, :], w[n][:, c, d * P:(d + 1) * P],
                                         mixed["rkv".index(n)][:, c, :], start=(c == 0), stop=(c == HC - 1))
                    last.then_inc(proj, 1)
                pe.wait_ge(rw_ready, HC * b + HC)
                for i in range(TT):
                    pe.wait_ge(added, TT * b + max(i - 1, 0))
                    for c in range(HC):
                        last = pe.matmul(ps[:, i % 2, :], rw[:, c, i * P:(i + 1) * P], w["o"][:, c, :],
                                         start=(c == 0), stop=(c == HC - 1))
                    last.then_inc(o_ready, 1)

        @block.vector
        def _(dve):
            own = Chain(dve, v_own, 67)
            dve.memset(xT[:, :, 0:1], 0.0)
            dve.memset(peak[:, :, 0:1], 1.0 - 1e30)
            dve.memset(sa[:, 0:1], 0.0)
            dve.memset(sb_[:, 0:1], 0.0)
            dve.wait_ge(decay_e, 1)
            own.inc(dve.tensor_scalar(decay[:, :], decay[:, :], -1.0, None, ALU.mult))

            def exponents(b, d):
                dve.wait_ge(moved, NP * b + HC + 2 * d + 2)
                k, pk, e = kk[:, d % 2, :], peak[:, d % 2, :], ex[:, d % 2, :, :]
                own.inc(dve.tensor_tensor_scan(pk[:, 1:], decay[:, d:d + 1].to_broadcast([P, T]), k,
                                               1.0 - 1e30, ALU.add, ALU.max))
                own.wait()
                own.inc(dve.scalar_tensor_tensor(q[:, :], k, first[:, d:d + 1], pk[:, 0:T], ALU.add, ALU.max))
                dve.scalar_tensor_tensor(e[:, 2, :], pk[:, 0:T], decay[:, d:d + 1], pk[:, 1:], ALU.add, ALU.subtract)
                dve.tensor_tensor(e[:, 3, :], k, pk[:, 1:], ALU.subtract)
                own.wait()
                dve.tensor_tensor(e[:, 0, :], pk[:, 0:T], q[:, :], ALU.subtract)
                dve.scalar_tensor_tensor(e[:, 1, :], k, first[:, d:d + 1], q[:, :],
                                         ALU.add, ALU.subtract).then_inc(diffs, 1)

            def weighted(b, d):
                dve.wait_ge(exps, HC * b + d + 1)
                v, e = vv[:, d % 2, :], ex[:, d % 2, :, :]
                own.inc(dve.tensor_tensor(cv[:, :], e[:, 3, :], v, ALU.mult))
                own.inc(dve.tensor_tensor_scan(sb_[:, 1:], e[:, 2, :], e[:, 3, :], 0.0, ALU.mult, ALU.add))
                own.wait()
                own.inc(dve.tensor_tensor_scan(sa[:, 1:], e[:, 2, :], cv[:, :], 0.0, ALU.mult, ALU.add))
                own.inc(dve.tensor_tensor(t2[:, :], e[:, 0, :], sb_[:, 0:T], ALU.mult))
                own.wait()
                own.inc(dve.tensor_tensor(t1[:, :], e[:, 0, :], sa[:, 0:T], ALU.mult))
                own.inc(dve.tensor_tensor(cv[:, :], e[:, 1, :], v, ALU.mult))
                own.wait()
                own.inc(dve.tensor_tensor(t2[:, :], t2[:, :], e[:, 1, :], ALU.add))
                own.inc(dve.tensor_tensor(t1[:, :], t1[:, :], cv[:, :], ALU.add))
                own.wait()
                own.inc(dve.scalar_tensor_tensor(q[:, :], t2[:, :], 0.0, t2[:, :], ALU.is_equal, ALU.add))
                own.wait()
                own.inc(dve.reciprocal(q[:, :], q[:, :]))
                own.inc(dve.scalar_tensor_tensor(t1[:, :], t2[:, :], 0.0, t1[:, :], ALU.not_equal, ALU.mult))
                own.wait()
                own.inc(dve.tensor_tensor(t1[:, :], t1[:, :], q[:, :], ALU.mult))
                own.wait()
                if d == 0:
                    dve.wait_ge(o_ready, TT * b)
                dve.tensor_tensor(rw[:, d, :], t1[:, :], r[:, d, :], ALU.mult).then_inc(rw_ready, 1)

            with dve.Fori(0, B) as b:
                own.turn(b)
                dve.wait_ge(x_in_s, 16 * b + 16)
                ln.statistics(dve, own, x).then_inc(ln.var_ready, 1)
                dve.wait_ge(ln.sd_ready, 2 * b + 1)
                dve.wait_ge(xl_added, TT * b)
                ln.normalise(dve, own, x, xl).then_inc(xl_ready, 1)
                dve.wait_ge(xl_ready, b + 1)
                ln.statistics(dve, own, xl).then_inc(ln.var_ready, 1)
                dve.wait_ge(ln.sd_ready, 2 * b + 2)
                dve.wait_ge(ln.turned, HC * b)
                ln.normalise(dve, own, xl, ln.xn).then_inc(ln.xn_ready, 1)
                dve.wait_ge(ln.xT_ready, HC * b + HC)
                own.inc(dve.tensor_tensor(step[:, :, :], xT[:, :, 1:], xT[:, :, 0:T], ALU.subtract))
                own.wait()
                for n, mix in enumerate((mix_r, mix_k, mix_v)):
                    for c in range(HC):
                        last = dve.scalar_tensor_tensor(mixed[n][:, c, :], step[:, c, :], mix[:, c:c + 1],
                                                        xT[:, c, 0:T], ALU.mult, ALU.add)
                    last.then_inc(mixed_ready, 1)
                exponents(b, 0)
                exponents(b, 1)
                for d in range(HC):
                    weighted(b, d)
                    if d + 2 < HC:
                        exponents(b, d + 2)
                dve.wait_ge(xl_added, TT * b + TT)
                for i in range(TT):
                    dve.wait_ge(o_ready, TT * b + i + 1)
                    dve.tensor_tensor(x[:, i, :], ps[:, i % 2, :], x[:, i, :], ALU.add).then_inc(added, 1)
                own.end()


def memory_attention(nc, ps, ident, eps, x_in, x_out, mem, memT, mask):
    MC = T // P
    SCALE = float(H) ** -0.5
    with ExitStack() as ctx:
        st = Stage(nc, ctx, "ma")
        x = st.sb("x", [P, TT, H])
        xT = st.sb("xT", [P, HC, T])
        memory = st.sb("memory", [P, MC, H])
        memoryT = st.sb("memoryT", [P, HC, T])
        mask8 = st.sb("mask8", [P, T], U8)
        maskf = st.sb("maskf", [P, T])
        neg = st.sb("neg", [P, T])
        valid = st.sb("valid", [P, 1])
        one_row = st.sb("one_row", [1, P])
        prob = st.sb("prob", [P, 2, T])
        probT = st.sb("probT", [P, 2, MC, P])
        top = st.sb("top", [P, TT])
        ntop = st.sb("ntop", [P, TT])
        total = st.sb("total", [P, TT])
        inv = st.sb("inv", [P, TT])
        ln = Columns(st, ps, ident, eps, xT)
        x_in_s, x_out_s, mem_in = st.sem("x_in"), st.sem("x_out"), st.sem("mem_in")
        set_up = st.sem("set_up")
        neg_ready = st.sem("neg_ready")
        scores = st.sem("scores")
        tops = st.sem("tops")
        probs = st.sem("probs")
        pT_psum = st.sem("pT_psum")
        pT_ready = st.sem("pT_ready")
        o_ready = st.sem("o_ready")
        added = st.sem("added")
        v_own = st.sem("v_own")
        block = ctx.enter_context(nc.Block())

        @block.sync
        def _(sp):
            with sp.Fori(0, B) as b:
                sp.wait_ge(x_out_s, 16 * b)
                sp.dma_start(x[:, :, :], rows_of(x_in, b)).then_inc(x_in_s, 16)
                sp.wait_ge(added, TT * b)
                sp.dma_start(memoryT[:, :, :], memT.rearrange("b (c p) m -> b p c m", p=P)[b]).then_inc(mem_in, 16)
                sp.dma_start(memory[:, :, :], mem.rearrange("b (c p) d -> b p c d", p=P)[b]).then_inc(mem_in, 16)
                sp.dma_start(mask8[:, :], mask.rearrange("b (a m) -> b a m", a=1)[b].to_broadcast([P, T])).then_inc(mem_in, 16)
                sp.wait_ge(added, TT * b + TT)
                sp.dma_start(rows_of(x_out, b), x[:, :, :]).then_inc(x_out_s, 16)
            sp.wait_ge(x_out_s, 16 * B)

        @block.scalar
        def _(act):
            with act.Fori(0, B) as b:
                ln.scalar_sd(act, b)
                ln.scalar_move(act, b)
                for i in range(TT):
                    act.wait_ge(tops, TT * b + i + 1)
                    act.wait_ge(pT_psum, TT * b + max(i - 1, 0))
                    act.activation(prob[:, i % 2, :], ps[:, 2 + i % 2, :], ACT.Exp, bias=ntop[:, i:i + 1],
                                   scale=SCALE, accum_out=total[:, i:i + 1]).then_inc(probs, 1)
                    act.wait_ge(pT_psum, TT * b + i + 1)
                    act.wait_ge(o_ready, TT * b + max(i - 1, 0))
                    act.activation(probT[:, i % 2, :, :], ps[:, 4 + i % 2, :], ACT.Identity).then_inc(pT_ready, 1)

        @block.tensor
        def _(pe):
            pe.wait_ge(set_up, 1)
            with pe.Fori(0, B) as b:
                pe.wait_ge(added, TT * b)
                ln.tensor(pe, b)
                pe.wait_ge(mem_in, 48 * b + 48)
                pe.wait_ge(neg_ready, b + 1)
                pe.wait_ge(ln.xT_ready, HC * b + HC)

                def score(i):
                    pe.wait_ge(probs, TT * b + max(i - 1, 0))
                    pe.matmul(ps[:, 2 + i % 2, :], one_row[:, :], neg[0:1, :], start=True, stop=False)
                    for c in range(HC):
                        last = pe.matmul(ps[:, 2 + i % 2, :], xT[:, c, i * P:(i + 1) * P], memoryT[:, c, :],
                                         start=False, stop=(c == HC - 1))
                    last.then_inc(scores, 1)

                score(0)
                for i in range(TT):
                    if i + 1 < TT:
                        score(i + 1)
                    pe.wait_ge(probs, TT * b + i + 1)
                    pe.wait_ge(pT_ready, TT * b + max(i - 1, 0))
                    for m in range(MC):
                        last = pe.transpose(ps[:, 4 + i % 2, m * P:(m + 1) * P],
                                            prob[:, i % 2, m * P:(m + 1) * P], ident)
                    last.then_inc(pT_psum, 1)
                    pe.wait_ge(pT_ready, TT * b + i + 1)
                    pe.wait_ge(added, TT * b + max(i - 1, 0))
                    for m in range(MC):
                        last = pe.matmul(ps[:, 6 + i % 2, :], probT[:, i % 2, m, :], memory[:, m, :],
                                         start=(m == 0), stop=(m == MC - 1))
                    last.then_inc(o_ready, 1)

        @block.vector
        def _(dve):
            own = Chain(dve, v_own, 19)
            dve.memset(one_row[:, :], 1.0).then_inc(set_up, 1)
            with dve.Fori(0, B) as b:
                own.turn(b)
                dve.wait_ge(x_in_s, 16 * b + 16)
                ln.vector(dve, own, b, x)
                dve.wait_ge(mem_in, 48 * b + 48)
                own.inc(dve.tensor_copy(maskf[:, :], mask8[:, :]))
                own.wait()
                dve.wait_ge(scores, TT * b)
                own.inc(dve.tensor_scalar(neg[:, :], maskf[:, :], -NEG, NEG, ALU.mult, ALU.add))
                dve.tensor_reduce(valid[:, :], maskf[:, :], AX.X, ALU.max).then_inc(neg_ready, 1)

                def finish(i):
                    dve.wait_ge(probs, TT * b + i + 1)
                    own.inc(dve.reciprocal(inv[:, i:i + 1], total[:, i:i + 1]))
                    own.wait()
                    own.inc(dve.tensor_scalar(inv[:, i:i + 1], inv[:, i:i + 1], valid[:, 0:1], None, ALU.mult))
                    own.wait()
                    dve.wait_ge(o_ready, TT * b + i + 1)
                    dve.scalar_tensor_tensor(x[:, i, :], ps[:, 6 + i % 2, :], inv[:, i:i + 1], x[:, i, :],
                                             ALU.mult, ALU.add).then_inc(added, 1)

                for i in range(TT):
                    dve.wait_ge(scores, TT * b + i + 1)
                    own.inc(dve.tensor_reduce(top[:, i:i + 1], ps[:, 2 + i % 2, :], AX.X, ALU.max))
                    own.wait()
                    dve.tensor_scalar(ntop[:, i:i + 1], top[:, i:i + 1], -SCALE, None, ALU.mult).then_inc(tops, 1)
                    if i:
                        finish(i - 1)
                finish(TT - 1)
                own.end()


F_IN = 2048
FC = F_IN // P


def ffn_inputs(i):
    return {
        "w1T": i["L0_ffn_w1"].T,
        "w2T": i["L0_ffn_w2"].T,
        "ffn_rows": np.stack([i["L0_ffn_b1"], i["L0_ffn_ln_g"], i["L0_ffn_ln_b"]]),
        "ffn_b2": i["L0_ffn_b2"].reshape(1, H),
    }


def ternary_ffn(nc, ps, ident, identb, ones, eps, x_in, x_out, dram):
    sizes = {"w1T": (HC, F_IN), "w2T": (FC, H)}
    with ExitStack() as outer:
        keep = Stage(nc, outer, "ff")
        tern = {n: keep.sb(f"tern_{n}", [P, *s], BF16) for n, s in sizes.items()}
        mean_w = keep.sb("mean_w", [P, 2])
        inv_w = keep.sb("inv_w", [P, 2])

        with ExitStack() as ctx:
            st = Stage(nc, ctx, "fq")
            w = {n: st.sb(n, [P, *s]) for n, s in sizes.items()}
            scrap = st.sb("scrap", [P, HC * F_IN], BF16)
            sums = st.sb("sums", [P, 2])
            w_in = [st.sem("w1_in"), st.sem("w2_in")]
            summed = st.sem("summed")
            total = st.sem("total")
            rounded = st.sem("rounded")
            done = st.sem("done")
            v_own = st.sem("v_own")
            block = ctx.enter_context(nc.Block())

            @block.sync
            def _(sp):
                for k, n in enumerate(sizes):
                    sp.dma_start(w[n][:, :, :], dram[n].rearrange("(c p) o -> p c o", p=P)).then_inc(w_in[k], 16)

            @block.scalar
            def _(act):
                for k, n in enumerate(sizes):
                    act.wait_ge(w_in[k], 16)
                    if k:
                        act.wait_ge(summed, k)
                    act.activation(scrap[:, :], w[n][:, :, :].rearrange("p c o -> p (c o)"), ACT.Abs,
                                   accum_out=sums[:, k:k + 1]).then_inc(summed, 1)
                for k, n in enumerate(sizes):
                    act.wait_ge(rounded, k + 1)
                    act.activation(tern[n][:, :, :], w[n][:, :, :], ACT.Copy, bias=-ROUND).then_inc(done, 1)

            @block.tensor
            def _(pe):
                pe.wait_ge(summed, 2)
                pe.matmul(ps[:, 0, 0:2], ones, sums[:, :], start=True, stop=True).then_inc(total, 1)

            @block.vector
            def _(dve):
                own = Chain(dve, v_own)
                dve.wait_ge(total, 1)
                own.inc(dve.tensor_scalar(mean_w[:, :], ps[:, 0, 0:2], 1.0 / (F_IN * H), 1e-5, ALU.mult, ALU.max))
                own.wait()
                own.inc(dve.reciprocal(inv_w[:, :], mean_w[:, :]))
                own.wait()
                for k, n in enumerate(sizes):
                    own.inc(dve.tensor_scalar(w[n][:, :, :], w[n][:, :, :], inv_w[:, k:k + 1], ROUND, ALU.mult, ALU.add))
                    own.wait()
                    dve.tensor_scalar(w[n][:, :, :], w[n][:, :, :], ROUND - 1.0, ROUND + 1.0,
                                      ALU.max, ALU.min).then_inc(rounded, 1)

        with ExitStack() as ctx:
            st = Stage(nc, ctx, "ff")
            x = st.sb("x", [P, TT, H])
            rows = st.sb("rows", [P, 3, F_IN])
            b2 = st.sb("b2", [P, H])
            h = st.sb("h", [P, TT, F_IN])
            scrap = st.sb("scrap", [P, F_IN], BF16)
            q1 = st.sb("q1", [P, TT, H], BF16)
            q1T = st.sb("q1T", [P, HC, T], BF16)
            q2 = st.sb("q2", [P, 2, F_IN], BF16)
            q2T = st.sb("q2T", [P, 2, FC, P], BF16)
            stats = st.sb("stats", [P, TT, F_IN // 512, 6])
            mv = st.sb("mv", [P, TT, 2])
            pause = st.sb("pause", [P, 1])
            sd, rstd, ss, rms, amax, step1, step2, f = (
                st.sb(n, [P, TT]) for n in ("sd", "rstd", "ss", "rms", "amax", "step1", "step2", "f"))
            c1, c2 = st.sb("c1", [P, TT]), st.sb("c2", [P, TT])
            ln = Columns(st, ps, ident, eps, None)
            x_in_s, x_out_s, rows_in = st.sem("x_in"), st.sem("x_out"), st.sem("rows_in")
            b2_added = st.sem("b2_added")
            squares = st.sem("squares")
            rms_ready = st.sem("rms_ready")
            clipped = st.sem("clipped")
            q_ready = st.sem("q_ready")
            turned1, q1T_ready = st.sem("turned1"), st.sem("q1T_ready")
            turned2, q2T_ready = st.sem("turned2"), st.sem("q2T_ready")
            h_psum = st.sem("h_psum")
            h_raw = st.sem("h_raw")
            h_act = st.sem("h_act")
            sd2 = st.sem("sd2")
            h_norm = st.sem("h_norm")
            h_ln = st.sem("h_ln")
            silu_done = st.sem("silu_done")
            var2 = st.sem("var2")
            o_ready = st.sem("o_ready")
            added = st.sem("added")
            v_own, a_own, g_own = st.sem("v_own"), st.sem("a_own"), st.sem("g_own")
            block = ctx.enter_context(nc.Block())

            @block.sync
            def _(sp):
                sp.dma_start(rows[:, :, :], dram["ffn_rows"].rearrange("(a r) o -> a r o", a=1)
                             .to_broadcast([P, 3, F_IN])).then_inc(rows_in, 16)
                sp.dma_start(b2[:, :], dram["ffn_b2"].to_broadcast([P, H])).then_inc(rows_in, 16)
                with sp.Fori(0, B) as b:
                    sp.wait_ge(x_out_s, 16 * b)
                    sp.dma_start(x[:, :, :], rows_of(x_in, b)).then_inc(x_in_s, 16)
                    sp.wait_ge(added, TT * b + TT)
                    sp.dma_start(rows_of(x_out, b), x[:, :, :]).then_inc(x_out_s, 16)
                sp.wait_ge(x_out_s, 16 * B)

            @block.gpsimd
            def _(pool):
                own = Chain(pool, g_own, TT)
                pool.wait_ge(rows_in, 32)
                with pool.Fori(0, B) as b:
                    own.turn(b)
                    pool.wait_ge(ln.xn_ready, b + 1)
                    for i in range(TT):
                        pool.tensor_tensor(x[:, i, :], x[:, i, :], b2[:, :], ALU.add).then_inc(b2_added, 1)
                    for i in range(TT):
                        pool.wait_ge(h_norm, TT * b + i + 1)
                        own.inc(pool.tensor_tensor(h[:, i, :], h[:, i, :], rows[:, 1, :], ALU.mult))
                        own.wait()
                        pool.tensor_tensor(h[:, i, :], h[:, i, :], rows[:, 2, :], ALU.add).then_inc(h_ln, 1)
                    own.end()

            @block.scalar
            def _(act):
                with act.Fori(0, B) as b:
                    ln.scalar_sd(act, b)
                    act.wait_ge(ln.xn_ready, b + 1)
                    for i in range(TT):
                        act.wait_ge(squares, 2 * TT * b + i)
                        act.activation(scrap[:, 0:H], ln.xn[:, i, :], ACT.Square,
                                       accum_out=ss[:, i:i + 1]).then_inc(squares, 1)
                    act.wait_ge(squares, 2 * TT * b + TT)
                    act.activation(rms[:, :], ss[:, :], ACT.Sqrt, bias=eps, scale=1.0 / H).then_inc(rms_ready, 1)
                    for i in range(TT):
                        act.wait_ge(clipped, 2 * TT * b + i + 1)
                        act.wait_ge(turned1, 2 * b)
                        act.activation(q1[:, i, :], ln.xn[:, i, :], ACT.Copy, bias=-ROUND).then_inc(q_ready, 1)
                    for k in range(2):
                        act.wait_ge(turned1, 2 * b + k + 1)
                        act.activation(q1T[:, 2 * k:2 * k + 2, :], ps[:, 4 + k, :].bitcast(BF16),
                                       ACT.Copy).then_inc(q1T_ready, 1)
                    for i in range(TT):
                        act.wait_ge(h_raw, TT * b + i + 1)
                        act.activation(h[:, i, :], h[:, i, :], ACT.Silu).then_inc(silu_done, 1)
                    for i in range(TT):
                        act.wait_ge(silu_done, TT * b + i + 1)
                        act.activation(h[:, i, :], h[:, i, :], ACT.Gelu).then_inc(h_act, 1)
                    act.wait_ge(var2, b + 1)
                    act.activation(sd[:, :], mv[:, :, 1], ACT.Sqrt, bias=eps).then_inc(sd2, 1)
                    for i in range(TT):
                        act.wait_ge(h_ln, TT * b + i + 1)
                        act.wait_ge(squares, 2 * TT * b + TT + i)
                        act.activation(scrap[:, :], h[:, i, :], ACT.Square,
                                       accum_out=ss[:, i:i + 1]).then_inc(squares, 1)
                    act.wait_ge(squares, 2 * TT * b + 2 * TT)
                    act.activation(rms[:, :], ss[:, :], ACT.Sqrt, bias=eps, scale=1.0 / F_IN).then_inc(rms_ready, 1)
                    for i in range(TT):
                        act.wait_ge(clipped, 2 * TT * b + TT + i + 1)
                        act.wait_ge(turned2, 2 * TT * b + max(2 * (i - 1), 0))
                        act.activation(q2[:, i % 2, :], h[:, i, :], ACT.Copy, bias=-ROUND).then_inc(q_ready, 1)
                        for k in range(2):
                            act.wait_ge(turned2, 2 * TT * b + 2 * i + k + 1)
                            act.wait_ge(o_ready, TT * b + max(i - 1, 0))
                            act.activation(q2T[:, i % 2, 8 * k:8 * k + 8, :], ps[:, 4 + k, :].bitcast(BF16),
                                           ACT.Copy).then_inc(q2T_ready, 1)

            @block.tensor
            def _(pe):
                with pe.Fori(0, B) as b:
                    pe.wait_ge(q_ready, 2 * TT * b + TT)
                    pe.wait_ge(q2T_ready, 2 * TT * b)
                    for k in range(2):
                        for c in range(2 * k, 2 * k + 2):
                            for i in range(TT):
                                last = pe.transpose(
                                    ps[:, 4 + k, :].bitcast(BF16)[:, (c % 2 * TT + i) * P:(c % 2 * TT + i + 1) * P],
                                    q1[:, i, c * P:(c + 1) * P], identb)
                        last.then_inc(turned1, 1)
                    pe.wait_ge(q1T_ready, 2 * b + 2)
                    for i in range(TT):
                        pe.wait_ge(h_raw, TT * b + i)
                        for n in range(F_IN // 512):
                            for c in range(HC):
                                last = pe.matmul(ps[:, n, :], q1T[:, c, i * P:(i + 1) * P],
                                                 tern["w1T"][:, c, n * 512:(n + 1) * 512],
                                                 start=(c == 0), stop=(c == HC - 1))
                        last.then_inc(h_psum, 1)
                    for i in range(TT):
                        pe.wait_ge(q_ready, 2 * TT * b + TT + i + 1)
                        for k in range(2):
                            pe.wait_ge(q1T_ready, 2 * b + 2)
                            pe.wait_ge(q2T_ready, 2 * TT * b + max(2 * i + k - 1, 0))
                            for c in range(8):
                                last = pe.transpose(ps[:, 4 + k, :].bitcast(BF16)[:, c * P:(c + 1) * P],
                                                    q2[:, i % 2, (8 * k + c) * P:(8 * k + c + 1) * P], identb)
                            last.then_inc(turned2, 1)
                        pe.wait_ge(q2T_ready, 2 * TT * b + 2 * i + 2)
                        pe.wait_ge(added, TT * b + max(i - 1, 0))
                        for c in range(FC):
                            last = pe.matmul(ps[:, 6 + i % 2, :], q2T[:, i % 2, c, :], tern["w2T"][:, c, :],
                                             start=(c == 0), stop=(c == FC - 1))
                        last.then_inc(o_ready, 1)

            @block.vector
            def _(dve):
                own = Chain(dve, v_own, 50)
                dve.wait_ge(rows_in, 32)

                def steps(n, step, mean, c):
                    own.inc(dve.reciprocal(rms[:, :], rms[:, :]))
                    own.wait()
                    own.inc(dve.tensor_tensor(step[:, :], amax[:, :], rms[:, :], ALU.mult))
                    own.wait()
                    own.inc(dve.tensor_scalar(step[:, :], step[:, :], 1e-5, 1.0 / 127.0, ALU.max, ALU.mult))
                    own.wait()
                    own.inc(dve.reciprocal(f[:, :], step[:, :]))
                    own.inc(dve.tensor_scalar(c[:, :], step[:, :], mean, None, ALU.mult))
                    own.wait()
                    own.inc(dve.tensor_tensor(f[:, :], f[:, :], rms[:, :], ALU.mult))
                    own.wait()

                def to_grid(v, i):
                    own.inc(dve.tensor_scalar(v[:, i, :], v[:, i, :], f[:, i:i + 1], ROUND, ALU.mult, ALU.add))
                    own.wait()
                    dve.tensor_scalar(v[:, i, :], v[:, i, :], ROUND - 128.0, ROUND + 127.0,
                                      ALU.max, ALU.min).then_inc(clipped, 1)

                with dve.Fori(0, B) as b:
                    own.turn(b)
                    dve.wait_ge(x_in_s, 16 * b + 16)
                    ln.statistics(dve, own, x).then_inc(ln.var_ready, 1)
                    dve.wait_ge(ln.sd_ready, b + 1)
                    ln.normalise(dve, own, x, ln.xn).then_inc(ln.xn_ready, 1)
                    dve.wait_ge(ln.xn_ready, b + 1)
                    for i in range(TT):
                        own.inc(dve.tensor_reduce(amax[:, i:i + 1], ln.xn[:, i, :], AX.X, ALU.max,
                                                  apply_absolute_value=True))
                    dve.wait_ge(rms_ready, 2 * b + 1)
                    steps(1, step1, mean_w[:, 0:1], c1)
                    for i in range(TT):
                        to_grid(ln.xn, i)
                    for i in range(TT):
                        dve.wait_ge(h_psum, TT * b + i + 1)
                        dve.scalar_tensor_tensor(h[:, i, :], ps[:, 0:4, :].rearrange("p a n -> p (a n)"),
                                                 c1[:, i:i + 1], rows[:, 0, :], ALU.mult, ALU.add).then_inc(h_raw, 1)
                    for i in range(TT):
                        dve.wait_ge(h_act, TT * b + i + 1)
                        for n in range(F_IN // 512):
                            own.inc(dve.bn_stats(stats[:, i, n, :], h[:, i, n * 512:(n + 1) * 512]))
                    own.wait()
                    dve.memset(pause[:, :], 0.0)
                    for i in range(TT):
                        last = dve.bn_aggr(mv[:, i, :], stats[:, i, :, :].rearrange("p a s -> p (a s)"))
                    last.then_inc(var2, 1)
                    dve.wait_ge(sd2, b + 1)
                    own.inc(dve.reciprocal(rstd[:, :], sd[:, :]))
                    own.wait()
                    for i in range(TT):
                        dve.tensor_scalar(h[:, i, :], h[:, i, :], mv[:, i, 0:1], rstd[:, i:i + 1],
                                          ALU.subtract, ALU.mult).then_inc(h_norm, 1)
                    for i in range(TT):
                        dve.wait_ge(h_ln, TT * b + i + 1)
                        own.inc(dve.tensor_reduce(amax[:, i:i + 1], h[:, i, :], AX.X, ALU.max,
                                                  apply_absolute_value=True))
                    dve.wait_ge(rms_ready, 2 * b + 2)
                    steps(2, step2, mean_w[:, 1:2], c2)
                    for i in range(TT):
                        to_grid(h, i)
                    for i in range(TT):
                        dve.wait_ge(o_ready, TT * b + i + 1)
                        dve.wait_ge(b2_added, TT * b + TT)
                        dve.scalar_tensor_tensor(x[:, i, :], ps[:, 6 + i % 2, :], c2[:, i:i + 1], x[:, i, :],
                                                 ALU.mult, ALU.add).then_inc(added, 1)
                    own.end()


DI, NS, RK, KC = 1024, 16, 128, 4
DC = DI // P


def mamba_inputs(i):
    per_channel = np.concatenate(
        [i["L1_attn_Wconv"].reshape(DI, KC)] + [i[f"L1_attn_{n}"].reshape(DI, 1) for n in ("bconv", "D", "bdt")]
        + [i["L1_attn_A_log"]], axis=1)
    return {
        "mb_cols": per_channel.reshape(DC, P, KC + 3 + NS).transpose(1, 0, 2),
        "WinT": i["L1_attn_Win"].T,
        "WxT": i["L1_attn_Wx"].T,
        "WdtT": i["L1_attn_Wdt"].T,
        "WoutT": i["L1_attn_Wout"].T,
    }


def mamba(nc, ps, ident, eps, x_in, x_out, dram):
    with ExitStack() as ctx:
        st = Stage(nc, ctx, "mb")
        x = st.sb("x", [P, TT, H])
        xT = st.sb("xT", [P, HC, T])
        ln = Columns(st, ps, ident, eps, xT)
        w_in = st.sb("w_in", [P, HC, 2 * DI])
        w_x = st.sb("w_x", [P, DC, RK + 2 * NS])
        w_dt = st.sb("w_dt", [P, DI])
        w_out = st.sb("w_out", [P, DC, H])
        col = st.sb("col", [P, DC, KC + 3 + NS])
        taps, bconv, skip, bdt = col[:, :, 0:KC], col[:, :, KC], col[:, :, KC + 1], col[:, :, KC + 2]
        neg_a = st.sb("neg_a", [P, DC, NS])
        hs = st.sb("hs", [P, DC, T])
        gate = st.sb("gate", [P, DC, T])
        dt_in = st.sb("dt_in", [P, T])
        bc = st.sb("bc", [2 * NS, T])
        bcs = st.sb("bcs", [P, 2 * NS, T])
        soft = st.sb("soft", [P, T])
        dt = st.sb("dt", [P, 2, T])
        u = st.sb("u", [P, 2, T])
        db = (st.sb("db", [P, 4, T]), xT)
        hc = ln.xn
        weights_in, x_in_s, x_out_s = st.sem("weights_in"), st.sem("x_in"), st.sem("x_out")
        a_exp, a_ready = st.sem("a_exp"), st.sem("a_ready")
        hs_psum, conv_done, hs_ready = st.sem("hs_psum"), st.sem("conv_done"), st.sem("hs_ready")
        gate_psum, gate_ready = st.sem("gate_psum"), st.sem("gate_ready")
        ssm_psum = st.sem("ssm_psum")
        ssm_moved = st.sem("ssm_moved")
        dt_psum = st.sem("dt_psum")
        dt_abs = st.sem("dt_abs")
        dt_e = st.sem("dt_e")
        dt_log = st.sem("dt_log")
        dt_relu = st.sem("dt_relu")
        dt_ready = st.sem("dt_ready")
        u_ready = st.sem("u_ready")
        db_ready = st.sem("db_ready")
        da_ready = st.sem("da_ready")
        scanned = st.sem("scanned")
        hc_ready = st.sem("hc_ready")
        summed = st.sem("summed")
        y_read = st.sem("y_read")
        yg_ready = st.sem("yg_ready")
        o_ready, added, v_own = st.sem("o_ready"), st.sem("added"), st.sem("v_own")
        block = ctx.enter_context(nc.Block())
        NU = DC * NS
        NB = 2 + 2 * NS

        @block.sync
        def _(sp):
            sp.dma_start(col[:, :, :], dram["mb_cols"]).then_inc(weights_in, 16)
            sp.dma_start(w_in[:, :, :], dram["WinT"].rearrange("(c p) e -> p c e", p=P)).then_inc(weights_in, 16)
            sp.dma_start(w_x[:, :, :], dram["WxT"].rearrange("(c p) e -> p c e", p=P)).then_inc(weights_in, 16)
            sp.dma_start(w_dt[:, :], dram["WdtT"]).then_inc(weights_in, 16)
            sp.dma_start(w_out[:, :, :], dram["WoutT"].rearrange("(c p) e -> p c e", p=P)).then_inc(weights_in, 16)
            with sp.Fori(0, B) as b:
                sp.wait_ge(x_out_s, 16 * b)
                sp.dma_start(x[:, :, :], rows_of(x_in, b)).then_inc(x_in_s, 16)
                sp.wait_ge(added, TT * b + TT)
                sp.dma_start(rows_of(x_out, b), x[:, :, :]).then_inc(x_out_s, 16)
            sp.wait_ge(x_out_s, 16 * B)

        @block.gpsimd
        def _(pool):
            with pool.Fori(0, B) as b:
                pool.wait_ge(ssm_moved, NB * b + NB)
                for d in range(DC):
                    pool.wait_ge(u_ready, DC * b + d + 1)
                    for g in range(NS // 4):
                        k = 4 * d + g
                        pool.wait_ge(scanned, NU * b + max(4 * (k - 1), 0))
                        pool.tensor_tensor(db[k % 2][:, :, :],
                                           u[:, d % 2, :].rearrange("p (a t) -> p a t", a=1).to_broadcast([P, 4, T]),
                                           bcs[:, 4 * g:4 * g + 4, :], ALU.mult).then_inc(db_ready, 1)

        @block.scalar
        def _(act):
            act.wait_ge(weights_in, 80)
            act.activation(neg_a[:, :, :], col[:, :, KC + 3:], ACT.Exp).then_inc(a_exp, 1)

            def softplus_parts(b, d):
                act.wait_ge(dt_psum, DC * b + d + 1)
                act.wait_ge(dt_ready, DC * b + d)
                act.wait_ge(u_ready, DC * b + d)
                act.activation(dt[:, d % 2, :], ps[:, 7, :], ACT.Relu, bias=bdt[:, d:d + 1]).then_inc(dt_relu, 1)
                act.activation(soft[:, :], ps[:, 7, :], ACT.Abs, bias=bdt[:, d:d + 1]).then_inc(dt_abs, 1)
                act.wait_ge(dt_abs, DC * b + d + 1)
                act.activation(soft[:, :], soft[:, :], ACT.Exp, scale=-1.0).then_inc(dt_e, 1)
                act.wait_ge(dt_e, DC * b + d + 1)
                act.activation(soft[:, :], soft[:, :], ACT.Ln, bias=1.0).then_inc(dt_log, 1)

            with act.Fori(0, B) as b:
                ln.scalar_sd(act, b)
                act.wait_ge(hs_psum, DC * b)
                act.wait_ge(gate_psum, DC * b)
                act.wait_ge(scanned, NU * b)
                ln.scalar_move(act, b)
                for c in range(DC):
                    act.wait_ge(conv_done, DC * b + c + 1)
                    act.activation(hs[:, c, :], hs[:, c, :], ACT.Silu, bias=bconv[:, c:c + 1]).then_inc(hs_ready, 1)
                    act.wait_ge(gate_psum, DC * b + c + 1)
                    act.wait_ge(o_ready, TT * b)
                    act.activation(gate[:, c, :], ps[:, 5 + c % 3, :], ACT.Silu).then_inc(gate_ready, 1)
                act.wait_ge(hc_ready, NU * b)
                for k in range(NB):
                    act.wait_ge(ssm_psum, NB * b + k + 1)
                    bank = ps[:, 2 + k % 6, :]
                    src, dst = ((bank, dt_in[:, :]), (bank[0:2 * NS, :], bc[:, :]), (bank, bcs[:, max(k - 2, 0), :]))[min(k, 2)]
                    act.activation(dst, src, ACT.Copy).then_inc(ssm_moved, 1)
                softplus_parts(b, 0)
                for d in range(DC):
                    act.wait_ge(dt_ready, DC * b + d + 1)
                    for n in range(NS):
                        k = NS * d + n
                        act.wait_ge(scanned, NU * b + max(k - 1, 0))
                        act.activation(ps[:, 2 + k % 2, :], dt[:, d % 2, :], ACT.Exp,
                                       scale=neg_a[:, d, n:n + 1]).then_inc(da_ready, 1)
                        if n == 4 and d + 1 < DC:
                            softplus_parts(b, d + 1)

        @block.tensor
        def _(pe):
            pe.wait_ge(weights_in, 80)
            with pe.Fori(0, B) as b:
                pe.wait_ge(added, TT * b)
                ln.tensor(pe, b)
                pe.wait_ge(ln.xT_ready, HC * b + HC)
                for c in range(DC):
                    pe.wait_ge(conv_done, DC * b + max(c - 2, 0))
                    for h in range(HC):
                        last = pe.matmul(ps[:, 2 + c % 3, :], w_in[:, h, c * P:(c + 1) * P], xT[:, h, :],
                                         start=(h == 0), stop=(h == HC - 1))
                    last.then_inc(hs_psum, 1)
                    pe.wait_ge(gate_ready, DC * b + max(c - 2, 0))
                    for h in range(HC):
                        last = pe.matmul(ps[:, 5 + c % 3, :], w_in[:, h, DI + c * P:DI + (c + 1) * P], xT[:, h, :],
                                         start=(h == 0), stop=(h == HC - 1))
                    last.then_inc(gate_psum, 1)
                pe.wait_ge(hs_ready, DC * b + DC)
                pe.wait_ge(gate_ready, DC * b + DC)
                for k in range(NB):
                    pe.wait_ge(ssm_moved, NB * b + max(k - 5, 0))
                    bank = ps[:, 2 + k % 6, :]
                    if k < 2:
                        for c in range(DC):
                            last = pe.matmul((bank, bank[0:2 * NS, :])[k],
                                             (w_x[:, c, 0:RK], w_x[:, c, RK:])[k], hs[:, c, :],
                                             start=(c == 0), stop=(c == DC - 1))
                    else:
                        pe.wait_ge(ssm_moved, NB * b + 2)
                        last = pe.matmul(bank, ident[0:2 * NS, k - 2:k - 1].to_broadcast([2 * NS, P]), bc[:, :],
                                         start=True, stop=True)
                    last.then_inc(ssm_psum, 1)
                pe.wait_ge(ssm_moved, NB * b + NB)

                def dt_chunk(d):
                    pe.wait_ge(dt_abs, DC * b + d)
                    pe.wait_ge(dt_relu, DC * b + d)
                    pe.matmul(ps[:, 7, :], w_dt[:, d * P:(d + 1) * P], dt_in[:, :],
                              start=True, stop=True).then_inc(dt_psum, 1)

                dt_chunk(0)
                for d in range(DC):
                    pe.wait_ge(y_read, DC * b + max(d - 1, 0))
                    for n in range(NS):
                        if n == 2 and d + 1 < DC:
                            dt_chunk(d + 1)
                        k = NS * d + n
                        pe.wait_ge(hc_ready, NU * b + k + 1)
                        pe.matmul(ps[:, d % 2, :], ident, hc[:, k % 4, :],
                                  start=(n == 0), stop=(n == NS - 1)).then_inc(summed, 1)
                pe.wait_ge(yg_ready, DC * b + DC)
                for i in range(TT):
                    pe.wait_ge(added, TT * b + max(i - 1, 0))
                    for d in range(DC):
                        last = pe.matmul(ps[:, i % 2, :], gate[:, d, i * P:(i + 1) * P], w_out[:, d, :],
                                         start=(d == 0), stop=(d == DC - 1))
                    last.then_inc(o_ready, 1)

        @block.vector
        def _(dve):
            own = Chain(dve, v_own, 29)
            dve.wait_ge(a_exp, 1)
            dve.tensor_scalar(neg_a[:, :, :], neg_a[:, :, :], -1.0, None, ALU.mult).then_inc(a_ready, 1)

            def dt_chunk(b, d):
                dve.wait_ge(dt_log, DC * b + d + 1)
                dve.wait_ge(dt_relu, DC * b + d + 1)
                dve.tensor_tensor(dt[:, d % 2, :], dt[:, d % 2, :], soft[:, :], ALU.add).then_inc(dt_ready, 1)
                dve.wait_ge(dt_ready, DC * b + d + 1)
                dve.tensor_tensor(u[:, d % 2, :], dt[:, d % 2, :], hs[:, d, :], ALU.mult).then_inc(u_ready, 1)

            def scan(b, k):
                dve.wait_ge(da_ready, NU * b + k + 1)
                dve.wait_ge(db_ready, NU // 4 * b + k // 4 + 1)
                dve.wait_ge(hc_ready, NU * b + max(k - 2, 0))
                dve.tensor_tensor_scan(ps[:, 4 + k % 3, :], ps[:, 2 + k % 2, :], db[k // 4 % 2][:, k % 4, :], 0.0,
                                       ALU.mult, ALU.add).then_inc(scanned, 1)

            def times_c(b, k):
                dve.wait_ge(scanned, NU * b + k + 1)
                dve.wait_ge(summed, NU * b + max(k - 3, 0))
                dve.tensor_tensor(hc[:, k % 4, :], ps[:, 4 + k % 3, :], bcs[:, NS + k % NS, :],
                                  ALU.mult).then_inc(hc_ready, 1)

            def finish(b, d):
                dve.wait_ge(summed, NU * b + NS * (d + 1))
                dve.scalar_tensor_tensor(hs[:, d, :], hs[:, d, :], skip[:, d:d + 1], ps[:, d % 2, :],
                                         ALU.mult, ALU.add).then_inc(y_read, 1)
                dve.wait_ge(y_read, DC * b + d + 1)
                dve.tensor_tensor(gate[:, d, :], gate[:, d, :], hs[:, d, :], ALU.mult).then_inc(yg_ready, 1)

            with dve.Fori(0, B) as b:
                own.turn(b)
                dve.wait_ge(x_in_s, 16 * b + 16)
                dve.wait_ge(summed, NU * b)
                ln.vector(dve, own, b, x)
                for c in range(DC):
                    dve.wait_ge(hs_psum, DC * b + c + 1)
                    dve.wait_ge(yg_ready, DC * b)
                    src = ps[:, 2 + c % 3, :]
                    own.inc(dve.tensor_scalar(hs[:, c, :], src, taps[:, c, KC - 1:KC], None, ALU.mult))
                    for j in range(1, KC):
                        own.wait()
                        last = dve.scalar_tensor_tensor(hs[:, c, j:], src[:, 0:T - j], taps[:, c, KC - 1 - j:KC - j],
                                                        hs[:, c, j:], ALU.mult, ALU.add)
                        if j < KC - 1:
                            own.inc(last)
                    last.then_inc(conv_done, 1)
                dt_chunk(b, 0)
                for k in range(NU):
                    scan(b, k)
                    if k:
                        times_c(b, k - 1)
                    if k % NS == 8 and k // NS + 1 < DC:
                        dt_chunk(b, k // NS + 1)
                    if k % NS == 3 and k >= NS:
                        finish(b, k // NS - 1)
                times_c(b, NU - 1)
                finish(b, DC - 1)
                for i in range(TT):
                    dve.wait_ge(o_ready, TT * b + i + 1)
                    dve.tensor_tensor(x[:, i, :], ps[:, i % 2, :], x[:, i, :], ALU.add).then_inc(added, 1)
                own.end()


NH, NKV, DH = 16, 4, 128
MEM = T
KT = (MEM + T) // P


def attention_inputs(i):
    f32 = np.float32
    inv_freq = (f32(1) / f32(10000) ** (np.arange(0, DH, 2, dtype=f32) / f32(DH))).astype(f32)
    angle = np.outer(np.arange(T, dtype=f32), inv_freq).astype(f32)
    half = np.cos(angle), np.sin(angle)
    rope = np.stack([np.concatenate([half[0], half[0]], 1), np.concatenate([-half[1], half[1]], 1)])
    late = np.where(np.arange(P)[None, :] > np.arange(P)[:, None], f32(NEG), f32(0))
    norm_rows = np.stack([i["L1_xattn_q_norm_w"], np.roll(i["L1_xattn_q_norm_w"], DH // 2),
                          i["L1_xattn_k_norm_w"], np.roll(i["L1_xattn_k_norm_w"], DH // 2)])
    return {
        "rope": rope.astype(f32),
        "late": late.astype(f32),
        "norm_rows": norm_rows,
        **{n: i[f"L1_xattn_{n}"] for n in ("wq", "wk", "wv", "wo", "wk_ctx", "wv_ctx")},
    }


def context_attention(nc, ps, ident, identb, eps, eps6, x_in, x_out, dram):
    SCALE = float(DH) ** -0.5
    HG = NH // NKV
    with ExitStack() as ctx:
        st = Stage(nc, ctx, "ca")
        x = st.sb("x", [P, TT, H])
        xT = st.sb("xT", [P, HC, T])
        ln = Columns(st, ps, ident, eps, xT)
        wq = st.sb("wq", [P, HC, NH * DH])
        wo = st.sb("wo", [P, NH, H])
        qT = st.sb("qT", [P, NH, T])
        kT = st.sb("kT", [P, NKV, MEM + T])
        v = st.sb("v", [P, KT, NKV * DH])
        tables = st.sb("tables", [P, 4, TT, DH])
        norm_rows = st.sb("norm_rows", [P, 4, DH])
        late = st.sb("late", [P, P])
        lateb = st.sb("lateb", [P, P], BF16)
        prob = st.sb("prob", [P, 2, MEM + T])
        pT = [st.sb("pT0", [P, KT, T]), st.sb("pT1", [P, KT, T])]
        memT = pT[0][:, 0:HC, :]
        w_kv = [pT[1][:, HC * s:HC * (s + 1), :] for s in range(2)]
        raw, sq, rot = ln.xn[:, 0:2, :], ln.xn[:, 2, :], ln.xn[:, 3, :]
        roped = prob[:, :, 0:512]
        ssq = st.sb("ssq", [P, TT, NH])
        q_scale = st.sb("q_scale", [P, TT, NH])
        ssk = st.sb("ssk", [P, 2, NKV])
        rk = st.sb("rk", [P, 2, NKV])
        top = st.sb("top", [P, 2])
        ntop = st.sb("ntop", [P, 2])
        total = st.sb("total", [P, 2])
        inv = st.sb("inv", [P, 2])

        weights_in, x_in_s, x_out_s, mem_in = (st.sem(n) for n in ("weights_in", "x_in", "x_out", "mem_in"))
        kv_in = [st.sem("wk_in"), st.sem("wkc_in"), st.sem("wv_in"), st.sem("wvc_in")]
        tables_ready = st.sem("tables_ready")
        proj = st.sem("proj")
        moved = st.sem("moved")
        squared = st.sem("squared")
        reduced = st.sem("reduced")
        rms_k = st.sem("rms_k")
        rope_done = st.sem("rope_done")
        qk_turned = st.sem("qk_turned")
        qk_moved = st.sem("qk_moved")
        rms_q = st.sem("rms_q")
        scale_ready = st.sem("scale_ready")
        scores = st.sem("scores")
        tops = st.sem("tops")
        exps = st.sem("exps")
        normed = st.sem("normed")
        turned = st.sem("turned")
        pT_moved = st.sem("pT_moved")
        pv_done = st.sem("pv_done")
        out_moved = st.sem("out_moved")
        o_ready, added, v_own = st.sem("o_ready"), st.sem("added"), st.sem("v_own")
        block = ctx.enter_context(nc.Block())

        turning = [("q", i, g) for i in range(TT) for g in range(NH // 4)] \
            + [("k", i, 0) for i in range(TT)] + [("kc", i, 1) for i in range(TT)]
        groups = turning + [("v", i, 2) for i in range(TT)] + [("vc", i, 3) for i in range(TT)]
        NJ, NQ, NR = len(groups), TT * NH // 4, len(turning)
        units = [(h, i) for h in range(NH) for i in range(TT)]
        NU = len(units)

        @block.sync
        def _(sp):
            sp.dma_start(ln.xn[:, 0:2, :].rearrange("p a (i d) -> p a i d", i=TT),
                         dram["rope"].rearrange("a (i p) d -> p a i d", p=P)).then_inc(weights_in, 16)
            sp.dma_start(norm_rows[:, :, :], dram["norm_rows"].rearrange("(a r) d -> a r d", a=1)
                         .to_broadcast([P, 4, DH])).then_inc(weights_in, 16)
            sp.dma_start(late[:, :], dram["late"]).then_inc(weights_in, 16)
            sp.dma_start(wq[:, :, :], dram["wq"].rearrange("(c p) n -> p c n", p=P)).then_inc(weights_in, 16)
            sp.dma_start(wo[:, :, :], dram["wo"].rearrange("(h p) n -> p h n", p=P)).then_inc(weights_in, 16)
            with sp.Fori(0, B) as b:
                sp.wait_ge(x_out_s, 16 * b)
                sp.dma_start(x[:, :, :], rows_of(x_in, b)).then_inc(x_in_s, 16)
                sp.wait_ge(pv_done, NH * b)
                sp.dma_start(memT[:, :, :], dram["ctxT"].rearrange("b (c p) m -> b p c m", p=P)[b]).then_inc(mem_in, 16)
                for k, n in enumerate(("wk", "wk_ctx", "wv", "wv_ctx")):
                    if k >= 2:
                        sp.wait_ge(proj, NJ * b + NQ + TT * (k - 1))
                    sp.dma_start(w_kv[k % 2], dram[n].rearrange("(c p) n -> p c n", p=P)).then_inc(kv_in[k], 16)
                sp.wait_ge(added, TT * b + TT)
                sp.dma_start(rows_of(x_out, b), x[:, :, :]).then_inc(x_out_s, 16)
            sp.wait_ge(x_out_s, 16 * B)

        @block.scalar
        def _(act):
            def move_turned(b, j):
                act.wait_ge(qk_turned, NR * b + j + 1)
                n, i, g = groups[j]
                dst = {"q": qT[:, 4 * g:4 * g + 4, i * P:(i + 1) * P],
                       "k": kT[:, :, MEM + i * P:MEM + (i + 1) * P],
                       "kc": kT[:, :, i * P:(i + 1) * P]}[n]
                act.activation(dst, ps[:, 4 + j % 2, :].rearrange("p (a s) -> p a s", a=4),
                               ACT.Copy).then_inc(qk_moved, 1)

            def exp(b, k):
                h, i = units[k]
                w = MEM + (i + 1) * P
                act.wait_ge(tops, NU * b + k + 1)
                act.wait_ge(turned, 2 * NU * b + max(2 * (k - 1), 0))
                act.activation(prob[:, k % 2, 0:w],
                               ps[:, 2 * (k % 2):2 * (k % 2) + 2, :].rearrange("p a n -> p (a n)")[:, 0:w], ACT.Exp,
                               bias=ntop[:, k % 2:k % 2 + 1], scale=q_scale[:, i, h:h + 1],
                               accum_out=total[:, k % 2:k % 2 + 1]).then_inc(exps, 1)

            def move_p(b, k):
                h, i = units[k]
                if i == 0:
                    act.wait_ge(pv_done, NH * b + max(h - 1, 0))
                for half, n in ((0, TT), (1, i + 1)):
                    act.wait_ge(turned, 2 * NU * b + 2 * k + half + 1)
                    act.activation(pT[h % 2][:, TT * half:TT * half + n, i * P:(i + 1) * P],
                                   ps[:, 4 + half, 0:n * P].rearrange("p (a s) -> p a s", a=n),
                                   ACT.Copy).then_inc(pT_moved, 1)

            with act.Fori(0, B) as b:
                ln.scalar_sd(act, b)
                ln.scalar_move(act, b)
                for j, (n, i, g) in enumerate(groups):
                    act.wait_ge(proj, NJ * b + j + 1)
                    if j >= NR:
                        act.activation(v[:, i + (TT if n == "v" else 0), :], ps[:, j % 4, :], ACT.Copy).then_inc(moved, 1)
                        if j == NR:
                            move_turned(b, NR - 1)
                        continue
                    act.wait_ge(rope_done, NR * b + max(j - 1, 0))
                    act.activation(raw[:, j % 2, :], ps[:, j % 4, :], ACT.Copy).then_inc(moved, 1)
                    act.wait_ge(moved, NJ * b + j + 1)
                    act.wait_ge(reduced, NR * b + j)
                    act.activation(sq, raw[:, j % 2, :], ACT.Square).then_inc(squared, 1)
                    if n != "q":
                        act.wait_ge(reduced, NR * b + j + 1)
                        act.activation(rk[:, j % 2, :], ssk[:, j % 2, :], ACT.Sqrt, bias=eps6,
                                       scale=1.0 / DH).then_inc(rms_k, 1)
                    if j:
                        move_turned(b, j - 1)
                act.activation(q_scale[:, :, :], ssq[:, :, :], ACT.Sqrt, bias=eps6, scale=1.0 / DH).then_inc(rms_q, 1)
                exp(b, 0)
                exp(b, 1)
                for k in range(NU):
                    move_p(b, k)
                    if k + 2 < NU:
                        exp(b, k + 2)

        @block.tensor
        def _(pe):
            pe.wait_ge(weights_in, 80)
            with pe.Fori(0, B) as b:
                pe.wait_ge(tables_ready, 1)
                pe.wait_ge(added, TT * b)
                ln.tensor(pe, b)
                pe.wait_ge(ln.xT_ready, HC * b + HC)
                pe.wait_ge(mem_in, 16 * b + 16)

                def turn_qk(j):
                    pe.wait_ge(rope_done, NR * b + j + 1)
                    pe.wait_ge(qk_moved, NR * b + max(j - 1, 0))
                    for a in range(4):
                        last = pe.transpose(ps[:, 4 + j % 2, a * P:(a + 1) * P],
                                            roped[:, j % 2, a * P:(a + 1) * P], ident)
                    last.then_inc(qk_turned, 1)

                for j, (n, i, g) in enumerate(groups):
                    if n != "q" and i == 0:
                        pe.wait_ge(kv_in[g], 16 * b + 16)
                    pe.wait_ge(moved, NJ * b + max(j - 3, 0))
                    src = memT if n in ("kc", "vc") else xT
                    for c in range(HC):
                        w = wq[:, c, g * 512:(g + 1) * 512] if n == "q" else w_kv[g % 2][:, c, :]
                        last = pe.matmul(ps[:, j % 4, :], src[:, c, i * P:(i + 1) * P], w,
                                         start=(c == 0), stop=(c == HC - 1))
                    last.then_inc(proj, 1)
                    if 1 <= j <= NR:
                        turn_qk(j - 1)
                pe.wait_ge(qk_moved, NR * b + NR)
                pe.wait_ge(moved, NJ * b + NJ)

                def score(k):
                    h, i = units[k]
                    pe.wait_ge(exps, NU * b + max(k - 1, 0))
                    q = qT[:, h, i * P:(i + 1) * P]
                    pe.matmul(ps[:, 2 * (k % 2), :], q, kT[:, h // HG, 0:MEM], start=True, stop=True)
                    own = ps[:, 2 * (k % 2) + 1, :]
                    pe.matmul(own[:, 0:(i + 1) * P], q, kT[:, h // HG, MEM:MEM + (i + 1) * P],
                              start=True, stop=False, skip_group_check=True)
                    pe.matmul(own[:, i * P:(i + 1) * P], identb, lateb[:, :], start=False, stop=True,
                              skip_group_check=True).then_inc(scores, 1)

                def turn(k):
                    h, i = units[k]
                    pe.wait_ge(normed, NU * b + k + 1)
                    for half, n in ((0, TT), (1, i + 1)):
                        pe.wait_ge(pT_moved, 2 * NU * b + max(2 * k + half - 1, 0))
                        for a in range(n):
                            m = TT * half + a
                            last = pe.transpose(ps[:, 4 + half, a * P:(a + 1) * P], prob[:, k % 2, m * P:(m + 1) * P], ident)
                        last.then_inc(turned, 1)

                def pv(h, part):
                    if part == 0:
                        pe.wait_ge(pT_moved, 2 * NU * b + 2 * TT * (h + 1))
                        pe.wait_ge(out_moved, NH * b + max(h - 1, 0))
                    for m in (2 * part, 2 * part + 1):
                        s0 = max(m - TT, 0) * P
                        last = pe.matmul(ps[:, 6 + h % 2, s0:T], v[:, m, h // HG * DH:(h // HG + 1) * DH],
                                         pT[h % 2][:, m, s0:T], start=(m == 0), stop=(m == KT - 1),
                                         skip_group_check=True)
                    if part == TT - 1:
                        last.then_inc(pv_done, 1)

                score(0)
                score(1)
                for k in range(NU + 6):
                    if k < NU:
                        turn(k)
                    if k + 2 < NU:
                        score(k + 2)
                    if k >= TT + 0 and (k - TT) // TT < NH:
                        pv((k - TT) // TT, (k - TT) % TT)
                for i in range(TT):
                    pe.wait_ge(out_moved, NH * b + NH)
                    pe.wait_ge(added, TT * b + max(i - 1, 0))
                    for h in range(NH):
                        last = pe.matmul(ps[:, i % 2, :], qT[:, h, i * P:(i + 1) * P], wo[:, h, :],
                                         start=(h == 0), stop=(h == NH - 1))
                    last.then_inc(o_ready, 1)

        @block.vector
        def _(dve):
            own = Chain(dve, v_own, 211)
            dve.wait_ge(weights_in, 80)
            dve.tensor_copy(lateb[:, :], late[:, :])
            for a in range(4):
                last = dve.tensor_tensor(tables[:, a, :, :], ln.xn[:, a % 2, :].rearrange("p (i d) -> p i d", i=TT),
                                         norm_rows[:, a:a + 1, :].to_broadcast([P, TT, DH]), ALU.mult)
            last.then_inc(tables_ready, 1)
            dve.wait_ge(tables_ready, 1)

            def by_head(t, lo=0, hi=DH):
                return t.rearrange("p (a d) -> p a d", d=DH)[:, :, lo:hi]

            def rope(b, j):
                n, i, g = groups[j]
                t = 0 if n == "q" else 2
                out, q = roped[:, j % 2, :], raw[:, j % 2, :]
                dve.wait_ge(squared, NR * b + j + 1)
                ss = ssq[:, i, 4 * g:4 * g + 4] if n == "q" else ssk[:, j % 2, :]
                dve.tensor_reduce(ss, by_head(sq), AX.X, ALU.add).then_inc(reduced, 1)
                dve.wait_ge(qk_turned, NR * b + max(j - 1, 0))
                if n == "kc":
                    own.inc(dve.tensor_tensor(by_head(out), by_head(q), norm_rows[:, 2:3, :].to_broadcast([P, 4, DH]),
                                              ALU.mult))
                    own.wait()
                else:
                    own.inc(dve.tensor_tensor(by_head(out), by_head(q),
                                              tables[:, t, i:i + 1, :].to_broadcast([P, 4, DH]), ALU.mult))
                    dve.wait_ge(rope_done, NR * b + j)
                    for lo in (0, DH // 2):
                        hi, other = lo + DH // 2, DH // 2 - lo
                        own.inc(dve.tensor_tensor(by_head(rot, lo, hi), by_head(q, other, other + DH // 2),
                                                  tables[:, t + 1, i:i + 1, lo:hi].to_broadcast([P, 4, DH // 2]),
                                                  ALU.mult))
                    own.wait()
                    last = dve.tensor_tensor(out, out, rot, ALU.add)
                    if n == "q":
                        last.then_inc(rope_done, 1)
                        return
                    own.inc(last)
                dve.wait_ge(rms_k, 2 * TT * b + j - NQ + 1)
                own.inc(dve.reciprocal(rk[:, j % 2, :], rk[:, j % 2, :]))
                own.wait()
                dve.tensor_tensor(by_head(out), by_head(out),
                                  rk[:, j % 2, :].rearrange("p (a o) -> p a o", o=1).to_broadcast([P, 4, DH]),
                                  ALU.mult).then_inc(rope_done, 1)

            def maximum(b, k):
                h, i = units[k]
                w = MEM + (i + 1) * P
                dve.wait_ge(scores, NU * b + k + 1)
                own.inc(dve.tensor_reduce(top[:, k % 2:k % 2 + 1],
                                          ps[:, 2 * (k % 2):2 * (k % 2) + 2, :].rearrange("p a n -> p (a n)")[:, 0:w],
                                          AX.X, ALU.max))
                own.wait()
                dve.tensor_scalar(ntop[:, k % 2:k % 2 + 1], top[:, k % 2:k % 2 + 1], q_scale[:, i, h:h + 1], -1.0,
                                  ALU.mult, ALU.mult).then_inc(tops, 1)

            def normalise(b, k):
                h, i = units[k]
                w = MEM + (i + 1) * P
                dve.wait_ge(exps, NU * b + k + 1)
                own.inc(dve.reciprocal(inv[:, k % 2:k % 2 + 1], total[:, k % 2:k % 2 + 1]))
                own.wait()
                dve.tensor_scalar(prob[:, k % 2, 0:w], prob[:, k % 2, 0:w], inv[:, k % 2:k % 2 + 1], None,
                                  ALU.mult).then_inc(normed, 1)

            def move_out(b, h):
                dve.wait_ge(pv_done, NH * b + h + 1)
                dve.tensor_copy(qT[:, h, :], ps[:, 6 + h % 2, :]).then_inc(out_moved, 1)

            with dve.Fori(0, B) as b:
                own.turn(b)
                dve.wait_ge(x_in_s, 16 * b + 16)
                ln.vector(dve, own, b, x)
                for j in range(NR):
                    rope(b, j)
                dve.wait_ge(rms_q, b + 1)
                own.inc(dve.reciprocal(q_scale[:, :, :], q_scale[:, :, :]))
                own.wait()
                own.inc(dve.tensor_scalar(q_scale[:, :, :], q_scale[:, :, :], SCALE, None, ALU.mult))
                own.wait()
                maximum(b, 0)
                for k in range(NU):
                    if k + 1 < NU:
                        maximum(b, k + 1)
                    normalise(b, k)
                    if k >= 2 * TT + 1 and k % TT == 1:
                        move_out(b, k // TT - 2)
                move_out(b, NH - 2)
                move_out(b, NH - 1)
                for i in range(TT):
                    dve.wait_ge(o_ready, TT * b + i + 1)
                    dve.tensor_tensor(x[:, i, :], ps[:, i % 2, :], x[:, i, :], ALU.add).then_inc(added, 1)
                own.end()


NE, TOP, SEL, FI = 64, 8, 4, 192
NT = B * TT


def expert_inputs(i):
    return {
        "gateT": i["L1_ffn_gate_weight"].T,
        "similarity": i["L1_ffn_similarity"],
        "guT": i["L1_ffn_gate_up_proj"].transpose(0, 2, 1),
        "downT": i["L1_ffn_down_proj"].transpose(0, 2, 1),
        "count_row": np.arange(NE, dtype=np.float32).reshape(1, NE),
    }


def route(nc, ps, ident, ones, eps, x_in, dram, x, xT, weight):
    with ExitStack() as ctx:
        st = Stage(nc, ctx, "rt")
        ln = Columns(st, ps, ident, eps, None)
        gateT = st.sb("gateT", [P, HC, NE])
        sim = st.sb("sim", [NE, NE])
        count = st.sb("count", [P, NE])
        prob = st.sb("prob", [P, NT, NE])
        top, total = st.sb("top", [P, NT]), st.sb("total", [P, NT])
        best = st.sb("best", [P, NT, TOP])
        index = st.sb("index", [P, NT, TOP], U32)
        indexf = st.sb("indexf", [P, NT, TOP])
        hot = st.sb("hot", [P, TT, TOP, NE])
        chosen = st.sb("chosen", [P, 2, NT, NE])
        later = st.sb("later", [P, NT, NE])
        laterT = st.sb("laterT", [NE, 2, P])
        primary = st.sb("primary", [NE, NE])
        cand = st.sb("cand", [NE, NE])
        cbest = st.sb("cbest", [NE, TOP])
        cindex = st.sb("cindex", [NE, TOP], U32)
        cindexf = st.sb("cindexf", [NE, TOP])
        moves = st.sb("moves", [NE, 3])
        to = st.sb("to", [NE, NE])
        const_in, x_in_s = st.sem("const_in"), st.sem("x_in")
        logits, logits_moved = st.sem("logits"), st.sem("logits_moved")
        shifted, exps = st.sem("shifted"), st.sem("exps")
        chosen_ready, counts = st.sem("chosen_ready"), st.sem("counts")
        to_ready = st.sem("to_ready")
        later_turned, later_moved = st.sem("later_turned"), st.sem("later_moved")
        sent, v_own = st.sem("sent"), st.sem("v_own")
        weight_ready = st.sem("weight_ready")
        block = ctx.enter_context(nc.Block())

        @block.sync
        def _(sp):
            sp.dma_start(x[:, :, :], x_in.rearrange("(n p) h -> p n h", p=P)).then_inc(x_in_s, 16)
            sp.dma_start(gateT[:, :, :], dram["gateT"].rearrange("(c p) e -> p c e", p=P)).then_inc(const_in, 16)
            sp.dma_start(sim[:, :], dram["similarity"]).then_inc(const_in, 16)
            sp.dma_start(count[:, :], dram["count_row"].to_broadcast([P, NE])).then_inc(const_in, 16)

        @block.scalar
        def _(act):
            with act.Fori(0, B) as b:
                ln.scalar_sd(act, b)
                for c in range(HC):
                    act.wait_ge(ln.turned, HC * b + c + 1)
                    act.activation(xT[:, b, c, :], ps[:, c % 2, :], ACT.Copy).then_inc(ln.xT_ready, 1)
            act.wait_ge(logits, 1)
            act.activation(prob[:, :, :].rearrange("p n e -> p (n e)"),
                           ps[:, 2:4, :].rearrange("p a n -> p (a n)"), ACT.Copy).then_inc(logits_moved, 1)
            act.wait_ge(shifted, 1)
            act.activation(prob[:, :, :], prob[:, :, :], ACT.Exp).then_inc(exps, 1)
            for n in range(NT):
                act.wait_ge(later_turned, n + 1)
                act.wait_ge(sent, max(n - 1, 0))
                act.activation(laterT[:, n % 2, :], ps[0:NE, n % 2, 0:P], ACT.Copy).then_inc(later_moved, 1)

        @block.tensor
        def _(pe):
            with pe.Fori(0, B) as b:
                ln.tensor(pe, b)
            pe.wait_ge(ln.xT_ready, HC * B)
            pe.wait_ge(const_in, 48)
            for n in range(NT):
                for c in range(HC):
                    last = pe.matmul(ps[:, 2 + n // 8, n % 8 * NE:(n % 8 + 1) * NE],
                                     xT[:, n // TT, c, n % TT * P:(n % TT + 1) * P], gateT[:, c, :],
                                     start=(c == 0), stop=(c == HC - 1))
            last.then_inc(logits, 1)
            pe.wait_ge(chosen_ready, B)
            for s in range(2):
                for n in range(NT):
                    pe.matmul(ps[:, 4, s * NE:(s + 1) * NE], ones, chosen[:, s, n, :],
                              start=(n == 0), stop=(n == NT - 1))
            for s in range(2):
                for n in range(NT):
                    last = pe.matmul(ps[0:NE, 5, s:s + 1], chosen[:, s, n, :], ones[:, 0:1],
                                     start=(n == 0), stop=(n == NT - 1))
            last.then_inc(counts, 1)
            for n in range(NT):
                pe.wait_ge(later_moved, max(n - 1, 0))
                pe.transpose(ps[0:NE, n % 2, 0:P], later[:, n, :], ident).then_inc(later_turned, 1)
                if n == 0:
                    pe.wait_ge(to_ready, 1)
                pe.wait_ge(later_moved, n + 1)
                pe.matmul(ps[:, 6 + n // 8, n % 8 * NE:(n % 8 + 1) * NE], laterT[:, n % 2, :], to[:, :],
                          start=True, stop=True).then_inc(sent, 1)

        @block.vector
        def _(dve):
            own = Chain(dve, v_own, 5)
            dve.wait_ge(x_in_s, 16)
            with dve.Fori(0, B) as b:
                own.turn(b)
                ln.vector(dve, own, b, x[:, :, :].rearrange("p (b i) h -> p b i h", b=B)[:, b])
                own.end()

            def step(instruction):
                own.inc(instruction)
                own.wait()

            own.turn(B)
            dve.wait_ge(logits_moved, 1)
            step(dve.tensor_reduce(top[:, :], prob[:, :, :], AX.X, ALU.max))

            def bc(t, shape):
                return t.rearrange("p (n o) -> p n o", o=1).to_broadcast(shape)

            dve.tensor_tensor(prob[:, :, :], prob[:, :, :], bc(top[:, :], [P, NT, NE]), ALU.subtract).then_inc(shifted, 1)
            dve.wait_ge(exps, 1)
            step(dve.tensor_reduce(total[:, :], prob[:, :, :], AX.X, ALU.add))
            step(dve.reciprocal(total[:, :], total[:, :]))
            step(dve.tensor_tensor(prob[:, :, :], prob[:, :, :], bc(total[:, :], [P, NT, NE]), ALU.mult))
            for n in range(NT):
                own.inc(dve.max(best[:, n, :], prob[:, n, :]))
            own.wait()
            for n in range(NT):
                own.inc(dve.max_index(index[:, n, :], best[:, n, :], prob[:, n, :]))
            own.wait()
            step(dve.tensor_copy(indexf[:, :, :], index[:, :, :]))
            step(dve.tensor_reduce(total[:, :], best[:, :, :], AX.X, ALU.add))
            step(dve.tensor_scalar(total[:, :], total[:, :], 1e-12, None, ALU.max))
            step(dve.reciprocal(total[:, :], total[:, :]))
            step(dve.tensor_tensor(best[:, :, :], best[:, :, :], bc(total[:, :], [P, NT, TOP]), ALU.mult))
            for b in range(B):
                of = slice(TT * b, TT * b + TT)
                for i in range(TT):
                    own.inc(dve.tensor_tensor(hot[:, i, :, :], bc(indexf[:, TT * b + i, :], [P, TOP, NE]),
                                              count[:, :].rearrange("p (o e) -> p o e", o=1).to_broadcast([P, TOP, NE]),
                                              ALU.is_equal))
                own.wait()
                for s in range(2):
                    for i in range(TT):
                        own.inc(dve.tensor_reduce(chosen[:, s, TT * b + i, :],
                                                  hot[:, i, s * SEL:(s + 1) * SEL, :].rearrange("p r e -> p e r"),
                                                  AX.X, ALU.add))
                own.wait()
                for i in range(TT):
                    own.inc(dve.tensor_tensor(hot[:, i, :, :], hot[:, i, :, :],
                                              bc(best[:, TT * b + i, :], [P, TOP, NE]), ALU.mult))
                own.wait()
                for s, dst in ((0, weight), (1, later)):
                    for i in range(TT):
                        last = dve.tensor_reduce(dst[:, TT * b + i, :],
                                                 hot[:, i, s * SEL:(s + 1) * SEL, :].rearrange("p r e -> p e r"),
                                                 AX.X, ALU.add)
                        if s == 0 or i < TT - 1:
                            own.inc(last)
                last.then_inc(chosen_ready, 1)
                dve.wait_ge(chosen_ready, b + 1)

            eye = ident[0:NE, 0:NE]
            step(dve.tensor_tensor(cand[:, :], sim[:, :], eye, ALU.mult))
            step(dve.tensor_tensor(sim[:, :], sim[:, :], cand[:, :], ALU.subtract))
            step(dve.tensor_tensor(sim[:, :], sim[:, :], eye, ALU.add))
            dve.wait_ge(counts, 1)
            step(dve.tensor_scalar(primary[:, :], ps[0:NE, 4, 0:NE], 0.5, None, ALU.is_ge))
            step(dve.tensor_tensor(cand[:, :], sim[:, :], primary[:, :], ALU.mult))
            step(dve.tensor_scalar(primary[:, :], primary[:, :], -NEG, NEG, ALU.mult, ALU.add))
            step(dve.tensor_tensor(cand[:, :], cand[:, :], primary[:, :], ALU.add))
            step(dve.max(cbest[:, :], cand[:, :]))
            step(dve.max_index(cindex[:, :], cbest[:, :], cand[:, :]))
            step(dve.tensor_copy(cindexf[:, :], cindex[:, :]))
            step(dve.tensor_scalar(moves[:, 0:1], ps[0:NE, 5, 0:1], 0.5, None, ALU.is_lt))
            step(dve.tensor_scalar(moves[:, 1:2], ps[0:NE, 5, 1:2], 0.5, None, ALU.is_ge))
            step(dve.tensor_scalar(moves[:, 2:3], cbest[:, 0:1], 0.5, None, ALU.is_ge))
            step(dve.tensor_tensor(moves[:, 0:1], moves[:, 0:1], moves[:, 1:2], ALU.mult))
            step(dve.tensor_tensor(moves[:, 0:1], moves[:, 0:1], moves[:, 2:3], ALU.mult))
            step(dve.tensor_scalar(to[:, :], count[0:NE, :], cindexf[:, 0:1], None, ALU.is_equal))
            step(dve.tensor_tensor(to[:, :], to[:, :], eye, ALU.subtract))
            step(dve.tensor_scalar(to[:, :], to[:, :], moves[:, 0:1], None, ALU.mult))
            dve.tensor_tensor(to[:, :], to[:, :], eye, ALU.add).then_inc(to_ready, 1)
            dve.wait_ge(sent, NT)
            dve.tensor_tensor(weight[:, :, :].rearrange("p n e -> p (n e)"),
                              ps[:, 6:8, :].rearrange("p a n -> p (a n)"),
                              weight[:, :, :].rearrange("p n e -> p (n e)"), ALU.add).then_inc(weight_ready, 1)
            dve.wait_ge(weight_ready, 1)


def experts(nc, ps, ident, ones, eps, x_in, x_out, dram):
    FH = FI // 2
    with ExitStack() as outer:
        keep = Stage(nc, outer, "ex")
        x = keep.sb("x", [P, NT, H])
        xT = keep.sb("xT", [P, B, HC, T])
        weight = keep.sb("weight", [P, NT, NE])
        route(nc, ps, ident, ones, eps, x_in, dram, x, xT, weight)
        with ExitStack() as ctx:
            st = Stage(nc, ctx, "ex")
            w_gu = [st.sb(f"w_gu{s}", [P, HC, 2 * FI]) for s in range(2)]
            w_d = [st.sb(f"w_d{s}", [FH, 2, H]) for s in range(2)]
            act_g = st.sb("act_g", [P, 2, FI])
            hid = st.sb("hid", [P, 2, FI])
            hidT = st.sb("hidT", [FH, 2, 2, P])
            w_in = [st.sem("w_in0"), st.sem("w_in1")]
            gu, silu, hid_ready = st.sem("gu"), st.sem("silu"), st.sem("hid_ready")
            turned, moved, o_ready, added = (st.sem(n) for n in ("turned", "moved", "o_ready", "added"))
            x_out_s = st.sem("x_out")
            block = ctx.enter_context(nc.Block())
            NU = 2 * NT

            @block.sync
            def _(sp):
                with sp.Fori(0, NE // 2) as r:
                    for s in range(2):
                        sp.wait_ge(o_ready, NU * r if s == 0 else NU * r)
                        sp.dma_start(w_gu[s][:, :, :], dram["guT"].rearrange("(r s) (c p) n -> r s p c n", p=P, s=2)
                                     [r, s]).then_inc(w_in[s], 16)
                        sp.dma_start(w_d[s][:, :, :], dram["downT"].rearrange("(r s) (c p) n -> r s p c n", p=FH, s=2)
                                     [r, s]).then_inc(w_in[s], 16)
                sp.wait_ge(added, NU * (NE // 2))
                sp.dma_start(x_out.rearrange("(n p) h -> p n h", p=P), x[:, :, :]).then_inc(x_out_s, 16)
                sp.wait_ge(x_out_s, 16)

            @block.scalar
            def _(act):
                with act.Fori(0, NE // 2) as r:
                    def move(k):
                        act.wait_ge(turned, NU * r + k + 1)
                        act.wait_ge(o_ready, NU * r + max(k - 1, 0))
                        act.activation(hidT[:, k % 2, :, :], ps[0:FH, 4 + k % 2, 0:2 * P], ACT.Copy).then_inc(moved, 1)

                    for k in range(NU):
                        act.wait_ge(gu, NU * r + k + 1)
                        act.wait_ge(hid_ready, NU * r + max(k - 1, 0))
                        act.activation(act_g[:, k % 2, :], ps[:, k % 4, 0:FI], ACT.Silu).then_inc(silu, 1)
                        if k:
                            move(k - 1)
                    move(NU - 1)

            @block.tensor
            def _(pe):
                with pe.Fori(0, NE // 2) as r:
                    def turn(k):
                        pe.wait_ge(hid_ready, NU * r + k + 1)
                        pe.wait_ge(moved, NU * r + max(k - 1, 0))
                        for a in range(2):
                            last = pe.transpose(ps[0:FH, 4 + k % 2, a * P:(a + 1) * P], hid[:, k % 2, a * FH:(a + 1) * FH], ident)
                        last.then_inc(turned, 1)

                    def down(k):
                        pe.wait_ge(moved, NU * r + k + 1)
                        pe.wait_ge(added, NU * r + max(k - 1, 0))
                        for a in range(2):
                            last = pe.matmul(ps[:, 6 + k % 2, :], hidT[:, k % 2, a, :], w_d[k // NT][:, a, :],
                                             start=(a == 0), stop=(a == 1))
                        last.then_inc(o_ready, 1)

                    for k in range(NU):
                        n = k % NT
                        if n == 0:
                            pe.wait_ge(w_in[k // NT], 32 * r + 32)
                        pe.wait_ge(hid_ready, NU * r + max(k - 3, 0))
                        for c in range(HC):
                            last = pe.matmul(ps[:, k % 4, 0:2 * FI], xT[:, n // TT, c, n % TT * P:(n % TT + 1) * P],
                                             w_gu[k // NT][:, c, :], start=(c == 0), stop=(c == HC - 1))
                        last.then_inc(gu, 1)
                        if k:
                            turn(k - 1)
                        if k >= 2:
                            down(k - 2)
                    turn(NU - 1)
                    down(NU - 2)
                    down(NU - 1)

            @block.vector
            def _(dve):
                by_turn = weight[:, :, :].rearrange("p n (r s) -> p n r s", s=2)
                with dve.Fori(0, NE // 2) as r:
                    def add(k):
                        dve.wait_ge(o_ready, NU * r + k + 1)
                        dve.tensor_tensor(x[:, k % NT, :], ps[:, 6 + k % 2, :], x[:, k % NT, :], ALU.add).then_inc(added, 1)

                    for k in range(NU):
                        dve.wait_ge(silu, NU * r + k + 1)
                        dve.wait_ge(turned, NU * r + max(k - 1, 0))
                        dve.scalar_tensor_tensor(hid[:, k % 2, :], ps[:, k % 4, FI:2 * FI],
                                                 by_turn[:, k % NT, r, k // NT:k // NT + 1], act_g[:, k % 2, :],
                                                 ALU.mult, ALU.mult).then_inc(hid_ready, 1)
                        if k >= 2:
                            add(k - 2)
                    add(NU - 2)
                    add(NU - 1)


STAGES = "ABCDEF"


def columns_of(*vectors):
    return np.ascontiguousarray(np.concatenate([np.asarray(v).reshape(-1, P).T for v in vectors], axis=1))


def build(nc, dram, out):
    res = nc.dram_tensor("residual", (B * T, H), F32, kind="Internal").ap()
    with ExitStack() as ctx:
        ps = ctx.enter_context(nc.psum_tensor("ps", [P, 8, 512], F32))
        ident_t = ctx.enter_context(nc.sbuf_tensor("ident", [P, P], F32))
        ones_t = ctx.enter_context(nc.sbuf_tensor("ones", [P, P], F32))
        identb_t = ctx.enter_context(nc.sbuf_tensor("identb", [P, P], BF16))
        eps_t = ctx.enter_context(nc.sbuf_tensor("eps", [P, 2], F32))
        const_in = ctx.enter_context(nc.semaphore("const_in"))
        const_set = ctx.enter_context(nc.semaphore("const_set"))
        with nc.Block() as block:
            @block.sync
            def _(sp):
                sp.dma_start(ident_t[:, :], dram["identity"]).then_inc(const_in, 16)
                sp.wait_ge(const_in, 16)

            @block.vector
            def _(dve):
                dve.memset(ones_t[:, :], 1.0)
                dve.memset(eps_t[:, 0:1], 1e-5)
                dve.memset(eps_t[:, 1:2], 1e-6)
                dve.wait_ge(const_in, 16)
                dve.tensor_copy(identb_t[:, :], ident_t[:, :]).then_inc(const_set, 1)
                dve.wait_ge(const_set, 1)
        ident, identb, ones = ident_t[:, :], identb_t[:, :], ones_t[:, :]
        eps, eps6 = eps_t[:, 0:1], eps_t[:, 1:2]
        at = dram["x"]
        for s in STAGES:
            to = out if s == STAGES[-1] else res
            if s == "A":
                time_mix(nc, ps, ident, eps, at, to, dram["tm_cols"],
                         {"r": dram["Wr"], "k": dram["Wk"], "v": dram["Wv"], "o": dram["Wo"]})
            elif s == "B":
                memory_attention(nc, ps, ident, eps, at, to, dram["ctx"], dram["ctxT"], dram["mask"])
            elif s == "C":
                ternary_ffn(nc, ps, ident, identb, ones, eps, at, to, dram)
            elif s == "D":
                mamba(nc, ps, ident, eps, at, to, dram)
            elif s == "E":
                context_attention(nc, ps, ident, identb, eps, eps6, at, to, dram)
            elif s == "F":
                experts(nc, ps, ident, ones, eps, at, to, dram)
            at = to


def laid_out(i):
    i = {k: np.asarray(v) for k, v in i.items()}
    d = {
        "x": i["x"].reshape(B * T, H),
        "identity": np.eye(P, dtype=np.float32),
    }
    if "A" in STAGES:
        d["tm_cols"] = columns_of(*(i[f"L0_attn_{n}"] for n in (
            "ln_scale", "ln_bias", "mix_k", "mix_v", "mix_r", "time_first", "time_decay")))
        for n in "rkvo":
            d[f"W{n}"] = i[f"L0_attn_W{n}"]
    if "B" in STAGES or "E" in STAGES:
        d["ctx"] = i["ctx_2048"]
        d["ctxT"] = i["ctx_2048"].transpose(0, 2, 1)
        d["mask"] = i["mask_BxS2_bk0"]
    if "C" in STAGES:
        d |= ffn_inputs(i)
    if "D" in STAGES:
        d |= mamba_inputs(i)
    if "E" in STAGES:
        d |= attention_inputs(i)
    if "F" in STAGES:
        d |= expert_inputs(i)
    return {k: np.ascontiguousarray(v) for k, v in d.items()}


def kernel(**inputs):
    import concourse.bacc as bacc
    from concourse.bass_utils import run_bass_kernel_spmd

    nc = bacc.Bacc("TRN2", target_bir_lowering=False, num_devices=1)
    arrays = laid_out(inputs)
    dram = {n: nc.dram_tensor(f"in_{n}", a.shape, mybir.dt.from_np(a.dtype), kind="ExternalInput").ap()
            for n, a in arrays.items()}
    out = nc.dram_tensor("out", (B * T, H), F32, kind="ExternalOutput").ap()
    build(nc, dram, out)
    r = run_bass_kernel_spmd(nc, [{f"in_{n}": a for n, a in arrays.items()}], core_ids=[0])
    return r.results[0]["out"].reshape(B, T, H)
```

```python
from contextlib import ExitStack

import concourse.bass as bass
import numpy as np
from concourse import mybir

ALU = mybir.AluOpType
ACT = mybir.ActivationFunctionType
AX = mybir.AxisListType
F32 = mybir.dt.float32
BF16 = mybir.dt.bfloat16
U8 = mybir.dt.uint8
U32 = mybir.dt.uint32
I32 = mybir.dt.int32

P = 128
B, T, H = 4, 512, 512
HC = H // P
TT = T // P
NEG = -1e30
ROUND = 1.5 * 2.0**23


class Chain:

    def __init__(self, eng, sem, per=0):
        self.eng, self.sem, self.per, self.base, self.n, self.start = eng, sem, per, 0, 0, None

    def turn(self, i):
        if self.start is None:
            self.start = self.n
        self.base, self.n = self.start + i * self.per, 0

    def inc(self, instruction):
        instruction.then_inc(self.sem, 1)
        self.n += 1

    def wait(self):
        self.eng.wait_ge(self.sem, self.base + self.n)

    def end(self):
        assert self.n == self.per, f"{self.sem}: {self.n} marks in a turn, not {self.per}"


class Stage:

    def __init__(self, nc, ctx, name, sems=None):
        self.nc, self.ctx, self.name, self.sems = nc, ctx, name, sems
        if sems is None:
            self.sems = []
            ctx.callback(self.clear)

    def clear(self):
        if self.sems:
            self.nc.clear_and_free_semaphores(self.sems)
            self.nc.all_engine_barrier()

    def sb(self, name, shape, dt=F32):
        return self.ctx.enter_context(self.nc.sbuf_tensor(f"{self.name}_{name}", shape, dt))

    def sem(self, name):
        self.sems.append(self.nc.alloc_semaphore(f"{self.name}_{name}"))
        return self.sems[-1]


class Columns:

    def __init__(self, st, ps, ident, eps_col, xT, pad=0):
        st = Stage(st.nc, st.ctx, st.name + "_ln", st.sems)
        self.pause = st.sb("pause", [P, 1])
        self.ps, self.ident, self.eps_col, self.xT, self.pad = ps, ident, eps_col, xT, pad
        self.xn = st.sb("xn", [P, TT, H])
        self.stats = st.sb("stats", [P, TT, 6])
        self.mv = st.sb("mv", [P, TT, 2])
        self.sd = st.sb("sd", [P, TT])
        self.rstd = st.sb("rstd", [P, TT])
        self.var_ready = st.sem("var_ready")
        self.sd_ready = st.sem("sd_ready")
        self.xn_ready = st.sem("xn_ready")
        self.turned = st.sem("turned")
        self.xT_ready = st.sem("xT_ready")

    def statistics(self, dve, chain, rows):
        for i in range(TT):
            chain.inc(dve.bn_stats(self.stats[:, i, :], rows[:, i, :]))
        chain.wait()
        dve.memset(self.pause[:, :], 0.0)
        for i in range(TT):
            last = dve.bn_aggr(self.mv[:, i, :], self.stats[:, i, :])
        return last

    def normalise(self, dve, chain, rows, out):
        chain.inc(dve.reciprocal(self.rstd[:, :], self.sd[:, :]))
        chain.wait()
        for i in range(TT):
            last = dve.tensor_scalar(out[:, i, :], rows[:, i, :], self.mv[:, i, 0:1],
                                     self.rstd[:, i:i + 1], ALU.subtract, ALU.mult)
        return last

    def vector(self, dve, chain, b, rows):
        self.statistics(dve, chain, rows).then_inc(self.var_ready, 1)
        dve.wait_ge(self.sd_ready, b + 1)
        dve.wait_ge(self.turned, HC * b)
        self.normalise(dve, chain, rows, self.xn).then_inc(self.xn_ready, 1)

    def scalar_sd(self, act, n):
        act.wait_ge(self.var_ready, n + 1)
        act.activation(self.sd[:, :], self.mv[:, :, 1], ACT.Sqrt, bias=self.eps_col).then_inc(self.sd_ready, 1)

    def scalar_move(self, act, b, scale=None, bias=None):
        for c in range(HC):
            act.wait_ge(self.turned, HC * b + c + 1)
            args = {} if scale is None else {"scale": scale[:, c:c + 1], "bias": bias[:, c:c + 1]}
            act.activation(self.xT[:, c, self.pad:self.pad + T], self.ps[:, c % 2, :], ACT.Identity,
                           **args).then_inc(self.xT_ready, 1)

    def tensor(self, pe, b):
        pe.wait_ge(self.xn_ready, b + 1)
        for c in range(HC):
            pe.wait_ge(self.xT_ready, HC * b + max(c - 1, 0))
            for i in range(TT):
                last = pe.transpose(self.ps[:, c % 2, i * P:(i + 1) * P],
                                    self.xn[:, i, c * P:(c + 1) * P], self.ident)
            last.then_inc(self.turned, 1)


def rows_of(x, b):
    return x.rearrange("(b i p) h -> b p i h", b=B, p=P)[b]


def time_mix(nc, ps, ident, eps, x_in, x_out, cols, weights, load_extra=None):
    n_cols = cols.shape[1]
    with ExitStack() as ctx:
        st = Stage(nc, ctx, "tm")
        x = st.sb("x", [P, TT, H])
        xl = st.sb("xl", [P, TT, H])
        xT = st.sb("xT", [P, HC, 1 + T])
        step = st.sb("step", [P, HC, T])
        mixed = [st.sb(f"mixed_{n}", [P, HC, T]) for n in "rkv"]
        w = {n: st.sb(f"w{n}", [P, HC, H]) for n in "rkvo"}
        col = st.sb("col", [P, n_cols])
        decay = st.sb("decay", [P, HC])
        r = st.sb("r", [P, HC, T])
        kk = st.sb("kk", [P, 2, T])
        vv = st.sb("vv", [P, 2, T])
        peak = st.sb("peak", [P, 2, 1 + T])
        q = st.sb("q", [P, T])
        ex = st.sb("ex", [P, 2, 4, T])
        cv = st.sb("cv", [P, T])
        sa = st.sb("sa", [P, 1 + T])
        sb_ = st.sb("sbb", [P, 1 + T])
        t1 = st.sb("t1", [P, T])
        t2 = st.sb("t2", [P, T])
        rw = st.sb("rw", [P, HC, T])
        ln = Columns(st, ps, ident, eps, xT, pad=1)
        scale, bias, mix_k, mix_v, mix_r, first, dec = (col[:, HC * j:HC * (j + 1)] for j in range(7))

        weights_in, x_in_s, x_out_s = st.sem("weights_in"), st.sem("x_in"), st.sem("x_out")
        xl_added = st.sem("xl_added")
        decay_e = st.sem("decay_e")
        mixed_ready = st.sem("mixed_ready")
        proj = st.sem("proj")
        moved = st.sem("moved")
        diffs = st.sem("diffs")
        exps = st.sem("exps")
        rw_ready = st.sem("rw_ready")
        o_ready = st.sem("o_ready")
        added = st.sem("added")
        xl_ready = st.sem("xl_ready")
        v_own = st.sem("v_own")
        block = ctx.enter_context(nc.Block())
        order = [("r", d) for d in range(HC)] + [(n, d) for d in range(HC) for n in "kv"]
        NP = len(order)

        @block.sync
        def _(sp):
            sp.dma_start(col[:, :], cols).then_inc(weights_in, 16)
            for n in "rkvo":
                sp.dma_start(w[n][:, :, :], weights[n].rearrange("(c p) d -> p c d", p=P)).then_inc(weights_in, 16)
            with sp.Fori(0, B) as b:
                sp.wait_ge(x_out_s, 16 * b)
                sp.dma_start(x[:, :, :], rows_of(x_in, b)).then_inc(x_in_s, 16)
                sp.wait_ge(added, TT * b + TT)
                sp.dma_start(rows_of(x_out, b), x[:, :, :]).then_inc(x_out_s, 16)
            sp.wait_ge(x_out_s, 16 * B)

        @block.gpsimd
        def _(pool):
            with pool.Fori(0, B) as b:
                pool.wait_ge(xl_ready, b + 1)
                for i in range(TT):
                    pool.tensor_tensor(x[:, i, :], x[:, i, :], xl[:, i, :], ALU.add).then_inc(xl_added, 1)

        @block.scalar
        def _(act):
            act.wait_ge(weights_in, 16 * 5)
            act.activation(decay[:, :], dec, ACT.Exp).then_inc(decay_e, 1)
            with act.Fori(0, B) as b:
                ln.scalar_sd(act, 2 * b)
                ln.scalar_sd(act, 2 * b + 1)
                ln.scalar_move(act, b, scale, bias)
                for j, (n, d) in enumerate(order):
                    act.wait_ge(proj, NP * b + j + 1)
                    bank = ps[:, 2 + j % 6, :]
                    if n == "r":
                        if d == 0:
                            act.wait_ge(rw_ready, HC * b)
                        act.activation(r[:, d, :], bank, ACT.Sigmoid).then_inc(moved, 1)
                        continue
                    if n == "k" and d >= 2:
                        act.wait_ge(rw_ready, HC * b + d - 1)
                    act.activation((kk if n == "k" else vv)[:, d % 2, :], bank, ACT.Identity).then_inc(moved, 1)
                    if n == "v":
                        act.wait_ge(diffs, HC * b + d + 1)
                        act.activation(ex[:, d % 2, :, :], ex[:, d % 2, :, :], ACT.Exp).then_inc(exps, 1)

        @block.tensor
        def _(pe):
            pe.wait_ge(weights_in, 16 * 5)
            with pe.Fori(0, B) as b:
                pe.wait_ge(added, TT * b)
                ln.tensor(pe, b)
                for j, (n, d) in enumerate(order):
                    pe.wait_ge(moved, NP * b + max(j - 5, 0))
                    pe.wait_ge(mixed_ready, 3 * b + 1 + "rkv".index(n))
                    for c in range(HC):
                        last = pe.matmul(ps[:, 2 + j % 6, :], w[n][:, c, d * P:(d + 1) * P],
                                         mixed["rkv".index(n)][:, c, :], start=(c == 0), stop=(c == HC - 1))
                    last.then_inc(proj, 1)
                pe.wait_ge(rw_ready, HC * b + HC)
                for i in range(TT):
                    pe.wait_ge(added, TT * b + max(i - 1, 0))
                    for c in range(HC):
                        last = pe.matmul(ps[:, i % 2, :], rw[:, c, i * P:(i + 1) * P], w["o"][:, c, :],
                                         start=(c == 0), stop=(c == HC - 1))
                    last.then_inc(o_ready, 1)

        @block.vector
        def _(dve):
            own = Chain(dve, v_own, 67)
            dve.memset(xT[:, :, 0:1], 0.0)
            dve.memset(peak[:, :, 0:1], 1.0 - 1e30)
            dve.memset(sa[:, 0:1], 0.0)
            dve.memset(sb_[:, 0:1], 0.0)
            dve.wait_ge(decay_e, 1)
            own.inc(dve.tensor_scalar(decay[:, :], decay[:, :], -1.0, None, ALU.mult))

            def exponents(b, d):
                dve.wait_ge(moved, NP * b + HC + 2 * d + 2)
                k, pk, e = kk[:, d % 2, :], peak[:, d % 2, :], ex[:, d % 2, :, :]
                own.inc(dve.tensor_tensor_scan(pk[:, 1:], decay[:, d:d + 1].to_broadcast([P, T]), k,
                                               1.0 - 1e30, ALU.add, ALU.max))
                own.wait()
                own.inc(dve.scalar_tensor_tensor(q[:, :], k, first[:, d:d + 1], pk[:, 0:T], ALU.add, ALU.max))
                dve.scalar_tensor_tensor(e[:, 2, :], pk[:, 0:T], decay[:, d:d + 1], pk[:, 1:], ALU.add, ALU.subtract)
                dve.tensor_tensor(e[:, 3, :], k, pk[:, 1:], ALU.subtract)
                own.wait()
                dve.tensor_tensor(e[:, 0, :], pk[:, 0:T], q[:, :], ALU.subtract)
                dve.scalar_tensor_tensor(e[:, 1, :], k, first[:, d:d + 1], q[:, :],
                                         ALU.add, ALU.subtract).then_inc(diffs, 1)

            def weighted(b, d):
                dve.wait_ge(exps, HC * b + d + 1)
                v, e = vv[:, d % 2, :], ex[:, d % 2, :, :]
                own.inc(dve.tensor_tensor(cv[:, :], e[:, 3, :], v, ALU.mult))
                own.inc(dve.tensor_tensor_scan(sb_[:, 1:], e[:, 2, :], e[:, 3, :], 0.0, ALU.mult, ALU.add))
                own.wait()
                own.inc(dve.tensor_tensor_scan(sa[:, 1:], e[:, 2, :], cv[:, :], 0.0, ALU.mult, ALU.add))
                own.inc(dve.tensor_tensor(t2[:, :], e[:, 0, :], sb_[:, 0:T], ALU.mult))
                own.wait()
                own.inc(dve.tensor_tensor(t1[:, :], e[:, 0, :], sa[:, 0:T], ALU.mult))
                own.inc(dve.tensor_tensor(cv[:, :], e[:, 1, :], v, ALU.mult))
                own.wait()
                own.inc(dve.tensor_tensor(t2[:, :], t2[:, :], e[:, 1, :], ALU.add))
                own.inc(dve.tensor_tensor(t1[:, :], t1[:, :], cv[:, :], ALU.add))
                own.wait()
                own.inc(dve.scalar_tensor_tensor(q[:, :], t2[:, :], 0.0, t2[:, :], ALU.is_equal, ALU.add))
                own.wait()
                own.inc(dve.reciprocal(q[:, :], q[:, :]))
                own.inc(dve.scalar_tensor_tensor(t1[:, :], t2[:, :], 0.0, t1[:, :], ALU.not_equal, ALU.mult))
                own.wait()
                own.inc(dve.tensor_tensor(t1[:, :], t1[:, :], q[:, :], ALU.mult))
                own.wait()
                if d == 0:
                    dve.wait_ge(o_ready, TT * b)
                dve.tensor_tensor(rw[:, d, :], t1[:, :], r[:, d, :], ALU.mult).then_inc(rw_ready, 1)

            with dve.Fori(0, B) as b:
                own.turn(b)
                dve.wait_ge(x_in_s, 16 * b + 16)
                ln.statistics(dve, own, x).then_inc(ln.var_ready, 1)
                dve.wait_ge(ln.sd_ready, 2 * b + 1)
                dve.wait_ge(xl_added, TT * b)
                ln.normalise(dve, own, x, xl).then_inc(xl_ready, 1)
                dve.wait_ge(xl_ready, b + 1)
                ln.statistics(dve, own, xl).then_inc(ln.var_ready, 1)
                dve.wait_ge(ln.sd_ready, 2 * b + 2)
                dve.wait_ge(ln.turned, HC * b)
                ln.normalise(dve, own, xl, ln.xn).then_inc(ln.xn_ready, 1)
                dve.wait_ge(ln.xT_ready, HC * b + HC)
                own.inc(dve.tensor_tensor(step[:, :, :], xT[:, :, 1:], xT[:, :, 0:T], ALU.subtract))
                own.wait()
                for n, mix in enumerate((mix_r, mix_k, mix_v)):
                    for c in range(HC):
                        last = dve.scalar_tensor_tensor(mixed[n][:, c, :], step[:, c, :], mix[:, c:c + 1],
                                                        xT[:, c, 0:T], ALU.mult, ALU.add)
                    last.then_inc(mixed_ready, 1)
                exponents(b, 0)
                exponents(b, 1)
                for d in range(HC):
                    weighted(b, d)
                    if d + 2 < HC:
                        exponents(b, d + 2)
                dve.wait_ge(xl_added, TT * b + TT)
                for i in range(TT):
                    dve.wait_ge(o_ready, TT * b + i + 1)
                    dve.tensor_tensor(x[:, i, :], ps[:, i % 2, :], x[:, i, :], ALU.add).then_inc(added, 1)
                own.end()


def memory_attention(nc, ps, ident, eps, x_in, x_out, mem, memT, mask):
    MC = T // P
    SCALE = float(H) ** -0.5
    with ExitStack() as ctx:
        st = Stage(nc, ctx, "ma")
        x = st.sb("x", [P, TT, H])
        xT = st.sb("xT", [P, HC, T])
        memory = st.sb("memory", [P, MC, H])
        memoryT = st.sb("memoryT", [P, HC, T])
        mask8 = st.sb("mask8", [P, T], U8)
        maskf = st.sb("maskf", [P, T])
        neg = st.sb("neg", [P, T])
        valid = st.sb("valid", [P, 1])
        one_row = st.sb("one_row", [1, P])
        prob = st.sb("prob", [P, 2, T])
        probT = st.sb("probT", [P, 2, MC, P])
        top = st.sb("top", [P, TT])
        ntop = st.sb("ntop", [P, TT])
        total = st.sb("total", [P, TT])
        inv = st.sb("inv", [P, TT])
        ln = Columns(st, ps, ident, eps, xT)
        x_in_s, x_out_s, mem_in = st.sem("x_in"), st.sem("x_out"), st.sem("mem_in")
        set_up = st.sem("set_up")
        neg_ready = st.sem("neg_ready")
        scores = st.sem("scores")
        tops = st.sem("tops")
        probs = st.sem("probs")
        pT_psum = st.sem("pT_psum")
        pT_ready = st.sem("pT_ready")
        o_ready = st.sem("o_ready")
        added = st.sem("added")
        v_own = st.sem("v_own")
        block = ctx.enter_context(nc.Block())

        @block.sync
        def _(sp):
            with sp.Fori(0, B) as b:
                sp.wait_ge(x_out_s, 16 * b)
                sp.dma_start(x[:, :, :], rows_of(x_in, b)).then_inc(x_in_s, 16)
                sp.wait_ge(added, TT * b)
                sp.dma_start(memoryT[:, :, :], memT.rearrange("b (c p) m -> b p c m", p=P)[b]).then_inc(mem_in, 16)
                sp.dma_start(memory[:, :, :], mem.rearrange("b (c p) d -> b p c d", p=P)[b]).then_inc(mem_in, 16)
                sp.dma_start(mask8[:, :], mask.rearrange("b (a m) -> b a m", a=1)[b].to_broadcast([P, T])).then_inc(mem_in, 16)
                sp.wait_ge(added, TT * b + TT)
                sp.dma_start(rows_of(x_out, b), x[:, :, :]).then_inc(x_out_s, 16)
            sp.wait_ge(x_out_s, 16 * B)

        @block.scalar
        def _(act):
            with act.Fori(0, B) as b:
                ln.scalar_sd(act, b)
                ln.scalar_move(act, b)
                for i in range(TT):
                    act.wait_ge(tops, TT * b + i + 1)
                    act.wait_ge(pT_psum, TT * b + max(i - 1, 0))
                    act.activation(prob[:, i % 2, :], ps[:, 2 + i % 2, :], ACT.Exp, bias=ntop[:, i:i + 1],
                                   scale=SCALE, accum_out=total[:, i:i + 1]).then_inc(probs, 1)
                    act.wait_ge(pT_psum, TT * b + i + 1)
                    act.wait_ge(o_ready, TT * b + max(i - 1, 0))
                    act.activation(probT[:, i % 2, :, :], ps[:, 4 + i % 2, :], ACT.Identity).then_inc(pT_ready, 1)

        @block.tensor
        def _(pe):
            pe.wait_ge(set_up, 1)
            with pe.Fori(0, B) as b:
                pe.wait_ge(added, TT * b)
                ln.tensor(pe, b)
                pe.wait_ge(mem_in, 48 * b + 48)
                pe.wait_ge(neg_ready, b + 1)
                pe.wait_ge(ln.xT_ready, HC * b + HC)

                def score(i):
                    pe.wait_ge(probs, TT * b + max(i - 1, 0))
                    pe.matmul(ps[:, 2 + i % 2, :], one_row[:, :], neg[0:1, :], start=True, stop=False)
                    for c in range(HC):
                        last = pe.matmul(ps[:, 2 + i % 2, :], xT[:, c, i * P:(i + 1) * P], memoryT[:, c, :],
                                         start=False, stop=(c == HC - 1))
                    last.then_inc(scores, 1)

                score(0)
                for i in range(TT):
                    if i + 1 < TT:
                        score(i + 1)
                    pe.wait_ge(probs, TT * b + i + 1)
                    pe.wait_ge(pT_ready, TT * b + max(i - 1, 0))
                    for m in range(MC):
                        last = pe.transpose(ps[:, 4 + i % 2, m * P:(m + 1) * P],
                                            prob[:, i % 2, m * P:(m + 1) * P], ident)
                    last.then_inc(pT_psum, 1)
                    pe.wait_ge(pT_ready, TT * b + i + 1)
                    pe.wait_ge(added, TT * b + max(i - 1, 0))
                    for m in range(MC):
                        last = pe.matmul(ps[:, 6 + i % 2, :], probT[:, i % 2, m, :], memory[:, m, :],
                                         start=(m == 0), stop=(m == MC - 1))
                    last.then_inc(o_ready, 1)

        @block.vector
        def _(dve):
            own = Chain(dve, v_own, 19)
            dve.memset(one_row[:, :], 1.0).then_inc(set_up, 1)
            with dve.Fori(0, B) as b:
                own.turn(b)
                dve.wait_ge(x_in_s, 16 * b + 16)
                ln.vector(dve, own, b, x)
                dve.wait_ge(mem_in, 48 * b + 48)
                own.inc(dve.tensor_copy(maskf[:, :], mask8[:, :]))
                own.wait()
                dve.wait_ge(scores, TT * b)
                own.inc(dve.tensor_scalar(neg[:, :], maskf[:, :], -NEG, NEG, ALU.mult, ALU.add))
                dve.tensor_reduce(valid[:, :], maskf[:, :], AX.X, ALU.max).then_inc(neg_ready, 1)

                def finish(i):
                    dve.wait_ge(probs, TT * b + i + 1)
                    own.inc(dve.reciprocal(inv[:, i:i + 1], total[:, i:i + 1]))
                    own.wait()
                    own.inc(dve.tensor_scalar(inv[:, i:i + 1], inv[:, i:i + 1], valid[:, 0:1], None, ALU.mult))
                    own.wait()
                    dve.wait_ge(o_ready, TT * b + i + 1)
                    dve.scalar_tensor_tensor(x[:, i, :], ps[:, 6 + i % 2, :], inv[:, i:i + 1], x[:, i, :],
                                             ALU.mult, ALU.add).then_inc(added, 1)

                for i in range(TT):
                    dve.wait_ge(scores, TT * b + i + 1)
                    own.inc(dve.tensor_reduce(top[:, i:i + 1], ps[:, 2 + i % 2, :], AX.X, ALU.max))
                    own.wait()
                    dve.tensor_scalar(ntop[:, i:i + 1], top[:, i:i + 1], -SCALE, None, ALU.mult).then_inc(tops, 1)
                    if i:
                        finish(i - 1)
                finish(TT - 1)
                own.end()


F_IN = 2048
FC = F_IN // P


def ffn_inputs(i):
    return {
        "w1T": i["L0_ffn_w1"].T,
        "w2T": i["L0_ffn_w2"].T,
        "ffn_rows": np.stack([i["L0_ffn_b1"], i["L0_ffn_ln_g"], i["L0_ffn_ln_b"]]),
        "ffn_b2": i["L0_ffn_b2"].reshape(1, H),
    }


def ternary_ffn(nc, ps, ident, identb, ones, eps, x_in, x_out, dram):
    sizes = {"w1T": (HC, F_IN), "w2T": (FC, H)}
    with ExitStack() as outer:
        keep = Stage(nc, outer, "ff")
        tern = {n: keep.sb(f"tern_{n}", [P, *s], BF16) for n, s in sizes.items()}
        mean_w = keep.sb("mean_w", [P, 2])
        inv_w = keep.sb("inv_w", [P, 2])

        with ExitStack() as ctx:
            st = Stage(nc, ctx, "fq")
            w = {n: st.sb(n, [P, *s]) for n, s in sizes.items()}
            scrap = st.sb("scrap", [P, HC * F_IN], BF16)
            sums = st.sb("sums", [P, 2])
            w_in = [st.sem("w1_in"), st.sem("w2_in")]
            summed = st.sem("summed")
            total = st.sem("total")
            rounded = st.sem("rounded")
            done = st.sem("done")
            v_own = st.sem("v_own")
            block = ctx.enter_context(nc.Block())

            @block.sync
            def _(sp):
                for k, n in enumerate(sizes):
                    sp.dma_start(w[n][:, :, :], dram[n].rearrange("(c p) o -> p c o", p=P)).then_inc(w_in[k], 16)

            @block.scalar
            def _(act):
                for k, n in enumerate(sizes):
                    act.wait_ge(w_in[k], 16)
                    if k:
                        act.wait_ge(summed, k)
                    act.activation(scrap[:, :], w[n][:, :, :].rearrange("p c o -> p (c o)"), ACT.Abs,
                                   accum_out=sums[:, k:k + 1]).then_inc(summed, 1)
                for k, n in enumerate(sizes):
                    act.wait_ge(rounded, k + 1)
                    act.activation(tern[n][:, :, :], w[n][:, :, :], ACT.Copy, bias=-ROUND).then_inc(done, 1)

            @block.tensor
            def _(pe):
                pe.wait_ge(summed, 2)
                pe.matmul(ps[:, 0, 0:2], ones, sums[:, :], start=True, stop=True).then_inc(total, 1)

            @block.vector
            def _(dve):
                own = Chain(dve, v_own)
                dve.wait_ge(total, 1)
                own.inc(dve.tensor_scalar(mean_w[:, :], ps[:, 0, 0:2], 1.0 / (F_IN * H), 1e-5, ALU.mult, ALU.max))
                own.wait()
                own.inc(dve.reciprocal(inv_w[:, :], mean_w[:, :]))
                own.wait()
                for k, n in enumerate(sizes):
                    own.inc(dve.tensor_scalar(w[n][:, :, :], w[n][:, :, :], inv_w[:, k:k + 1], ROUND, ALU.mult, ALU.add))
                    own.wait()
                    dve.tensor_scalar(w[n][:, :, :], w[n][:, :, :], ROUND - 1.0, ROUND + 1.0,
                                      ALU.max, ALU.min).then_inc(rounded, 1)

        with ExitStack() as ctx:
            st = Stage(nc, ctx, "ff")
            x = st.sb("x", [P, TT, H])
            rows = st.sb("rows", [P, 3, F_IN])
            b2 = st.sb("b2", [P, H])
            h = st.sb("h", [P, TT, F_IN])
            scrap = st.sb("scrap", [P, F_IN], BF16)
            q1 = st.sb("q1", [P, TT, H], BF16)
            q1T = st.sb("q1T", [P, HC, T], BF16)
            q2 = st.sb("q2", [P, 2, F_IN], BF16)
            q2T = st.sb("q2T", [P, 2, FC, P], BF16)
            stats = st.sb("stats", [P, TT, F_IN // 512, 6])
            mv = st.sb("mv", [P, TT, 2])
            pause = st.sb("pause", [P, 1])
            sd, rstd, ss, rms, amax, step1, step2, f = (
                st.sb(n, [P, TT]) for n in ("sd", "rstd", "ss", "rms", "amax", "step1", "step2", "f"))
            c1, c2 = st.sb("c1", [P, TT]), st.sb("c2", [P, TT])
            ln = Columns(st, ps, ident, eps, None)
            x_in_s, x_out_s, rows_in = st.sem("x_in"), st.sem("x_out"), st.sem("rows_in")
            b2_added = st.sem("b2_added")
            squares = st.sem("squares")
            rms_ready = st.sem("rms_ready")
            clipped = st.sem("clipped")
            q_ready = st.sem("q_ready")
            turned1, q1T_ready = st.sem("turned1"), st.sem("q1T_ready")
            turned2, q2T_ready = st.sem("turned2"), st.sem("q2T_ready")
            h_psum = st.sem("h_psum")
            h_raw = st.sem("h_raw")
            h_act = st.sem("h_act")
            sd2 = st.sem("sd2")
            h_norm = st.sem("h_norm")
            h_ln = st.sem("h_ln")
            silu_done = st.sem("silu_done")
            var2 = st.sem("var2")
            o_ready = st.sem("o_ready")
            added = st.sem("added")
            v_own, a_own, g_own = st.sem("v_own"), st.sem("a_own"), st.sem("g_own")
            block = ctx.enter_context(nc.Block())

            @block.sync
            def _(sp):
                sp.dma_start(rows[:, :, :], dram["ffn_rows"].rearrange("(a r) o -> a r o", a=1)
                             .to_broadcast([P, 3, F_IN])).then_inc(rows_in, 16)
                sp.dma_start(b2[:, :], dram["ffn_b2"].to_broadcast([P, H])).then_inc(rows_in, 16)
                with sp.Fori(0, B) as b:
                    sp.wait_ge(x_out_s, 16 * b)
                    sp.dma_start(x[:, :, :], rows_of(x_in, b)).then_inc(x_in_s, 16)
                    sp.wait_ge(added, TT * b + TT)
                    sp.dma_start(rows_of(x_out, b), x[:, :, :]).then_inc(x_out_s, 16)
                sp.wait_ge(x_out_s, 16 * B)

            @block.gpsimd
            def _(pool):
                own = Chain(pool, g_own, TT)
                pool.wait_ge(rows_in, 32)
                with pool.Fori(0, B) as b:
                    own.turn(b)
                    pool.wait_ge(ln.xn_ready, b + 1)
                    for i in range(TT):
                        pool.tensor_tensor(x[:, i, :], x[:, i, :], b2[:, :], ALU.add).then_inc(b2_added, 1)
                    for i in range(TT):
                        pool.wait_ge(h_norm, TT * b + i + 1)
                        own.inc(pool.tensor_tensor(h[:, i, :], h[:, i, :], rows[:, 1, :], ALU.mult))
                        own.wait()
                        pool.tensor_tensor(h[:, i, :], h[:, i, :], rows[:, 2, :], ALU.add).then_inc(h_ln, 1)
                    own.end()

            @block.scalar
            def _(act):
                with act.Fori(0, B) as b:
                    ln.scalar_sd(act, b)
                    act.wait_ge(ln.xn_ready, b + 1)
                    for i in range(TT):
                        act.wait_ge(squares, 2 * TT * b + i)
                        act.activation(scrap[:, 0:H], ln.xn[:, i, :], ACT.Square,
                                       accum_out=ss[:, i:i + 1]).then_inc(squares, 1)
                    act.wait_ge(squares, 2 * TT * b + TT)
                    act.activation(rms[:, :], ss[:, :], ACT.Sqrt, bias=eps, scale=1.0 / H).then_inc(rms_ready, 1)
                    for i in range(TT):
                        act.wait_ge(clipped, 2 * TT * b + i + 1)
                        act.wait_ge(turned1, 2 * b)
                        act.activation(q1[:, i, :], ln.xn[:, i, :], ACT.Copy, bias=-ROUND).then_inc(q_ready, 1)
                    for k in range(2):
                        act.wait_ge(turned1, 2 * b + k + 1)
                        act.activation(q1T[:, 2 * k:2 * k + 2, :], ps[:, 4 + k, :].bitcast(BF16),
                                       ACT.Copy).then_inc(q1T_ready, 1)
                    for i in range(TT):
                        act.wait_ge(h_raw, TT * b + i + 1)
                        act.activation(h[:, i, :], h[:, i, :], ACT.Silu).then_inc(silu_done, 1)
                    for i in range(TT):
                        act.wait_ge(silu_done, TT * b + i + 1)
                        act.activation(h[:, i, :], h[:, i, :], ACT.Gelu).then_inc(h_act, 1)
                    act.wait_ge(var2, b + 1)
                    act.activation(sd[:, :], mv[:, :, 1], ACT.Sqrt, bias=eps).then_inc(sd2, 1)
                    for i in range(TT):
                        act.wait_ge(h_ln, TT * b + i + 1)
                        act.wait_ge(squares, 2 * TT * b + TT + i)
                        act.activation(scrap[:, :], h[:, i, :], ACT.Square,
                                       accum_out=ss[:, i:i + 1]).then_inc(squares, 1)
                    act.wait_ge(squares, 2 * TT * b + 2 * TT)
                    act.activation(rms[:, :], ss[:, :], ACT.Sqrt, bias=eps, scale=1.0 / F_IN).then_inc(rms_ready, 1)
                    for i in range(TT):
                        act.wait_ge(clipped, 2 * TT * b + TT + i + 1)
                        act.wait_ge(turned2, 2 * TT * b + max(2 * (i - 1), 0))
                        act.activation(q2[:, i % 2, :], h[:, i, :], ACT.Copy, bias=-ROUND).then_inc(q_ready, 1)
                        for k in range(2):
                            act.wait_ge(turned2, 2 * TT * b + 2 * i + k + 1)
                            act.wait_ge(o_ready, TT * b + max(i - 1, 0))
                            act.activation(q2T[:, i % 2, 8 * k:8 * k + 8, :], ps[:, 4 + k, :].bitcast(BF16),
                                           ACT.Copy).then_inc(q2T_ready, 1)

            @block.tensor
            def _(pe):
                with pe.Fori(0, B) as b:
                    pe.wait_ge(q_ready, 2 * TT * b + TT)
                    pe.wait_ge(q2T_ready, 2 * TT * b)
                    for k in range(2):
                        for c in range(2 * k, 2 * k + 2):
                            for i in range(TT):
                                last = pe.transpose(
                                    ps[:, 4 + k, :].bitcast(BF16)[:, (c % 2 * TT + i) * P:(c % 2 * TT + i + 1) * P],
                                    q1[:, i, c * P:(c + 1) * P], identb)
                        last.then_inc(turned1, 1)
                    pe.wait_ge(q1T_ready, 2 * b + 2)
                    for i in range(TT):
                        pe.wait_ge(h_raw, TT * b + i)
                        for n in range(F_IN // 512):
                            for c in range(HC):
                                last = pe.matmul(ps[:, n, :], q1T[:, c, i * P:(i + 1) * P],
                                                 tern["w1T"][:, c, n * 512:(n + 1) * 512],
                                                 start=(c == 0), stop=(c == HC - 1))
                        last.then_inc(h_psum, 1)
                    for i in range(TT):
                        pe.wait_ge(q_ready, 2 * TT * b + TT + i + 1)
                        for k in range(2):
                            pe.wait_ge(q1T_ready, 2 * b + 2)
                            pe.wait_ge(q2T_ready, 2 * TT * b + max(2 * i + k - 1, 0))
                            for c in range(8):
                                last = pe.transpose(ps[:, 4 + k, :].bitcast(BF16)[:, c * P:(c + 1) * P],
                                                    q2[:, i % 2, (8 * k + c) * P:(8 * k + c + 1) * P], identb)
                            last.then_inc(turned2, 1)
                        pe.wait_ge(q2T_ready, 2 * TT * b + 2 * i + 2)
                        pe.wait_ge(added, TT * b + max(i - 1, 0))
                        for c in range(FC):
                            last = pe.matmul(ps[:, 6 + i % 2, :], q2T[:, i % 2, c, :], tern["w2T"][:, c, :],
                                             start=(c == 0), stop=(c == FC - 1))
                        last.then_inc(o_ready, 1)

            @block.vector
            def _(dve):
                own = Chain(dve, v_own, 50)
                dve.wait_ge(rows_in, 32)

                def steps(n, step, mean, c):
                    own.inc(dve.reciprocal(rms[:, :], rms[:, :]))
                    own.wait()
                    own.inc(dve.tensor_tensor(step[:, :], amax[:, :], rms[:, :], ALU.mult))
                    own.wait()
                    own.inc(dve.tensor_scalar(step[:, :], step[:, :], 1e-5, 1.0 / 127.0, ALU.max, ALU.mult))
                    own.wait()
                    own.inc(dve.reciprocal(f[:, :], step[:, :]))
                    own.inc(dve.tensor_scalar(c[:, :], step[:, :], mean, None, ALU.mult))
                    own.wait()
                    own.inc(dve.tensor_tensor(f[:, :], f[:, :], rms[:, :], ALU.mult))
                    own.wait()

                def to_grid(v, i):
                    own.inc(dve.tensor_scalar(v[:, i, :], v[:, i, :], f[:, i:i + 1], ROUND, ALU.mult, ALU.add))
                    own.wait()
                    dve.tensor_scalar(v[:, i, :], v[:, i, :], ROUND - 128.0, ROUND + 127.0,
                                      ALU.max, ALU.min).then_inc(clipped, 1)

                with dve.Fori(0, B) as b:
                    own.turn(b)
                    dve.wait_ge(x_in_s, 16 * b + 16)
                    ln.statistics(dve, own, x).then_inc(ln.var_ready, 1)
                    dve.wait_ge(ln.sd_ready, b + 1)
                    ln.normalise(dve, own, x, ln.xn).then_inc(ln.xn_ready, 1)
                    dve.wait_ge(ln.xn_ready, b + 1)
                    for i in range(TT):
                        own.inc(dve.tensor_reduce(amax[:, i:i + 1], ln.xn[:, i, :], AX.X, ALU.max,
                                                  apply_absolute_value=True))
                    dve.wait_ge(rms_ready, 2 * b + 1)
                    steps(1, step1, mean_w[:, 0:1], c1)
                    for i in range(TT):
                        to_grid(ln.xn, i)
                    for i in range(TT):
                        dve.wait_ge(h_psum, TT * b + i + 1)
                        dve.scalar_tensor_tensor(h[:, i, :], ps[:, 0:4, :].rearrange("p a n -> p (a n)"),
                                                 c1[:, i:i + 1], rows[:, 0, :], ALU.mult, ALU.add).then_inc(h_raw, 1)
                    for i in range(TT):
                        dve.wait_ge(h_act, TT * b + i + 1)
                        for n in range(F_IN // 512):
                            own.inc(dve.bn_stats(stats[:, i, n, :], h[:, i, n * 512:(n + 1) * 512]))
                    own.wait()
                    dve.memset(pause[:, :], 0.0)
                    for i in range(TT):
                        last = dve.bn_aggr(mv[:, i, :], stats[:, i, :, :].rearrange("p a s -> p (a s)"))
                    last.then_inc(var2, 1)
                    dve.wait_ge(sd2, b + 1)
                    own.inc(dve.reciprocal(rstd[:, :], sd[:, :]))
                    own.wait()
                    for i in range(TT):
                        dve.tensor_scalar(h[:, i, :], h[:, i, :], mv[:, i, 0:1], rstd[:, i:i + 1],
                                          ALU.subtract, ALU.mult).then_inc(h_norm, 1)
                    for i in range(TT):
                        dve.wait_ge(h_ln, TT * b + i + 1)
                        own.inc(dve.tensor_reduce(amax[:, i:i + 1], h[:, i, :], AX.X, ALU.max,
                                                  apply_absolute_value=True))
                    dve.wait_ge(rms_ready, 2 * b + 2)
                    steps(2, step2, mean_w[:, 1:2], c2)
                    for i in range(TT):
                        to_grid(h, i)
                    for i in range(TT):
                        dve.wait_ge(o_ready, TT * b + i + 1)
                        dve.wait_ge(b2_added, TT * b + TT)
                        dve.scalar_tensor_tensor(x[:, i, :], ps[:, 6 + i % 2, :], c2[:, i:i + 1], x[:, i, :],
                                                 ALU.mult, ALU.add).then_inc(added, 1)
                    own.end()


DI, NS, RK, KC = 1024, 16, 128, 4
DC = DI // P


def mamba_inputs(i):
    per_channel = np.concatenate(
        [i["L1_attn_Wconv"].reshape(DI, KC)] + [i[f"L1_attn_{n}"].reshape(DI, 1) for n in ("bconv", "D", "bdt")]
        + [i["L1_attn_A_log"]], axis=1)
    return {
        "mb_cols": per_channel.reshape(DC, P, KC + 3 + NS).transpose(1, 0, 2),
        "WinT": i["L1_attn_Win"].T,
        "WxT": i["L1_attn_Wx"].T,
        "WdtT": i["L1_attn_Wdt"].T,
        "WoutT": i["L1_attn_Wout"].T,
    }


def mamba(nc, ps, ident, eps, x_in, x_out, dram):
    with ExitStack() as ctx:
        st = Stage(nc, ctx, "mb")
        x = st.sb("x", [P, TT, H])
        xT = st.sb("xT", [P, HC, T])
        ln = Columns(st, ps, ident, eps, xT)
        w_in = st.sb("w_in", [P, HC, 2 * DI])
        w_x = st.sb("w_x", [P, DC, RK + 2 * NS])
        w_dt = st.sb("w_dt", [P, DI])
        w_out = st.sb("w_out", [P, DC, H])
        col = st.sb("col", [P, DC, KC + 3 + NS])
        taps, bconv, skip, bdt = col[:, :, 0:KC], col[:, :, KC], col[:, :, KC + 1], col[:, :, KC + 2]
        neg_a = st.sb("neg_a", [P, DC, NS])
        hs = st.sb("hs", [P, DC, T])
        gate = st.sb("gate", [P, DC, T])
        dt_in = st.sb("dt_in", [P, T])
        bc = st.sb("bc", [2 * NS, T])
        bcs = st.sb("bcs", [P, 2 * NS, T])
        soft = st.sb("soft", [P, T])
        dt = st.sb("dt", [P, 2, T])
        u = st.sb("u", [P, 2, T])
        db = (st.sb("db", [P, 4, T]), xT)
        hc = ln.xn
        weights_in, x_in_s, x_out_s = st.sem("weights_in"), st.sem("x_in"), st.sem("x_out")
        a_exp, a_ready = st.sem("a_exp"), st.sem("a_ready")
        hs_psum, conv_done, hs_ready = st.sem("hs_psum"), st.sem("conv_done"), st.sem("hs_ready")
        gate_psum, gate_ready = st.sem("gate_psum"), st.sem("gate_ready")
        ssm_psum = st.sem("ssm_psum")
        ssm_moved = st.sem("ssm_moved")
        dt_psum = st.sem("dt_psum")
        dt_abs = st.sem("dt_abs")
        dt_e = st.sem("dt_e")
        dt_log = st.sem("dt_log")
        dt_relu = st.sem("dt_relu")
        dt_ready = st.sem("dt_ready")
        u_ready = st.sem("u_ready")
        db_ready = st.sem("db_ready")
        da_ready = st.sem("da_ready")
        scanned = st.sem("scanned")
        hc_ready = st.sem("hc_ready")
        summed = st.sem("summed")
        y_read = st.sem("y_read")
        yg_ready = st.sem("yg_ready")
        o_ready, added, v_own = st.sem("o_ready"), st.sem("added"), st.sem("v_own")
        block = ctx.enter_context(nc.Block())
        NU = DC * NS
        NB = 2 + 2 * NS

        @block.sync
        def _(sp):
            sp.dma_start(col[:, :, :], dram["mb_cols"]).then_inc(weights_in, 16)
            sp.dma_start(w_in[:, :, :], dram["WinT"].rearrange("(c p) e -> p c e", p=P)).then_inc(weights_in, 16)
            sp.dma_start(w_x[:, :, :], dram["WxT"].rearrange("(c p) e -> p c e", p=P)).then_inc(weights_in, 16)
            sp.dma_start(w_dt[:, :], dram["WdtT"]).then_inc(weights_in, 16)
            sp.dma_start(w_out[:, :, :], dram["WoutT"].rearrange("(c p) e -> p c e", p=P)).then_inc(weights_in, 16)
            with sp.Fori(0, B) as b:
                sp.wait_ge(x_out_s, 16 * b)
                sp.dma_start(x[:, :, :], rows_of(x_in, b)).then_inc(x_in_s, 16)
                sp.wait_ge(added, TT * b + TT)
                sp.dma_start(rows_of(x_out, b), x[:, :, :]).then_inc(x_out_s, 16)
            sp.wait_ge(x_out_s, 16 * B)

        @block.gpsimd
        def _(pool):
            with pool.Fori(0, B) as b:
                pool.wait_ge(ssm_moved, NB * b + NB)
                for d in range(DC):
                    pool.wait_ge(u_ready, DC * b + d + 1)
                    for g in range(NS // 4):
                        k = 4 * d + g
                        pool.wait_ge(scanned, NU * b + max(4 * (k - 1), 0))
                        pool.tensor_tensor(db[k % 2][:, :, :],
                                           u[:, d % 2, :].rearrange("p (a t) -> p a t", a=1).to_broadcast([P, 4, T]),
                                           bcs[:, 4 * g:4 * g + 4, :], ALU.mult).then_inc(db_ready, 1)

        @block.scalar
        def _(act):
            act.wait_ge(weights_in, 80)
            act.activation(neg_a[:, :, :], col[:, :, KC + 3:], ACT.Exp).then_inc(a_exp, 1)

            def softplus_parts(b, d):
                act.wait_ge(dt_psum, DC * b + d + 1)
                act.wait_ge(dt_ready, DC * b + d)
                act.wait_ge(u_ready, DC * b + d)
                act.activation(dt[:, d % 2, :], ps[:, 7, :], ACT.Relu, bias=bdt[:, d:d + 1]).then_inc(dt_relu, 1)
                act.activation(soft[:, :], ps[:, 7, :], ACT.Abs, bias=bdt[:, d:d + 1]).then_inc(dt_abs, 1)
                act.wait_ge(dt_abs, DC * b + d + 1)
                act.activation(soft[:, :], soft[:, :], ACT.Exp, scale=-1.0).then_inc(dt_e, 1)
                act.wait_ge(dt_e, DC * b + d + 1)
                act.activation(soft[:, :], soft[:, :], ACT.Ln, bias=1.0).then_inc(dt_log, 1)

            with act.Fori(0, B) as b:
                ln.scalar_sd(act, b)
                act.wait_ge(hs_psum, DC * b)
                act.wait_ge(gate_psum, DC * b)
                act.wait_ge(scanned, NU * b)
                ln.scalar_move(act, b)
                for c in range(DC):
                    act.wait_ge(conv_done, DC * b + c + 1)
                    act.activation(hs[:, c, :], hs[:, c, :], ACT.Silu, bias=bconv[:, c:c + 1]).then_inc(hs_ready, 1)
                    act.wait_ge(gate_psum, DC * b + c + 1)
                    act.wait_ge(o_ready, TT * b)
                    act.activation(gate[:, c, :], ps[:, 5 + c % 3, :], ACT.Silu).then_inc(gate_ready, 1)
                act.wait_ge(hc_ready, NU * b)
                for k in range(NB):
                    act.wait_ge(ssm_psum, NB * b + k + 1)
                    bank = ps[:, 2 + k % 6, :]
                    src, dst = ((bank, dt_in[:, :]), (bank[0:2 * NS, :], bc[:, :]), (bank, bcs[:, max(k - 2, 0), :]))[min(k, 2)]
                    act.activation(dst, src, ACT.Copy).then_inc(ssm_moved, 1)
                softplus_parts(b, 0)
                for d in range(DC):
                    act.wait_ge(dt_ready, DC * b + d + 1)
                    for n in range(NS):
                        k = NS * d + n
                        act.wait_ge(scanned, NU * b + max(k - 1, 0))
                        act.activation(ps[:, 2 + k % 2, :], dt[:, d % 2, :], ACT.Exp,
                                       scale=neg_a[:, d, n:n + 1]).then_inc(da_ready, 1)
                        if n == 4 and d + 1 < DC:
                            softplus_parts(b, d + 1)

        @block.tensor
        def _(pe):
            pe.wait_ge(weights_in, 80)
            with pe.Fori(0, B) as b:
                pe.wait_ge(added, TT * b)
                ln.tensor(pe, b)
                pe.wait_ge(ln.xT_ready, HC * b + HC)
                for c in range(DC):
                    pe.wait_ge(conv_done, DC * b + max(c - 2, 0))
                    for h in range(HC):
                        last = pe.matmul(ps[:, 2 + c % 3, :], w_in[:, h, c * P:(c + 1) * P], xT[:, h, :],
                                         start=(h == 0), stop=(h == HC - 1))
                    last.then_inc(hs_psum, 1)
                    pe.wait_ge(gate_ready, DC * b + max(c - 2, 0))
                    for h in range(HC):
                        last = pe.matmul(ps[:, 5 + c % 3, :], w_in[:, h, DI + c * P:DI + (c + 1) * P], xT[:, h, :],
                                         start=(h == 0), stop=(h == HC - 1))
                    last.then_inc(gate_psum, 1)
                pe.wait_ge(hs_ready, DC * b + DC)
                pe.wait_ge(gate_ready, DC * b + DC)
                for k in range(NB):
                    pe.wait_ge(ssm_moved, NB * b + max(k - 5, 0))
                    bank = ps[:, 2 + k % 6, :]
                    if k < 2:
                        for c in range(DC):
                            last = pe.matmul((bank, bank[0:2 * NS, :])[k],
                                             (w_x[:, c, 0:RK], w_x[:, c, RK:])[k], hs[:, c, :],
                                             start=(c == 0), stop=(c == DC - 1))
                    else:
                        pe.wait_ge(ssm_moved, NB * b + 2)
                        last = pe.matmul(bank, ident[0:2 * NS, k - 2:k - 1].to_broadcast([2 * NS, P]), bc[:, :],
                                         start=True, stop=True)
                    last.then_inc(ssm_psum, 1)
                pe.wait_ge(ssm_moved, NB * b + NB)

                def dt_chunk(d):
                    pe.wait_ge(dt_abs, DC * b + d)
                    pe.wait_ge(dt_relu, DC * b + d)
                    pe.matmul(ps[:, 7, :], w_dt[:, d * P:(d + 1) * P], dt_in[:, :],
                              start=True, stop=True).then_inc(dt_psum, 1)

                dt_chunk(0)
                for d in range(DC):
                    pe.wait_ge(y_read, DC * b + max(d - 1, 0))
                    for n in range(NS):
                        if n == 2 and d + 1 < DC:
                            dt_chunk(d + 1)
                        k = NS * d + n
                        pe.wait_ge(hc_ready, NU * b + k + 1)
                        pe.matmul(ps[:, d % 2, :], ident, hc[:, k % 4, :],
                                  start=(n == 0), stop=(n == NS - 1)).then_inc(summed, 1)
                pe.wait_ge(yg_ready, DC * b + DC)
                for i in range(TT):
                    pe.wait_ge(added, TT * b + max(i - 1, 0))
                    for d in range(DC):
                        last = pe.matmul(ps[:, i % 2, :], gate[:, d, i * P:(i + 1) * P], w_out[:, d, :],
                                         start=(d == 0), stop=(d == DC - 1))
                    last.then_inc(o_ready, 1)

        @block.vector
        def _(dve):
            own = Chain(dve, v_own, 29)
            dve.wait_ge(a_exp, 1)
            dve.tensor_scalar(neg_a[:, :, :], neg_a[:, :, :], -1.0, None, ALU.mult).then_inc(a_ready, 1)

            def dt_chunk(b, d):
                dve.wait_ge(dt_log, DC * b + d + 1)
                dve.wait_ge(dt_relu, DC * b + d + 1)
                dve.tensor_tensor(dt[:, d % 2, :], dt[:, d % 2, :], soft[:, :], ALU.add).then_inc(dt_ready, 1)
                dve.wait_ge(dt_ready, DC * b + d + 1)
                dve.tensor_tensor(u[:, d % 2, :], dt[:, d % 2, :], hs[:, d, :], ALU.mult).then_inc(u_ready, 1)

            def scan(b, k):
                dve.wait_ge(da_ready, NU * b + k + 1)
                dve.wait_ge(db_ready, NU // 4 * b + k // 4 + 1)
                dve.wait_ge(hc_ready, NU * b + max(k - 2, 0))
                dve.tensor_tensor_scan(ps[:, 4 + k % 3, :], ps[:, 2 + k % 2, :], db[k // 4 % 2][:, k % 4, :], 0.0,
                                       ALU.mult, ALU.add).then_inc(scanned, 1)

            def times_c(b, k):
                dve.wait_ge(scanned, NU * b + k + 1)
                dve.wait_ge(summed, NU * b + max(k - 3, 0))
                dve.tensor_tensor(hc[:, k % 4, :], ps[:, 4 + k % 3, :], bcs[:, NS + k % NS, :],
                                  ALU.mult).then_inc(hc_ready, 1)

            def finish(b, d):
                dve.wait_ge(summed, NU * b + NS * (d + 1))
                dve.scalar_tensor_tensor(hs[:, d, :], hs[:, d, :], skip[:, d:d + 1], ps[:, d % 2, :],
                                         ALU.mult, ALU.add).then_inc(y_read, 1)
                dve.wait_ge(y_read, DC * b + d + 1)
                dve.tensor_tensor(gate[:, d, :], gate[:, d, :], hs[:, d, :], ALU.mult).then_inc(yg_ready, 1)

            with dve.Fori(0, B) as b:
                own.turn(b)
                dve.wait_ge(x_in_s, 16 * b + 16)
                dve.wait_ge(summed, NU * b)
                ln.vector(dve, own, b, x)
                for c in range(DC):
                    dve.wait_ge(hs_psum, DC * b + c + 1)
                    dve.wait_ge(yg_ready, DC * b)
                    src = ps[:, 2 + c % 3, :]
                    own.inc(dve.tensor_scalar(hs[:, c, :], src, taps[:, c, KC - 1:KC], None, ALU.mult))
                    for j in range(1, KC):
                        own.wait()
                        last = dve.scalar_tensor_tensor(hs[:, c, j:], src[:, 0:T - j], taps[:, c, KC - 1 - j:KC - j],
                                                        hs[:, c, j:], ALU.mult, ALU.add)
                        if j < KC - 1:
                            own.inc(last)
                    last.then_inc(conv_done, 1)
                dt_chunk(b, 0)
                for k in range(NU):
                    scan(b, k)
                    if k:
                        times_c(b, k - 1)
                    if k % NS == 8 and k // NS + 1 < DC:
                        dt_chunk(b, k // NS + 1)
                    if k % NS == 3 and k >= NS:
                        finish(b, k // NS - 1)
                times_c(b, NU - 1)
                finish(b, DC - 1)
                for i in range(TT):
                    dve.wait_ge(o_ready, TT * b + i + 1)
                    dve.tensor_tensor(x[:, i, :], ps[:, i % 2, :], x[:, i, :], ALU.add).then_inc(added, 1)
                own.end()


NH, NKV, DH = 16, 4, 128
MEM = T
KT = (MEM + T) // P


def attention_inputs(i):
    f32 = np.float32
    inv_freq = (f32(1) / f32(10000) ** (np.arange(0, DH, 2, dtype=f32) / f32(DH))).astype(f32)
    angle = np.outer(np.arange(T, dtype=f32), inv_freq).astype(f32)
    half = np.cos(angle), np.sin(angle)
    rope = np.stack([np.concatenate([half[0], half[0]], 1), np.concatenate([-half[1], half[1]], 1)])
    late = np.where(np.arange(P)[None, :] > np.arange(P)[:, None], f32(NEG), f32(0))
    norm_rows = np.stack([i["L1_xattn_q_norm_w"], np.roll(i["L1_xattn_q_norm_w"], DH // 2),
                          i["L1_xattn_k_norm_w"], np.roll(i["L1_xattn_k_norm_w"], DH // 2)])
    return {
        "rope": rope.astype(f32),
        "late": late.astype(f32),
        "norm_rows": norm_rows,
        **{n: i[f"L1_xattn_{n}"] for n in ("wq", "wk", "wv", "wo", "wk_ctx", "wv_ctx")},
    }


def context_attention(nc, ps, ident, identb, eps, eps6, x_in, x_out, dram):
    SCALE = float(DH) ** -0.5
    HG = NH // NKV
    with ExitStack() as ctx:
        st = Stage(nc, ctx, "ca")
        x = st.sb("x", [P, TT, H])
        xT = st.sb("xT", [P, HC, T])
        ln = Columns(st, ps, ident, eps, xT)
        wq = st.sb("wq", [P, HC, NH * DH])
        wo = st.sb("wo", [P, NH, H])
        qT = st.sb("qT", [P, NH, T])
        kT = st.sb("kT", [P, NKV, MEM + T])
        v = st.sb("v", [P, KT, NKV * DH])
        tables = st.sb("tables", [P, 4, TT, DH])
        norm_rows = st.sb("norm_rows", [P, 4, DH])
        late = st.sb("late", [P, P])
        lateb = st.sb("lateb", [P, P], BF16)
        prob = st.sb("prob", [P, 2, MEM + T])
        pT = [st.sb("pT0", [P, KT, T]), st.sb("pT1", [P, KT, T])]
        memT = pT[0][:, 0:HC, :]
        w_kv = [pT[1][:, HC * s:HC * (s + 1), :] for s in range(2)]
        raw, sq, rot = ln.xn[:, 0:2, :], ln.xn[:, 2, :], ln.xn[:, 3, :]
        roped = prob[:, :, 0:512]
        ssq = st.sb("ssq", [P, TT, NH])
        q_scale = st.sb("q_scale", [P, TT, NH])
        ssk = st.sb("ssk", [P, 2, NKV])
        rk = st.sb("rk", [P, 2, NKV])
        top = st.sb("top", [P, 2])
        ntop = st.sb("ntop", [P, 2])
        total = st.sb("total", [P, 2])
        inv = st.sb("inv", [P, 2])

        weights_in, x_in_s, x_out_s, mem_in = (st.sem(n) for n in ("weights_in", "x_in", "x_out", "mem_in"))
        kv_in = [st.sem("wk_in"), st.sem("wkc_in"), st.sem("wv_in"), st.sem("wvc_in")]
        tables_ready = st.sem("tables_ready")
        proj = st.sem("proj")
        moved = st.sem("moved")
        squared = st.sem("squared")
        reduced = st.sem("reduced")
        rms_k = st.sem("rms_k")
        rope_done = st.sem("rope_done")
        qk_turned = st.sem("qk_turned")
        qk_moved = st.sem("qk_moved")
        rms_q = st.sem("rms_q")
        scale_ready = st.sem("scale_ready")
        scores = st.sem("scores")
        tops = st.sem("tops")
        exps = st.sem("exps")
        normed = st.sem("normed")
        turned = st.sem("turned")
        pT_moved = st.sem("pT_moved")
        pv_done = st.sem("pv_done")
        out_moved = st.sem("out_moved")
        o_ready, added, v_own = st.sem("o_ready"), st.sem("added"), st.sem("v_own")
        block = ctx.enter_context(nc.Block())

        turning = [("q", i, g) for i in range(TT) for g in range(NH // 4)] \
            + [("k", i, 0) for i in range(TT)] + [("kc", i, 1) for i in range(TT)]
        groups = turning + [("v", i, 2) for i in range(TT)] + [("vc", i, 3) for i in range(TT)]
        NJ, NQ, NR = len(groups), TT * NH // 4, len(turning)
        units = [(h, i) for h in range(NH) for i in range(TT)]
        NU = len(units)

        @block.sync
        def _(sp):
            sp.dma_start(ln.xn[:, 0:2, :].rearrange("p a (i d) -> p a i d", i=TT),
                         dram["rope"].rearrange("a (i p) d -> p a i d", p=P)).then_inc(weights_in, 16)
            sp.dma_start(norm_rows[:, :, :], dram["norm_rows"].rearrange("(a r) d -> a r d", a=1)
                         .to_broadcast([P, 4, DH])).then_inc(weights_in, 16)
            sp.dma_start(late[:, :], dram["late"]).then_inc(weights_in, 16)
            sp.dma_start(wq[:, :, :], dram["wq"].rearrange("(c p) n -> p c n", p=P)).then_inc(weights_in, 16)
            sp.dma_start(wo[:, :, :], dram["wo"].rearrange("(h p) n -> p h n", p=P)).then_inc(weights_in, 16)
            with sp.Fori(0, B) as b:
                sp.wait_ge(x_out_s, 16 * b)
                sp.dma_start(x[:, :, :], rows_of(x_in, b)).then_inc(x_in_s, 16)
                sp.wait_ge(pv_done, NH * b)
                sp.dma_start(memT[:, :, :], dram["ctxT"].rearrange("b (c p) m -> b p c m", p=P)[b]).then_inc(mem_in, 16)
                for k, n in enumerate(("wk", "wk_ctx", "wv", "wv_ctx")):
                    if k >= 2:
                        sp.wait_ge(proj, NJ * b + NQ + TT * (k - 1))
                    sp.dma_start(w_kv[k % 2], dram[n].rearrange("(c p) n -> p c n", p=P)).then_inc(kv_in[k], 16)
                sp.wait_ge(added, TT * b + TT)
                sp.dma_start(rows_of(x_out, b), x[:, :, :]).then_inc(x_out_s, 16)
            sp.wait_ge(x_out_s, 16 * B)

        @block.scalar
        def _(act):
            def move_turned(b, j):
                act.wait_ge(qk_turned, NR * b + j + 1)
                n, i, g = groups[j]
                dst = {"q": qT[:, 4 * g:4 * g + 4, i * P:(i + 1) * P],
                       "k": kT[:, :, MEM + i * P:MEM + (i + 1) * P],
                       "kc": kT[:, :, i * P:(i + 1) * P]}[n]
                act.activation(dst, ps[:, 4 + j % 2, :].rearrange("p (a s) -> p a s", a=4),
                               ACT.Copy).then_inc(qk_moved, 1)

            def exp(b, k):
                h, i = units[k]
                w = MEM + (i + 1) * P
                act.wait_ge(tops, NU * b + k + 1)
                act.wait_ge(turned, 2 * NU * b + max(2 * (k - 1), 0))
                act.activation(prob[:, k % 2, 0:w],
                               ps[:, 2 * (k % 2):2 * (k % 2) + 2, :].rearrange("p a n -> p (a n)")[:, 0:w], ACT.Exp,
                               bias=ntop[:, k % 2:k % 2 + 1], scale=q_scale[:, i, h:h + 1],
                               accum_out=total[:, k % 2:k % 2 + 1]).then_inc(exps, 1)

            def move_p(b, k):
                h, i = units[k]
                if i == 0:
                    act.wait_ge(pv_done, NH * b + max(h - 1, 0))
                for half, n in ((0, TT), (1, i + 1)):
                    act.wait_ge(turned, 2 * NU * b + 2 * k + half + 1)
                    act.activation(pT[h % 2][:, TT * half:TT * half + n, i * P:(i + 1) * P],
                                   ps[:, 4 + half, 0:n * P].rearrange("p (a s) -> p a s", a=n),
                                   ACT.Copy).then_inc(pT_moved, 1)

            with act.Fori(0, B) as b:
                ln.scalar_sd(act, b)
                ln.scalar_move(act, b)
                for j, (n, i, g) in enumerate(groups):
                    act.wait_ge(proj, NJ * b + j + 1)
                    if j >= NR:
                        act.activation(v[:, i + (TT if n == "v" else 0), :], ps[:, j % 4, :], ACT.Copy).then_inc(moved, 1)
                        if j == NR:
                            move_turned(b, NR - 1)
                        continue
                    act.wait_ge(rope_done, NR * b + max(j - 1, 0))
                    act.activation(raw[:, j % 2, :], ps[:, j % 4, :], ACT.Copy).then_inc(moved, 1)
                    act.wait_ge(moved, NJ * b + j + 1)
                    act.wait_ge(reduced, NR * b + j)
                    act.activation(sq, raw[:, j % 2, :], ACT.Square).then_inc(squared, 1)
                    if n != "q":
                        act.wait_ge(reduced, NR * b + j + 1)
                        act.activation(rk[:, j % 2, :], ssk[:, j % 2, :], ACT.Sqrt, bias=eps6,
                                       scale=1.0 / DH).then_inc(rms_k, 1)
                    if j:
                        move_turned(b, j - 1)
                act.activation(q_scale[:, :, :], ssq[:, :, :], ACT.Sqrt, bias=eps6, scale=1.0 / DH).then_inc(rms_q, 1)
                exp(b, 0)
                exp(b, 1)
                for k in range(NU):
                    move_p(b, k)
                    if k + 2 < NU:
                        exp(b, k + 2)

        @block.tensor
        def _(pe):
            pe.wait_ge(weights_in, 80)
            with pe.Fori(0, B) as b:
                pe.wait_ge(tables_ready, 1)
                pe.wait_ge(added, TT * b)
                ln.tensor(pe, b)
                pe.wait_ge(ln.xT_ready, HC * b + HC)
                pe.wait_ge(mem_in, 16 * b + 16)

                def turn_qk(j):
                    pe.wait_ge(rope_done, NR * b + j + 1)
                    pe.wait_ge(qk_moved, NR * b + max(j - 1, 0))
                    for a in range(4):
                        last = pe.transpose(ps[:, 4 + j % 2, a * P:(a + 1) * P],
                                            roped[:, j % 2, a * P:(a + 1) * P], ident)
                    last.then_inc(qk_turned, 1)

                for j, (n, i, g) in enumerate(groups):
                    if n != "q" and i == 0:
                        pe.wait_ge(kv_in[g], 16 * b + 16)
                    pe.wait_ge(moved, NJ * b + max(j - 3, 0))
                    src = memT if n in ("kc", "vc") else xT
                    for c in range(HC):
                        w = wq[:, c, g * 512:(g + 1) * 512] if n == "q" else w_kv[g % 2][:, c, :]
                        last = pe.matmul(ps[:, j % 4, :], src[:, c, i * P:(i + 1) * P], w,
                                         start=(c == 0), stop=(c == HC - 1))
                    last.then_inc(proj, 1)
                    if 1 <= j <= NR:
                        turn_qk(j - 1)
                pe.wait_ge(qk_moved, NR * b + NR)
                pe.wait_ge(moved, NJ * b + NJ)

                def score(k):
                    h, i = units[k]
                    pe.wait_ge(exps, NU * b + max(k - 1, 0))
                    q = qT[:, h, i * P:(i + 1) * P]
                    pe.matmul(ps[:, 2 * (k % 2), :], q, kT[:, h // HG, 0:MEM], start=True, stop=True)
                    own = ps[:, 2 * (k % 2) + 1, :]
                    pe.matmul(own[:, 0:(i + 1) * P], q, kT[:, h // HG, MEM:MEM + (i + 1) * P],
                              start=True, stop=False, skip_group_check=True)
                    pe.matmul(own[:, i * P:(i + 1) * P], identb, lateb[:, :], start=False, stop=True,
                              skip_group_check=True).then_inc(scores, 1)

                def turn(k):
                    h, i = units[k]
                    pe.wait_ge(normed, NU * b + k + 1)
                    for half, n in ((0, TT), (1, i + 1)):
                        pe.wait_ge(pT_moved, 2 * NU * b + max(2 * k + half - 1, 0))
                        for a in range(n):
                            m = TT * half + a
                            last = pe.transpose(ps[:, 4 + half, a * P:(a + 1) * P], prob[:, k % 2, m * P:(m + 1) * P], ident)
                        last.then_inc(turned, 1)

                def pv(h, part):
                    if part == 0:
                        pe.wait_ge(pT_moved, 2 * NU * b + 2 * TT * (h + 1))
                        pe.wait_ge(out_moved, NH * b + max(h - 1, 0))
                    for m in (2 * part, 2 * part + 1):
                        s0 = max(m - TT, 0) * P
                        last = pe.matmul(ps[:, 6 + h % 2, s0:T], v[:, m, h // HG * DH:(h // HG + 1) * DH],
                                         pT[h % 2][:, m, s0:T], start=(m == 0), stop=(m == KT - 1),
                                         skip_group_check=True)
                    if part == TT - 1:
                        last.then_inc(pv_done, 1)

                score(0)
                score(1)
                for k in range(NU + 6):
                    if k < NU:
                        turn(k)
                    if k + 2 < NU:
                        score(k + 2)
                    if k >= TT + 0 and (k - TT) // TT < NH:
                        pv((k - TT) // TT, (k - TT) % TT)
                for i in range(TT):
                    pe.wait_ge(out_moved, NH * b + NH)
                    pe.wait_ge(added, TT * b + max(i - 1, 0))
                    for h in range(NH):
                        last = pe.matmul(ps[:, i % 2, :], qT[:, h, i * P:(i + 1) * P], wo[:, h, :],
                                         start=(h == 0), stop=(h == NH - 1))
                    last.then_inc(o_ready, 1)

        @block.vector
        def _(dve):
            own = Chain(dve, v_own, 211)
            dve.wait_ge(weights_in, 80)
            dve.tensor_copy(lateb[:, :], late[:, :])
            for a in range(4):
                last = dve.tensor_tensor(tables[:, a, :, :], ln.xn[:, a % 2, :].rearrange("p (i d) -> p i d", i=TT),
                                         norm_rows[:, a:a + 1, :].to_broadcast([P, TT, DH]), ALU.mult)
            last.then_inc(tables_ready, 1)
            dve.wait_ge(tables_ready, 1)

            def by_head(t, lo=0, hi=DH):
                return t.rearrange("p (a d) -> p a d", d=DH)[:, :, lo:hi]

            def rope(b, j):
                n, i, g = groups[j]
                t = 0 if n == "q" else 2
                out, q = roped[:, j % 2, :], raw[:, j % 2, :]
                dve.wait_ge(squared, NR * b + j + 1)
                ss = ssq[:, i, 4 * g:4 * g + 4] if n == "q" else ssk[:, j % 2, :]
                dve.tensor_reduce(ss, by_head(sq), AX.X, ALU.add).then_inc(reduced, 1)
                dve.wait_ge(qk_turned, NR * b + max(j - 1, 0))
                if n == "kc":
                    own.inc(dve.tensor_tensor(by_head(out), by_head(q), norm_rows[:, 2:3, :].to_broadcast([P, 4, DH]),
                                              ALU.mult))
                    own.wait()
                else:
                    own.inc(dve.tensor_tensor(by_head(out), by_head(q),
                                              tables[:, t, i:i + 1, :].to_broadcast([P, 4, DH]), ALU.mult))
                    dve.wait_ge(rope_done, NR * b + j)
                    for lo in (0, DH // 2):
                        hi, other = lo + DH // 2, DH // 2 - lo
                        own.inc(dve.tensor_tensor(by_head(rot, lo, hi), by_head(q, other, other + DH // 2),
                                                  tables[:, t + 1, i:i + 1, lo:hi].to_broadcast([P, 4, DH // 2]),
                                                  ALU.mult))
                    own.wait()
                    last = dve.tensor_tensor(out, out, rot, ALU.add)
                    if n == "q":
                        last.then_inc(rope_done, 1)
                        return
                    own.inc(last)
                dve.wait_ge(rms_k, 2 * TT * b + j - NQ + 1)
                own.inc(dve.reciprocal(rk[:, j % 2, :], rk[:, j % 2, :]))
                own.wait()
                dve.tensor_tensor(by_head(out), by_head(out),
                                  rk[:, j % 2, :].rearrange("p (a o) -> p a o", o=1).to_broadcast([P, 4, DH]),
                                  ALU.mult).then_inc(rope_done, 1)

            def maximum(b, k):
                h, i = units[k]
                w = MEM + (i + 1) * P
                dve.wait_ge(scores, NU * b + k + 1)
                own.inc(dve.tensor_reduce(top[:, k % 2:k % 2 + 1],
                                          ps[:, 2 * (k % 2):2 * (k % 2) + 2, :].rearrange("p a n -> p (a n)")[:, 0:w],
                                          AX.X, ALU.max))
                own.wait()
                dve.tensor_scalar(ntop[:, k % 2:k % 2 + 1], top[:, k % 2:k % 2 + 1], q_scale[:, i, h:h + 1], -1.0,
                                  ALU.mult, ALU.mult).then_inc(tops, 1)

            def normalise(b, k):
                h, i = units[k]
                w = MEM + (i + 1) * P
                dve.wait_ge(exps, NU * b + k + 1)
                own.inc(dve.reciprocal(inv[:, k % 2:k % 2 + 1], total[:, k % 2:k % 2 + 1]))
                own.wait()
                dve.tensor_scalar(prob[:, k % 2, 0:w], prob[:, k % 2, 0:w], inv[:, k % 2:k % 2 + 1], None,
                                  ALU.mult).then_inc(normed, 1)

            def move_out(b, h):
                dve.wait_ge(pv_done, NH * b + h + 1)
                dve.tensor_copy(qT[:, h, :], ps[:, 6 + h % 2, :]).then_inc(out_moved, 1)

            with dve.Fori(0, B) as b:
                own.turn(b)
                dve.wait_ge(x_in_s, 16 * b + 16)
                ln.vector(dve, own, b, x)
                for j in range(NR):
                    rope(b, j)
                dve.wait_ge(rms_q, b + 1)
                own.inc(dve.reciprocal(q_scale[:, :, :], q_scale[:, :, :]))
                own.wait()
                own.inc(dve.tensor_scalar(q_scale[:, :, :], q_scale[:, :, :], SCALE, None, ALU.mult))
                own.wait()
                maximum(b, 0)
                for k in range(NU):
                    if k + 1 < NU:
                        maximum(b, k + 1)
                    normalise(b, k)
                    if k >= 2 * TT + 1 and k % TT == 1:
                        move_out(b, k // TT - 2)
                move_out(b, NH - 2)
                move_out(b, NH - 1)
                for i in range(TT):
                    dve.wait_ge(o_ready, TT * b + i + 1)
                    dve.tensor_tensor(x[:, i, :], ps[:, i % 2, :], x[:, i, :], ALU.add).then_inc(added, 1)
                own.end()


NE, TOP, SEL, FI = 64, 8, 4, 192
NT = B * TT
SLOT_TILES = B * T * TOP // P + NE
SLOTS = SLOT_TILES * P


def expert_inputs(i):
    return {
        "gateT": i["L1_ffn_gate_weight"].T,
        "similarity": i["L1_ffn_similarity"],
        "guT": i["L1_ffn_gate_up_proj"].transpose(0, 2, 1),
        "downT": i["L1_ffn_down_proj"].transpose(0, 2, 1),
        "count_row": np.arange(SLOT_TILES, dtype=np.float32).reshape(1, SLOT_TILES),
        "before": np.triu(np.ones((P, P), np.float32), 1),
        "token_ids": np.arange(B * T, dtype=np.float32).reshape(NT, P).T,
    }


def route(nc, ps, ident, ones, eps, x_in, dram, x, keep):
    xn_rows, slot_tokens = keep["xn_rows"], keep["slot_tokens"]
    slot, share, tile_expert, tokens = (keep[n] for n in ("slot", "share", "tile_expert", "tokens"))
    with ExitStack() as ctx:
        st = Stage(nc, ctx, "rt")
        xT = st.sb("xT", [P, B, HC, T])
        ln = Columns(st, ps, ident, eps, None)
        gateT = st.sb("gateT", [P, HC, NE])
        sim = st.sb("sim", [NE, NE])
        count = st.sb("count", [P, SLOT_TILES])
        before = st.sb("before", [P, P])
        upto = st.sb("upto", [NE, NE])
        token_ids = st.sb("token_ids", [P, NT])
        prob = st.sb("prob", [P, NT, NE])
        top, total = st.sb("top", [P, NT]), st.sb("total", [P, NT])
        index = st.sb("index", [P, NT, TOP], U32)
        indexf = st.sb("indexf", [P, NT, TOP])
        hot = st.sb("hot", [P, NT, TOP, NE])
        chosen = st.sb("chosen", [P, 2, NT, NE])
        turned_sb = st.sb("turned_sb", [NE, 2, P])
        primary = st.sb("primary", [NE, NE])
        cand = st.sb("cand", [NE, NE])
        cbest = st.sb("cbest", [NE, TOP])
        cindex = st.sb("cindex", [NE, TOP], U32)
        cindexf = st.sb("cindexf", [NE, TOP])
        moves = st.sb("moves", [NE, 3])
        to = st.sb("to", [NE, NE])
        toT = st.sb("toT", [NE, NE])
        member = st.sb("member", [P, NT, NE])
        earlier = st.sb("earlier", [P, NT + 1, NE])
        tiles = st.sb("tiles", [NE, 1])
        end = st.sb("end", [NE, 1])
        base = st.sb("base", [P, NE])
        place = st.sb("place", [P, 2, NT, NE])
        past = st.sb("past", [NE, SLOT_TILES])
        slotf = st.sb("slotf", [P, NT, TOP])
        zero = st.sb("zero", [P, SLOT_TILES])
        lists = st.sb("lists", [P, 2, P])
        const_in, x_in_s, xn_out = st.sem("const_in"), st.sem("x_in"), st.sem("xn_out")
        list_cleared, scattered, list_in = st.sem("list_cleared"), st.sem("scattered"), st.sem("list_in")
        logits, logits_moved = st.sem("logits"), st.sem("logits_moved")
        shifted, exps = st.sem("shifted"), st.sem("exps")
        zero_set = st.sem("zero_set")
        chosen_ready, counts = st.sem("chosen_ready"), st.sem("counts")
        to_ready = st.sem("to_ready")
        to_turned, to_moved = st.sem("to_turned"), st.sem("to_moved")
        later_turned, later_moved = st.sem("later_turned"), st.sem("later_moved")
        sent = st.sem("sent")
        member_ready, ranked = st.sem("member_ready"), st.sem("ranked")
        tiles_ready, based = st.sem("tiles_ready"), st.sem("based")
        past_ready, past_summed = st.sem("past_ready"), st.sem("past_summed")
        place_ready = st.sem("place_ready")
        slots_ready, lists_turned = st.sem("slots_ready"), st.sem("lists_turned")
        v_own = st.sem("v_own")
        block = ctx.enter_context(nc.Block())

        @block.sync
        def _(sp):
            sp.dma_start(x[:, :, :], x_in.rearrange("(n p) h -> p n h", p=P)).then_inc(x_in_s, 16)
            sp.dma_start(gateT[:, :, :], dram["gateT"].rearrange("(c p) e -> p c e", p=P)).then_inc(const_in, 16)
            sp.dma_start(sim[:, :], dram["similarity"]).then_inc(const_in, 16)
            sp.dma_start(count[:, :], dram["count_row"].to_broadcast([P, SLOT_TILES])).then_inc(const_in, 16)
            sp.dma_start(before[:, :], dram["before"]).then_inc(const_in, 16)
            sp.dma_start(token_ids[:, :], dram["token_ids"]).then_inc(const_in, 16)
            sp.wait_ge(zero_set, 1)
            sp.dma_start(slot_tokens.rearrange("(p j) o -> p (j o)", p=P), zero[:, :]).then_inc(list_cleared, 16)
            with sp.Fori(0, B) as b:
                sp.wait_ge(ln.xn_ready, b + 1)
                sp.dma_start(rows_of(xn_rows, b), ln.xn[:, :, :]).then_inc(xn_out, 16)
            sp.wait_ge(xn_out, 16 * B)
            sp.wait_ge(scattered, 16 * NT * TOP)
            sp.dma_start(lists[:, 0, :], slot_tokens[0:P * P].rearrange("(j p) o -> j (p o)", p=P)).then_inc(list_in, 16)
            sp.dma_start(lists[0:SLOT_TILES - P, 1, :],
                         slot_tokens[P * P:SLOTS].rearrange("(j p) o -> j (p o)", p=P)).then_inc(list_in, 16)

        @block.gpsimd
        def _(pool):
            pool.wait_ge(list_cleared, 16)
            pool.wait_ge(slots_ready, 1)
            for n in range(NT):
                for r in range(TOP):
                    pool.indirect_dma_start(
                        slot_tokens, bass.IndirectOffsetOnAxis(ap=slot[:, n, r:r + 1], axis=0),
                        token_ids[:, n:n + 1], None).then_inc(scattered, 16)

        @block.scalar
        def _(act):
            with act.Fori(0, B) as b:
                ln.scalar_sd(act, b)
                for c in range(HC):
                    act.wait_ge(ln.turned, HC * b + c + 1)
                    act.activation(xT[:, b, c, :], ps[:, c % 2, :], ACT.Copy).then_inc(ln.xT_ready, 1)
            act.wait_ge(logits, 1)
            act.activation(prob[:, :, :].rearrange("p n e -> p (n e)"),
                           ps[:, 2:4, :].rearrange("p a n -> p (a n)"), ACT.Copy).then_inc(logits_moved, 1)
            act.wait_ge(shifted, 1)
            act.activation(prob[:, :, :], prob[:, :, :], ACT.Exp).then_inc(exps, 1)
            act.wait_ge(to_turned, 1)
            act.activation(toT[:, :], ps[0:NE, 0, 0:NE], ACT.Copy).then_inc(to_moved, 1)
            for k in range(2 * NT):
                act.wait_ge(later_turned, k + 1)
                if k >= 2:
                    act.wait_ge(sent, k - 1)
                act.activation(turned_sb[:, k % 2, :], ps[0:NE, k % 2, 0:P], ACT.Copy).then_inc(later_moved, 1)

        @block.tensor
        def _(pe):
            with pe.Fori(0, B) as b:
                ln.tensor(pe, b)
            pe.wait_ge(ln.xT_ready, HC * B)
            pe.wait_ge(const_in, 16 * 5)
            for n in range(NT):
                for c in range(HC):
                    last = pe.matmul(ps[:, 2 + n // 8, n % 8 * NE:(n % 8 + 1) * NE],
                                     xT[:, n // TT, c, n % TT * P:(n % TT + 1) * P], gateT[:, c, :],
                                     start=(c == 0), stop=(c == HC - 1))
            last.then_inc(logits, 1)
            pe.wait_ge(chosen_ready, B)
            for s in range(2):
                for n in range(NT):
                    pe.matmul(ps[:, 4, s * NE:(s + 1) * NE], ones, chosen[:, s, n, :],
                              start=(n == 0), stop=(n == NT - 1))
            for s in range(2):
                for n in range(NT):
                    last = pe.matmul(ps[0:NE, 5, s:s + 1], chosen[:, s, n, :], ones[:, 0:1],
                                     start=(n == 0), stop=(n == NT - 1))
            last.then_inc(counts, 1)
            pe.wait_ge(to_ready, 1)
            pe.transpose(ps[0:NE, 0, 0:NE], to[:, :], ident[0:NE, 0:NE]).then_inc(to_turned, 1)
            pe.wait_ge(to_moved, 1)

            def times(k, rows, right):
                n = k % NT
                if k >= 2:
                    pe.wait_ge(later_moved, k - 1)
                pe.transpose(ps[0:NE, k % 2, 0:P], rows, ident).then_inc(later_turned, 1)
                pe.wait_ge(later_moved, k + 1)
                pe.matmul(ps[:, 6 + n // 8, n % 8 * NE:(n % 8 + 1) * NE], turned_sb[:, k % 2, :], right,
                          start=True, stop=True).then_inc(sent, 1)

            for n in range(NT):
                times(n, chosen[:, 1, n, :], to[:, :])
            pe.wait_ge(member_ready, 1)
            for n in range(NT):
                out = ps[:, 2 + n // 8, n % 8 * NE:(n % 8 + 1) * NE]
                pe.matmul(out, before[:, :], member[:, n, :], start=True, stop=False)
                pe.matmul(out, ones, earlier[:, n, :], start=False, stop=True)
            pe.matmul(ps[0:NE, 5, 4:5], earlier[:, NT, :], ones[:, 0:1], start=True, stop=True).then_inc(ranked, 1)
            pe.wait_ge(tiles_ready, 1)
            pe.matmul(ps[:, 4, 0:NE], tiles[:, 0:1].to_broadcast([NE, P]), before[0:NE, 0:NE], start=True, stop=True)
            pe.matmul(ps[0:NE, 4, NE:NE + 1], upto[:, :], tiles[:, :], start=True, stop=True).then_inc(based, 1)
            pe.wait_ge(past_ready, 1)
            pe.matmul(ps[:, 5, 0:SLOT_TILES], ones[0:NE, :], past[:, :], start=True, stop=True).then_inc(past_summed, 1)
            pe.wait_ge(place_ready, 1)
            for n in range(NT):
                times(NT + n, place[:, 0, n, :], toT[:, :])
            pe.wait_ge(list_in, 32)
            pe.transpose(ps[:, 0, 0:P], lists[:, 0, :], ident)
            pe.transpose(ps[:, 0, P:SLOT_TILES], lists[0:SLOT_TILES - P, 1, :],
                         ident[0:SLOT_TILES - P, 0:SLOT_TILES - P]).then_inc(lists_turned, 1)

        @block.vector
        def _(dve):
            own = Chain(dve, v_own, 5)
            dve.memset(zero[:, :], 0.0).then_inc(zero_set, 1)
            dve.wait_ge(x_in_s, 16)
            with dve.Fori(0, B) as b:
                own.turn(b)
                dve.wait_ge(xn_out, 16 * b)
                ln.vector(dve, own, b, x[:, :, :].rearrange("p (b i) h -> p b i h", b=B)[:, b])
                own.end()

            def step(instruction):
                own.inc(instruction)
                own.wait()

            def bc(t, shape):
                return t.rearrange("p (n o) -> p n o", o=1).to_broadcast(shape)

            def flat(t):
                return t.rearrange("p n e -> p (n e)")

            own.turn(B)
            dve.wait_ge(logits_moved, 1)
            step(dve.tensor_reduce(top[:, :], prob[:, :, :], AX.X, ALU.max))
            dve.tensor_tensor(prob[:, :, :], prob[:, :, :], bc(top[:, :], [P, NT, NE]), ALU.subtract).then_inc(shifted, 1)
            dve.wait_ge(exps, 1)
            step(dve.tensor_reduce(total[:, :], prob[:, :, :], AX.X, ALU.add))
            step(dve.reciprocal(total[:, :], total[:, :]))
            step(dve.tensor_tensor(prob[:, :, :], prob[:, :, :], bc(total[:, :], [P, NT, NE]), ALU.mult))
            for n in range(NT):
                own.inc(dve.max(share[:, n, :], prob[:, n, :]))
            own.wait()
            for n in range(NT):
                own.inc(dve.max_index(index[:, n, :], share[:, n, :], prob[:, n, :]))
            own.wait()
            step(dve.tensor_copy(indexf[:, :, :], index[:, :, :]))
            step(dve.tensor_reduce(total[:, :], share[:, :, :], AX.X, ALU.add))
            step(dve.tensor_scalar(total[:, :], total[:, :], 1e-12, None, ALU.max))
            step(dve.reciprocal(total[:, :], total[:, :]))
            step(dve.tensor_tensor(share[:, :, :], share[:, :, :], bc(total[:, :], [P, NT, TOP]), ALU.mult))
            dve.wait_ge(const_in, 16 * 5)
            for b in range(B):
                for n in range(TT * b, TT * b + TT):
                    own.inc(dve.tensor_tensor(hot[:, n, :, :], bc(indexf[:, n, :], [P, TOP, NE]),
                                              count[:, 0:NE].rearrange("p (o e) -> p o e", o=1)
                                              .to_broadcast([P, TOP, NE]), ALU.is_equal))
                own.wait()
                for s in range(2):
                    for n in range(TT * b, TT * b + TT):
                        last = dve.tensor_reduce(chosen[:, s, n, :],
                                                 hot[:, n, s * SEL:(s + 1) * SEL, :].rearrange("p r e -> p e r"),
                                                 AX.X, ALU.add)
                last.then_inc(chosen_ready, 1)

            eye = ident[0:NE, 0:NE]
            step(dve.tensor_tensor(upto[:, :], before[0:NE, 0:NE], eye, ALU.add))
            step(dve.tensor_tensor(cand[:, :], sim[:, :], eye, ALU.mult))
            step(dve.tensor_tensor(sim[:, :], sim[:, :], cand[:, :], ALU.subtract))
            step(dve.tensor_tensor(sim[:, :], sim[:, :], eye, ALU.add))
            dve.wait_ge(counts, 1)
            step(dve.tensor_scalar(primary[:, :], ps[0:NE, 4, 0:NE], 0.5, None, ALU.is_ge))
            step(dve.tensor_tensor(cand[:, :], sim[:, :], primary[:, :], ALU.mult))
            step(dve.tensor_scalar(primary[:, :], primary[:, :], -NEG, NEG, ALU.mult, ALU.add))
            step(dve.tensor_tensor(cand[:, :], cand[:, :], primary[:, :], ALU.add))
            step(dve.max(cbest[:, :], cand[:, :]))
            step(dve.max_index(cindex[:, :], cbest[:, :], cand[:, :]))
            step(dve.tensor_copy(cindexf[:, :], cindex[:, :]))
            step(dve.tensor_scalar(moves[:, 0:1], ps[0:NE, 5, 0:1], 0.5, None, ALU.is_lt))
            step(dve.tensor_scalar(moves[:, 1:2], ps[0:NE, 5, 1:2], 0.5, None, ALU.is_ge))
            step(dve.tensor_scalar(moves[:, 2:3], cbest[:, 0:1], 0.5, None, ALU.is_ge))
            step(dve.tensor_tensor(moves[:, 0:1], moves[:, 0:1], moves[:, 1:2], ALU.mult))
            step(dve.tensor_tensor(moves[:, 0:1], moves[:, 0:1], moves[:, 2:3], ALU.mult))
            step(dve.tensor_scalar(to[:, :], count[0:NE, 0:NE], cindexf[:, 0:1], None, ALU.is_equal))
            step(dve.tensor_tensor(to[:, :], to[:, :], eye, ALU.subtract))
            step(dve.tensor_scalar(to[:, :], to[:, :], moves[:, 0:1], None, ALU.mult))
            dve.tensor_tensor(to[:, :], to[:, :], eye, ALU.add).then_inc(to_ready, 1)

            both = ps[:, 6:8, :].rearrange("p a n -> p (a n)")
            own.inc(dve.memset(earlier[:, 0, :], 0.0))
            dve.wait_ge(sent, NT)
            step(dve.tensor_tensor(flat(member[:, :, :]), both, flat(chosen[:, 0, :, :]), ALU.add))
            step(dve.tensor_scalar(member[:, :, :], member[:, :, :], 0.5, None, ALU.is_ge))
            for n in range(NT):
                last = dve.tensor_tensor(earlier[:, n + 1, :], earlier[:, n, :], member[:, n, :], ALU.add)
                if n < NT - 1:
                    step(last)
            last.then_inc(member_ready, 1)
            dve.wait_ge(ranked, 1)
            step(dve.tensor_scalar(tiles[:, :], ps[0:NE, 5, 4:5], 1.0 / P, (P - 1) / (2.0 * P), ALU.mult, ALU.add))
            step(dve.tensor_scalar(tiles[:, :], tiles[:, :], ROUND, None, ALU.add))
            dve.tensor_scalar(tiles[:, :], tiles[:, :], ROUND, None, ALU.subtract).then_inc(tiles_ready, 1)
            dve.wait_ge(based, 1)
            step(dve.tensor_scalar(base[:, :], ps[:, 4, 0:NE], float(P), None, ALU.mult))
            step(dve.tensor_copy(end[:, :], ps[0:NE, 4, NE:NE + 1]))
            dve.tensor_scalar(past[:, :], count[0:NE, :], end[:, 0:1], None, ALU.is_ge).then_inc(past_ready, 1)
            dve.tensor_tensor(place[:, 0, :, :], ps[:, 2:4, :].rearrange("p a (n e) -> p (a n) e", e=NE),
                              base[:, :].rearrange("p (o e) -> p o e", o=1).to_broadcast([P, NT, NE]),
                              ALU.add).then_inc(place_ready, 1)
            dve.wait_ge(past_summed, 1)
            own.inc(dve.tensor_scalar(tile_expert[:, :], ps[0:1, 5, 0:SLOT_TILES], float(NE - 1), None, ALU.min))
            dve.wait_ge(sent, 2 * NT)
            step(dve.tensor_copy(flat(place[:, 1, :, :]), both))
            for s in range(2):
                for n in range(NT):
                    part = hot[:, n, s * SEL:(s + 1) * SEL, :]
                    own.inc(dve.tensor_tensor(part, part, place[:, s, n:n + 1, :].to_broadcast([P, SEL, NE]), ALU.mult))
            own.wait()
            step(dve.tensor_reduce(slotf[:, :, :], hot[:, :, :, :], AX.X, ALU.add))
            dve.tensor_copy(slot[:, :, :], slotf[:, :, :]).then_inc(slots_ready, 1)
            dve.wait_ge(lists_turned, 1)
            step(dve.tensor_copy(tokens[:, :], ps[:, 0, 0:SLOT_TILES]))


def experts(nc, ps, ident, ones, eps, x_in, x_out, dram):
    xn_rows = nc.dram_tensor("xn_rows", (B * T, H), F32, kind="Internal").ap()
    slot_tokens = nc.dram_tensor("slot_tokens", (SLOTS, 1), F32, kind="Internal").ap()
    y_rows = nc.dram_tensor("y_rows", (SLOTS, H), F32, kind="Internal").ap()
    with ExitStack() as outer:
        held = Stage(nc, outer, "ex")
        x = held.sb("x", [P, NT, H])
        slot = held.sb("slot", [P, NT, TOP], U32)
        share = held.sb("share", [P, NT, TOP])
        tile_expert = held.sb("tile_expert", [1, SLOT_TILES], I32)
        tokens = held.sb("tokens", [P, SLOT_TILES], U32)
        route(nc, ps, ident, ones, eps, x_in, dram, x, {
            "xn_rows": xn_rows, "slot_tokens": slot_tokens, "slot": slot, "share": share,
            "tile_expert": tile_expert, "tokens": tokens})
        slot_products(nc, ps, ident, dram, xn_rows, y_rows, tile_expert, tokens)
        combine(nc, x, x_out, y_rows, slot, share)


def slot_products(nc, ps, ident, dram, xn_rows, y_rows, tile_expert, tokens):
    FH = FI // 2
    D = 4
    with ExitStack() as ctx:
        st = Stage(nc, ctx, "sp")
        w_gu = [st.sb(f"w_gu{s}", [P, HC, 2 * FI]) for s in range(D)]
        w_d = [st.sb(f"w_d{s}", [FH, 2, H]) for s in range(D)]
        idx = [st.sb(f"idx{s}", [P, 1], U32) for s in range(D)]
        xg = [st.sb(f"xg{s}", [P, H]) for s in range(D)]
        y = [st.sb(f"y{s}", [P, H]) for s in range(D)]
        xgT = st.sb("xgT", [P, 2, HC, P])
        act_g = st.sb("act_g", [P, 2, FI])
        hid = st.sb("hid", [P, 2, FI])
        hidT = st.sb("hidT", [FH, 2, 2, P])
        w_in = [st.sem(f"w_in{s}") for s in range(D)]
        gathered = [st.sem(f"gathered{s}") for s in range(D)]
        y_out = [st.sem(f"y_out{s}") for s in range(D)]
        idx_ready = st.sem("idx_ready")
        x_turned = st.sem("x_turned")
        x_moved = st.sem("x_moved")
        gu_done = st.sem("gu_done")
        silu = st.sem("silu")
        hid_ready = st.sem("hid_ready")
        h_turned = st.sem("h_turned")
        h_moved = st.sem("h_moved")
        o_done = st.sem("o_done")
        y_ready = st.sem("y_ready")
        passed = st.sem("passed")
        block = ctx.enter_context(nc.Block())

        def pipeline(eng, steps):
            for j in range(D):
                steps(j, j)
            with eng.Fori(D, SLOT_TILES - D, D) as j0:
                j0 = nc.s_assert_within(j0, D, SLOT_TILES - 2 * D)
                for s in range(D):
                    steps(j0 + s, s)
            for s in range(D):
                steps(SLOT_TILES - D + s, s)

        def exists(j):
            return not isinstance(j, int) or 0 <= j < SLOT_TILES

        def ring(eng, sem, per, j, s):
            eng.wait_ge(sem[s], per // D * (j - s) + per)

        def reused(j):
            return not isinstance(j, int) or j >= D

        def reused2(j):
            return not isinstance(j, int) or j >= 2

        @block.sync
        def _(sp):
            def load(j, s):
                if not exists(j):
                    return
                e = sp.value_load(tile_expert[0:1, j:j + 1] if isinstance(j, int) else tile_expert[0:1, bass.ds(j, 1)],
                                  min_val=0, max_val=NE - 1)
                if reused(j):
                    sp.wait_ge(o_done, j - D + 1)
                sp.dma_start(w_gu[s][:, :, :], dram["guT"].rearrange("e (c p) n -> e p c n", p=P)[e]).then_inc(w_in[s], 16)
                sp.dma_start(w_d[s][:, :, :], dram["downT"].rearrange("e (c p) n -> e p c n", p=FH)[e]).then_inc(w_in[s], 16)

            def store(j, s):
                if not exists(j):
                    return
                sp.wait_ge(y_ready, j + 1)
                sp.dma_start(y_rows.rearrange("(j p) h -> j p h", p=P)[j], y[s][:, :]).then_inc(y_out[s], 16)

            for j in range(3):
                load(j, j)

            def steps(j, s):
                load(j + 3, (s + 3) % D)
                store(j - 2 if not isinstance(j, int) or j >= 2 else -1, (s + 2) % D)

            pipeline(sp, steps)
            for j in (SLOT_TILES - 2, SLOT_TILES - 1):
                store(j, j % D)
            for s in range(D):
                sp.wait_ge(y_out[s], 16 * (SLOT_TILES // D))

        @block.gpsimd
        def _(pool):
            def gather(j, s):
                if not exists(j):
                    return
                if reused(j):
                    pool.wait_ge(x_turned, j - D + 1)
                pool.tensor_copy(idx[s][:, :], tokens[:, j:j + 1] if isinstance(j, int)
                                 else tokens[:, bass.ds(j, 1)]).then_inc(idx_ready, 1)
                pool.wait_ge(idx_ready, j + 1)
                pool.sem_inc(passed, 1)
                pool.indirect_dma_start(xg[s][:, :], None, xn_rows,
                                        bass.IndirectOffsetOnAxis(ap=idx[s][:, 0:1], axis=0)).then_inc(gathered[s], 16)

            for j in range(3):
                gather(j, j)
            pipeline(pool, lambda j, s: gather(j + 3, (s + 3) % D))

        @block.scalar
        def _(act):
            def move_x(j, s):
                if not exists(j):
                    return
                act.wait_ge(x_turned, j + 1)
                if reused2(j):
                    act.wait_ge(gu_done, j - 1)
                act.activation(xgT[:, s % 2, :, :], ps[:, s % 2, :], ACT.Copy).then_inc(x_moved, 1)

            def steps(j, s):
                if isinstance(j, int) and j == 0:
                    move_x(0, 0)
                move_x(j + 1, s + 1)
                act.wait_ge(gu_done, j + 1)
                if reused2(j):
                    act.wait_ge(hid_ready, j - 1)
                act.activation(act_g[:, s % 2, :], ps[:, 2 + s % 2, 0:FI], ACT.Silu).then_inc(silu, 1)
                if isinstance(j, int) and j == 0:
                    return
                move_h(j - 1, s + 1)

            def move_h(j, s):
                act.wait_ge(h_turned, j + 1)
                if reused2(j):
                    act.wait_ge(o_done, j - 1)
                act.activation(hidT[:, s % 2, :, :], ps[0:FH, 4 + s % 2, 0:2 * P], ACT.Copy).then_inc(h_moved, 1)

            pipeline(act, steps)
            move_h(SLOT_TILES - 1, 1)

        @block.tensor
        def _(pe):
            def turn_x(j, s):
                if not exists(j):
                    return
                ring(pe, gathered, 16, j, s)
                if reused2(j):
                    pe.wait_ge(x_moved, j - 1)
                for c in range(HC):
                    last = pe.transpose(ps[:, s % 2, c * P:(c + 1) * P], xg[s][:, c * P:(c + 1) * P], ident)
                last.then_inc(x_turned, 1)

            def gate_up(j, s):
                ring(pe, w_in, 32, j, s)
                pe.wait_ge(x_moved, j + 1)
                if reused2(j):
                    pe.wait_ge(hid_ready, j - 1)
                for c in range(HC):
                    last = pe.matmul(ps[:, 2 + s % 2, 0:2 * FI], xgT[:, s % 2, c, :], w_gu[s][:, c, :],
                                     start=(c == 0), stop=(c == HC - 1))
                last.then_inc(gu_done, 1)

            def turn_h(j, s):
                pe.wait_ge(hid_ready, j + 1)
                if reused2(j):
                    pe.wait_ge(h_moved, j - 1)
                for a in range(2):
                    last = pe.transpose(ps[0:FH, 4 + s % 2, a * P:(a + 1) * P], hid[:, s % 2, a * FH:(a + 1) * FH], ident)
                last.then_inc(h_turned, 1)

            def down(j, s):
                pe.wait_ge(h_moved, j + 1)
                if reused2(j):
                    pe.wait_ge(y_ready, j - 1)
                for a in range(2):
                    last = pe.matmul(ps[:, 6 + s % 2, :], hidT[:, s % 2, a, :], w_d[s][:, a, :],
                                     start=(a == 0), stop=(a == 1))
                last.then_inc(o_done, 1)

            def steps(j, s):
                turn_x(j + 1, (s + 1) % D)
                gate_up(j, s)
                if not isinstance(j, int) or j >= 1:
                    turn_h(j - 1, (s + 3) % D)
                if not isinstance(j, int) or j >= 2:
                    down(j - 2, (s + 2) % D)

            turn_x(0, 0)
            pipeline(pe, steps)
            turn_h(SLOT_TILES - 1, D - 1)
            down(SLOT_TILES - 2, D - 2)
            down(SLOT_TILES - 1, D - 1)

        @block.vector
        def _(dve):
            def move_y(j, s):
                dve.wait_ge(o_done, j + 1)
                if reused(j):
                    ring(dve, y_out, 16, j - D, s)
                dve.tensor_copy(y[s][:, :], ps[:, 6 + s % 2, :]).then_inc(y_ready, 1)

            def steps(j, s):
                dve.wait_ge(silu, j + 1)
                if reused2(j):
                    dve.wait_ge(h_turned, j - 1)
                dve.tensor_tensor(hid[:, s % 2, :], ps[:, 2 + s % 2, FI:2 * FI], act_g[:, s % 2, :],
                                  ALU.mult).then_inc(hid_ready, 1)
                if not isinstance(j, int) or j >= 2:
                    move_y(j - 2, (s + 2) % D)

            pipeline(dve, steps)
            move_y(SLOT_TILES - 2, D - 2)
            move_y(SLOT_TILES - 1, D - 1)


def combine(nc, x, x_out, y_rows, slot, share):
    with ExitStack() as ctx:
        st = Stage(nc, ctx, "cb")
        idx = st.sb("idx", [P, TOP], U32)
        yg = [st.sb(f"yg{r}", [P, H]) for r in range(TOP)]
        idx_ready = st.sem("idx_ready")
        gathered = [st.sem(f"gathered{r}") for r in range(TOP)]
        used = st.sem("used")
        x_out_s = st.sem("x_out")
        passed = st.sem("passed")
        block = ctx.enter_context(nc.Block())

        @block.gpsimd
        def _(pool):
            def tile(n):
                for r in range(TOP):
                    if not isinstance(n, int):
                        pool.wait_ge(used, TOP * (n - 1) + r + 1)
                    pool.tensor_copy(idx[:, r:r + 1], slot[:, n, r:r + 1]).then_inc(idx_ready, 1)
                    pool.wait_ge(idx_ready, TOP * n + r + 1)
                    pool.sem_inc(passed, 1)
                    pool.indirect_dma_start(yg[r][:, :], None, y_rows,
                                            bass.IndirectOffsetOnAxis(ap=idx[:, r:r + 1], axis=0)).then_inc(gathered[r], 16)

            tile(0)
            with pool.Fori(1, NT) as n:
                for r in range(TOP):
                    pool.wait_ge(gathered[r], 16 * n)
                tile(n)

        @block.vector
        def _(dve):
            with dve.Fori(0, NT) as n:
                for r in range(TOP):
                    dve.wait_ge(gathered[r], 16 * n + 16)
                    if r:
                        dve.wait_ge(used, TOP * n + r)
                    dve.scalar_tensor_tensor(x[:, n, :], yg[r][:, :], share[:, n, r:r + 1], x[:, n, :],
                                             ALU.mult, ALU.add).then_inc(used, 1)

        @block.sync
        def _(sp):
            with sp.Fori(0, NT) as n:
                sp.wait_ge(used, TOP * n + TOP)
                sp.dma_start(x_out.rearrange("(n p) h -> n p h", p=P)[n], x[:, n, :]).then_inc(x_out_s, 16)
            sp.wait_ge(x_out_s, 16 * NT)


STAGES = "ABCDEF"


def columns_of(*vectors):
    return np.ascontiguousarray(np.concatenate([np.asarray(v).reshape(-1, P).T for v in vectors], axis=1))


def build(nc, dram, out):
    res = nc.dram_tensor("residual", (B * T, H), F32, kind="Internal").ap()
    with ExitStack() as ctx:
        ps = ctx.enter_context(nc.psum_tensor("ps", [P, 8, 512], F32))
        ident_t = ctx.enter_context(nc.sbuf_tensor("ident", [P, P], F32))
        ones_t = ctx.enter_context(nc.sbuf_tensor("ones", [P, P], F32))
        identb_t = ctx.enter_context(nc.sbuf_tensor("identb", [P, P], BF16))
        eps_t = ctx.enter_context(nc.sbuf_tensor("eps", [P, 2], F32))
        const_in = ctx.enter_context(nc.semaphore("const_in"))
        const_set = ctx.enter_context(nc.semaphore("const_set"))
        with nc.Block() as block:
            @block.sync
            def _(sp):
                sp.dma_start(ident_t[:, :], dram["identity"]).then_inc(const_in, 16)
                sp.wait_ge(const_in, 16)

            @block.vector
            def _(dve):
                dve.memset(ones_t[:, :], 1.0)
                dve.memset(eps_t[:, 0:1], 1e-5)
                dve.memset(eps_t[:, 1:2], 1e-6)
                dve.wait_ge(const_in, 16)
                dve.tensor_copy(identb_t[:, :], ident_t[:, :]).then_inc(const_set, 1)
                dve.wait_ge(const_set, 1)
        ident, identb, ones = ident_t[:, :], identb_t[:, :], ones_t[:, :]
        eps, eps6 = eps_t[:, 0:1], eps_t[:, 1:2]
        at = dram["x"]
        for s in STAGES:
            to = out if s == STAGES[-1] else res
            if s == "A":
                time_mix(nc, ps, ident, eps, at, to, dram["tm_cols"],
                         {"r": dram["Wr"], "k": dram["Wk"], "v": dram["Wv"], "o": dram["Wo"]})
            elif s == "B":
                memory_attention(nc, ps, ident, eps, at, to, dram["ctx"], dram["ctxT"], dram["mask"])
            elif s == "C":
                ternary_ffn(nc, ps, ident, identb, ones, eps, at, to, dram)
            elif s == "D":
                mamba(nc, ps, ident, eps, at, to, dram)
            elif s == "E":
                context_attention(nc, ps, ident, identb, eps, eps6, at, to, dram)
            elif s == "F":
                experts(nc, ps, ident, ones, eps, at, to, dram)
            at = to


def laid_out(i):
    i = {k: np.asarray(v) for k, v in i.items()}
    d = {
        "x": i["x"].reshape(B * T, H),
        "identity": np.eye(P, dtype=np.float32),
    }
    if "A" in STAGES:
        d["tm_cols"] = columns_of(*(i[f"L0_attn_{n}"] for n in (
            "ln_scale", "ln_bias", "mix_k", "mix_v", "mix_r", "time_first", "time_decay")))
        for n in "rkvo":
            d[f"W{n}"] = i[f"L0_attn_W{n}"]
    if "B" in STAGES or "E" in STAGES:
        d["ctx"] = i["ctx_2048"]
        d["ctxT"] = i["ctx_2048"].transpose(0, 2, 1)
        d["mask"] = i["mask_BxS2_bk0"]
    if "C" in STAGES:
        d |= ffn_inputs(i)
    if "D" in STAGES:
        d |= mamba_inputs(i)
    if "E" in STAGES:
        d |= attention_inputs(i)
    if "F" in STAGES:
        d |= expert_inputs(i)
    return {k: np.ascontiguousarray(v) for k, v in d.items()}


def kernel(**inputs):
    import concourse.bacc as bacc
    from concourse.bass_utils import run_bass_kernel_spmd

    nc = bacc.Bacc("TRN2", target_bir_lowering=False, num_devices=1)
    arrays = laid_out(inputs)
    dram = {n: nc.dram_tensor(f"in_{n}", a.shape, mybir.dt.from_np(a.dtype), kind="ExternalInput").ap()
            for n, a in arrays.items()}
    out = nc.dram_tensor("out", (B * T, H), F32, kind="ExternalOutput").ap()
    build(nc, dram, out)
    r = run_bass_kernel_spmd(nc, [{f"in_{n}": a for n, a in arrays.items()}], core_ids=[0])
    return r.results[0]["out"].reshape(B, T, H)
```

```python
from contextlib import ExitStack

import concourse.bass as bass
import numpy as np
from concourse import mybir

ALU = mybir.AluOpType
ACT = mybir.ActivationFunctionType
AX = mybir.AxisListType
F32 = mybir.dt.float32
BF16 = mybir.dt.bfloat16
U8 = mybir.dt.uint8
U32 = mybir.dt.uint32
I32 = mybir.dt.int32

P = 128
B, T, H = 4, 512, 512
HC = H // P
TT = T // P
NEG = -1e30
ROUND = 1.5 * 2.0**23


class Chain:

    def __init__(self, eng, sem, per=0):
        self.eng, self.sem, self.per, self.base, self.n, self.start = eng, sem, per, 0, 0, None

    def turn(self, i):
        if self.start is None:
            self.start = self.n
        self.base, self.n = self.start + i * self.per, 0

    def inc(self, instruction):
        instruction.then_inc(self.sem, 1)
        self.n += 1

    def wait(self):
        self.eng.wait_ge(self.sem, 1 + self.base + self.n)

    def end(self):
        assert self.n == self.per, f"{self.sem}: {self.n} marks in a turn, not {self.per}"


class Stage:

    def __init__(self, nc, ctx, name, sems=None):
        self.nc, self.ctx, self.name, self.sems, self.from_zero = nc, ctx, name, sems, []
        if sems is None:
            self.sems = []
            ctx.callback(self.clear)

    def clear(self):
        if self.sems:
            self.nc.clear_and_free_semaphores(self.sems)
            self.nc.all_engine_barrier()

    def sb(self, name, shape, dt=F32):
        return self.ctx.enter_context(self.nc.sbuf_tensor(f"{self.name}_{name}", shape, dt))

    def block(self):
        for sem in self.sems:
            if sem not in self.from_zero:
                self.nc.vector.sem_inc(sem, 1)
        self.nc.all_engine_barrier()
        return self.ctx.enter_context(self.nc.Block())

    def sem(self, name, from_zero=False):
        self.sems.append(self.nc.alloc_semaphore(f"{self.name}_{name}"))
        if from_zero:
            self.from_zero.append(self.sems[-1])
        return self.sems[-1]


class Columns:

    def __init__(self, st, ps, ident, eps_col, xT, pad=0):
        st = Stage(st.nc, st.ctx, st.name + "_ln", st.sems)
        self.pause = st.sb("pause", [P, 1])
        self.ps, self.ident, self.eps_col, self.xT, self.pad = ps, ident, eps_col, xT, pad
        self.xn = st.sb("xn", [P, TT, H])
        self.stats = st.sb("stats", [P, TT, 6])
        self.mv = st.sb("mv", [P, TT, 2])
        self.sd = st.sb("sd", [P, TT])
        self.rstd = st.sb("rstd", [P, TT])
        self.var_ready = st.sem("var_ready")
        self.sd_ready = st.sem("sd_ready")
        self.xn_ready = st.sem("xn_ready")
        self.turned = st.sem("turned")
        self.xT_ready = st.sem("xT_ready")

    def statistics(self, dve, chain, rows):
        for i in range(TT):
            chain.inc(dve.bn_stats(self.stats[:, i, :], rows[:, i, :]))
        chain.wait()
        dve.memset(self.pause[:, :], 0.0)
        for i in range(TT):
            last = dve.bn_aggr(self.mv[:, i, :], self.stats[:, i, :])
        return last

    def normalise(self, dve, chain, rows, out):
        chain.inc(dve.reciprocal(self.rstd[:, :], self.sd[:, :]))
        chain.wait()
        for i in range(TT):
            last = dve.tensor_scalar(out[:, i, :], rows[:, i, :], self.mv[:, i, 0:1],
                                     self.rstd[:, i:i + 1], ALU.subtract, ALU.mult)
        return last

    def vector(self, dve, chain, b, rows):
        self.statistics(dve, chain, rows).then_inc(self.var_ready, 1)
        dve.wait_ge(self.sd_ready, 1 + b + 1)
        dve.wait_ge(self.turned, 1 + HC * b)
        self.normalise(dve, chain, rows, self.xn).then_inc(self.xn_ready, 1)

    def scalar_sd(self, act, n):
        act.wait_ge(self.var_ready, 1 + n + 1)
        act.activation(self.sd[:, :], self.mv[:, :, 1], ACT.Sqrt, bias=self.eps_col).then_inc(self.sd_ready, 1)

    def scalar_move(self, act, b, scale=None, bias=None):
        for c in range(HC):
            act.wait_ge(self.turned, 1 + HC * b + c + 1)
            args = {} if scale is None else {"scale": scale[:, c:c + 1], "bias": bias[:, c:c + 1]}
            act.activation(self.xT[:, c, self.pad:self.pad + T], self.ps[:, c % 2, :], ACT.Identity,
                           **args).then_inc(self.xT_ready, 1)

    def tensor(self, pe, b):
        pe.wait_ge(self.xn_ready, 1 + b + 1)
        for c in range(HC):
            pe.wait_ge(self.xT_ready, 1 + HC * b + max(c - 1, 0))
            for i in range(TT):
                last = pe.transpose(self.ps[:, c % 2, i * P:(i + 1) * P],
                                    self.xn[:, i, c * P:(c + 1) * P], self.ident)
            last.then_inc(self.turned, 1)


def rows_of(x, b):
    return x.rearrange("(b i p) h -> b p i h", b=B, p=P)[b]


def time_mix(nc, ps, ident, eps, x_in, x_out, cols, weights):
    n_cols = cols.shape[1]
    with ExitStack() as ctx:
        st = Stage(nc, ctx, "tm")
        x_rows = st.sb("x_rows", [P, TT, H])
        x = st.sb("x", [P, TT, H])
        xl = st.sb("xl", [P, TT, H])
        xT = st.sb("xT", [P, HC, 1 + T])
        step = st.sb("step", [P, HC, T])
        mixed = [st.sb(f"mixed_{n}", [P, HC, T]) for n in "rkv"]
        w = {n: st.sb(f"w{n}", [P, HC, H]) for n in "rkvo"}
        col = st.sb("col", [P, n_cols])
        decay = st.sb("decay", [P, HC])
        r = st.sb("r", [P, HC, T])
        kk = st.sb("kk", [P, 2, T])
        vv = st.sb("vv", [P, 2, T])
        peak = st.sb("peak", [P, 2, 1 + T])
        q = st.sb("q", [P, T])
        ex = st.sb("ex", [P, 2, 4, T])
        ev = st.sb("ev", [P, 2, 2, T])
        sa = st.sb("sa", [P, 1 + T])
        sb_ = st.sb("sbb", [P, 1 + T])
        t1 = st.sb("t1", [P, T])
        t2 = st.sb("t2", [P, T])
        rw = st.sb("rw", [P, HC, T])
        ln = Columns(st, ps, ident, eps, xT, pad=1)
        scale, bias, mix_k, mix_v, mix_r, first, dec = (col[:, HC * j:HC * (j + 1)] for j in range(7))

        col_in, x_in_s, x_out_s = st.sem("col_in"), st.sem("x_in"), st.sem("x_out")
        w_in = {n: st.sem(f"w{n}_in") for n in "rkvo"}
        xl_added = st.sem("xl_added")
        decay_e = st.sem("decay_e")
        mixed_ready = st.sem("mixed_ready")
        proj = st.sem("proj")
        moved = st.sem("moved")
        diffs = st.sem("diffs")
        exps = st.sem("exps")
        ev_ready = st.sem("ev_ready")
        rw_ready = st.sem("rw_ready")
        o_ready = st.sem("o_ready")
        added = st.sem("added")
        xl_ready = st.sem("xl_ready")
        v_own = st.sem("v_own")
        block = st.block()
        order = [(n, d) for d in (0, 1) for n in "kv"] + [("r", d) for d in range(HC)] \
            + [(n, d) for d in (2, 3) for n in "kv"]
        NP = len(order)

        @block.sync
        def _(sp):
            sp.dma_start(x_rows[:, :, :], rows_of(x_in, 0)).then_inc(x_in_s, 16)
            sp.dma_start(col[:, :], cols).then_inc(col_in, 16)
            for n in "kvro":
                sp.dma_start(w[n][:, :, :], weights[n].rearrange("(c p) d -> p c d", p=P)).then_inc(w_in[n], 16)
            with sp.Fori(0, B - 1) as b:
                sp.wait_ge(xl_added, 1 + TT * b + TT)
                sp.dma_start(x_rows[:, :, :], rows_of(x_in, b + 1)).then_inc(x_in_s, 16)
                sp.wait_ge(added, 1 + TT * b + TT)
                sp.dma_start(rows_of(x_out, b), x[:, :, :]).then_inc(x_out_s, 16)
            sp.wait_ge(added, 1 + TT * B)
            sp.dma_start(rows_of(x_out, B - 1), x[:, :, :]).then_inc(x_out_s, 16)
            sp.wait_ge(x_out_s, 1 + 16 * B)

        @block.gpsimd
        def _(pool):
            with pool.Fori(0, B) as b:
                pool.wait_ge(xl_ready, 1 + b + 1)
                pool.wait_ge(x_out_s, 1 + 16 * b)
                for i in range(TT):
                    pool.tensor_tensor(x[:, i, :], x_rows[:, i, :], xl[:, i, :], ALU.add).then_inc(xl_added, 1)
                for d in range(HC):
                    pool.wait_ge(exps, 1 + HC * b + d + 1)
                    pool.wait_ge(rw_ready, 1 + HC * b + max(d - 1, 0))
                    pool.tensor_tensor(ev[:, d % 2, :, :], ex[:, d % 2, 1:4:2, :],
                                       vv[:, d % 2:d % 2 + 1, :].to_broadcast([P, 2, T]), ALU.mult).then_inc(ev_ready, 1)

        @block.scalar
        def _(act):
            act.wait_ge(col_in, 1 + 16)
            act.activation(decay[:, :], dec, ACT.Exp).then_inc(decay_e, 1)

            def columns(b):
                ln.scalar_sd(act, 2 * b)
                ln.scalar_sd(act, 2 * b + 1)
                ln.scalar_move(act, b, scale, bias)

            def batch(b):
                for j, (n, d) in enumerate(order):
                    act.wait_ge(proj, 1 + NP * b + j + 1)
                    bank = ps[:, 2 + j % 6, :]
                    if n == "r":
                        if d == 0:
                            act.wait_ge(rw_ready, 1 + HC * b)
                        act.activation(r[:, d, :], bank, ACT.Sigmoid).then_inc(moved, 1)
                        continue
                    if n == "k" and d >= 2:
                        act.wait_ge(rw_ready, 1 + HC * b + d - 1)
                    act.activation((kk if n == "k" else vv)[:, d % 2, :], bank, ACT.Identity).then_inc(moved, 1)
                    if n == "v":
                        act.wait_ge(diffs, 1 + HC * b + d + 1)
                        act.activation(ex[:, d % 2, :, :], ex[:, d % 2, :, :], ACT.Exp).then_inc(exps, 1)

            columns(0)
            with act.Fori(0, B - 1) as b:
                batch(b)
                columns(b + 1)
            batch(B - 1)

        @block.tensor
        def _(pe):

            def batch(b):
                pe.wait_ge(added, 1 + TT * b)
                for j, (n, d) in enumerate(order):
                    pe.wait_ge(moved, 1 + NP * b + max(j - 5, 0))
                    pe.wait_ge(w_in[n], 1 + 16)
                    pe.wait_ge(mixed_ready, 1 + 3 * b + 1 + "kvr".index(n))
                    for c in range(HC):
                        last = pe.matmul(ps[:, 2 + j % 6, :], w[n][:, c, d * P:(d + 1) * P],
                                         mixed["rkv".index(n)][:, c, :], start=(c == 0), stop=(c == HC - 1))
                    last.then_inc(proj, 1)
                pe.wait_ge(rw_ready, 1 + HC * b + HC)
                pe.wait_ge(moved, 1 + NP * b + NP)
                pe.wait_ge(w_in["o"], 1 + 16)
                for i in range(TT):
                    for c in range(HC):
                        last = pe.matmul(ps[:, 4 + i, :], rw[:, c, i * P:(i + 1) * P], w["o"][:, c, :],
                                         start=(c == 0), stop=(c == HC - 1))
                    last.then_inc(o_ready, 1)

            ln.tensor(pe, 0)
            with pe.Fori(0, B - 1) as b:
                batch(b)
                ln.tensor(pe, b + 1)
            batch(B - 1)

        @block.vector
        def _(dve):
            own = Chain(dve, v_own, 59)
            dve.memset(xT[:, :, 0:1], 0.0)
            dve.memset(peak[:, :, 0:1], 1.0 - 1e30)
            dve.memset(sa[:, 0:1], 0.0)
            dve.memset(sb_[:, 0:1], 0.0)
            dve.wait_ge(decay_e, 2)
            own.inc(dve.tensor_scalar(decay[:, :], decay[:, :], -1.0, None, ALU.mult))

            def exponents(b, d):
                dve.wait_ge(moved, 1 + NP * b + order.index(("v", d)) + 1)
                k, pk, e = kk[:, d % 2, :], peak[:, d % 2, :], ex[:, d % 2, :, :]
                own.inc(dve.tensor_tensor_scan(pk[:, 1:], decay[:, d:d + 1].to_broadcast([P, T]), k,
                                               1.0 - 1e30, ALU.add, ALU.max))
                own.wait()
                own.inc(dve.scalar_tensor_tensor(q[:, :], k, first[:, d:d + 1], pk[:, 0:T], ALU.add, ALU.max))
                dve.scalar_tensor_tensor(e[:, 2, :], pk[:, 0:T], decay[:, d:d + 1], pk[:, 1:], ALU.add, ALU.subtract)
                dve.tensor_tensor(e[:, 3, :], k, pk[:, 1:], ALU.subtract)
                own.wait()
                dve.tensor_tensor(e[:, 0, :], pk[:, 0:T], q[:, :], ALU.subtract)
                dve.scalar_tensor_tensor(e[:, 1, :], k, first[:, d:d + 1], q[:, :],
                                         ALU.add, ALU.subtract).then_inc(diffs, 1)

            def weighted(b, d):
                dve.wait_ge(exps, 1 + HC * b + d + 1)
                e = ex[:, d % 2, :, :]
                own.inc(dve.tensor_tensor_scan(sb_[:, 1:], e[:, 2, :], e[:, 3, :], 0.0, ALU.mult, ALU.add))
                dve.wait_ge(ev_ready, 1 + HC * b + d + 1)
                own.inc(dve.tensor_tensor_scan(sa[:, 1:], e[:, 2, :], ev[:, d % 2, 1, :], 0.0, ALU.mult, ALU.add))
                own.wait()
                own.inc(dve.tensor_tensor(t2[:, :], e[:, 0, :], sb_[:, 0:T], ALU.mult))
                own.inc(dve.tensor_tensor(t1[:, :], e[:, 0, :], sa[:, 0:T], ALU.mult))
                own.wait()
                own.inc(dve.tensor_tensor(t2[:, :], t2[:, :], e[:, 1, :], ALU.add))
                own.inc(dve.tensor_tensor(t1[:, :], t1[:, :], ev[:, d % 2, 0, :], ALU.add))
                own.wait()
                own.inc(dve.scalar_tensor_tensor(q[:, :], t2[:, :], 0.0, t2[:, :], ALU.is_equal, ALU.add))
                own.wait()
                own.inc(dve.reciprocal(q[:, :], q[:, :]))
                own.inc(dve.scalar_tensor_tensor(t1[:, :], t2[:, :], 0.0, t1[:, :], ALU.not_equal, ALU.mult))
                own.wait()
                own.inc(dve.tensor_tensor(t1[:, :], t1[:, :], q[:, :], ALU.mult))
                own.wait()
                if d == 0:
                    dve.wait_ge(o_ready, 1 + TT * b)
                dve.wait_ge(moved, 1 + NP * b + order.index(("r", d)) + 1)
                dve.tensor_tensor(rw[:, d, :], t1[:, :], r[:, d, :], ALU.mult).then_inc(rw_ready, 1)

            def layer_norms(b):
                dve.wait_ge(x_in_s, 1 + 16 * b + 16)
                ln.statistics(dve, own, x_rows).then_inc(ln.var_ready, 1)
                dve.wait_ge(ln.sd_ready, 1 + 2 * b + 1)
                dve.wait_ge(xl_added, 1 + TT * b)
                ln.normalise(dve, own, x_rows, xl).then_inc(xl_ready, 1)
                dve.wait_ge(xl_ready, 1 + b + 1)
                ln.statistics(dve, own, xl).then_inc(ln.var_ready, 1)
                dve.wait_ge(ln.sd_ready, 1 + 2 * b + 2)
                dve.wait_ge(ln.turned, 1 + HC * b)
                ln.normalise(dve, own, xl, ln.xn).then_inc(ln.xn_ready, 1)

            def batch(b, last_one=False):
                dve.wait_ge(ln.xT_ready, 1 + HC * b + HC)
                own.inc(dve.tensor_tensor(step[:, :, :], xT[:, :, 1:], xT[:, :, 0:T], ALU.subtract))
                own.wait()
                for n, mix in ((1, mix_k), (2, mix_v), (0, mix_r)):
                    for c in range(HC):
                        last = dve.scalar_tensor_tensor(mixed[n][:, c, :], step[:, c, :], mix[:, c:c + 1],
                                                        xT[:, c, 0:T], ALU.mult, ALU.add)
                    last.then_inc(mixed_ready, 1)
                exponents(b, 0)
                exponents(b, 1)
                for d in range(HC):
                    weighted(b, d)
                    if d + 2 < HC:
                        exponents(b, d + 2)
                if not last_one:
                    layer_norms(b + 1)
                dve.wait_ge(xl_added, 1 + TT * b + TT)
                for i in range(TT):
                    dve.wait_ge(o_ready, 1 + TT * b + i + 1)
                    dve.tensor_tensor(x[:, i, :], ps[:, 4 + i, :], x[:, i, :], ALU.add).then_inc(added, 1)

            layer_norms(0)
            with dve.Fori(0, B - 1) as b:
                own.turn(b)
                batch(b)
                own.end()
            own.turn(B - 1)
            batch(B - 1, True)


def memory_attention(nc, ps, ident, eps, x_in, x_out, mem, memT, mask):
    MC = T // P
    SCALE = float(H) ** -0.5
    with ExitStack() as ctx:
        st = Stage(nc, ctx, "ma")
        x = st.sb("x", [P, TT, H])
        xT = st.sb("xT", [P, HC, T])
        memory = st.sb("memory", [P, MC, H])
        memoryT = st.sb("memoryT", [P, HC, T])
        mask8 = st.sb("mask8", [P, B, T], U8)
        maskf = st.sb("maskf", [P, T])
        neg = st.sb("neg", [P, T])
        valid = st.sb("valid", [P, 1])
        one_row = st.sb("one_row", [1, P])
        prob = st.sb("prob", [P, 2, T])
        probT = st.sb("probT", [P, 2, MC, P])
        top = st.sb("top", [P, TT])
        ntop = st.sb("ntop", [P, TT])
        total = st.sb("total", [P, TT])
        inv = st.sb("inv", [P, TT])
        ln = Columns(st, ps, ident, eps, xT)
        x_in_s, x_out_s, rows_in = st.sem("x_in"), st.sem("x_out"), st.sem("rows_in")
        memT_in, mem_in, mask_in = st.sem("memT_in"), st.sem("mem_in"), st.sem("mask_in")
        set_up = st.sem("set_up")
        neg_ready = st.sem("neg_ready")
        scores = st.sem("scores")
        tops = st.sem("tops")
        probs = st.sem("probs")
        pT_psum = st.sem("pT_psum")
        pT_ready = st.sem("pT_ready")
        o_ready = st.sem("o_ready")
        added = st.sem("added")
        v_own = st.sem("v_own")
        block = st.block()

        @block.sync
        def _(sp):
            def load_rows(b):
                sp.dma_start(ln.xn[:, :, :], rows_of(x_in, b)).then_inc(rows_in, 16)

            def load_columns(b):
                sp.dma_start(memoryT[:, :, :], memT.rearrange("b (c p) m -> b p c m", p=P)[b]).then_inc(memT_in, 16)

            def load_memory(b):
                sp.dma_start(memory[:, :, :], mem.rearrange("b (c p) d -> b p c d", p=P)[b]).then_inc(mem_in, 16)

            load_rows(0)
            sp.dma_start(mask8[:, :, :], mask.rearrange("(a b) m -> a b m", a=1).to_broadcast([P, B, T])).then_inc(mask_in, 16)
            load_columns(0)
            load_memory(0)
            sp.dma_start(x[:, :, :], rows_of(x_in, 0)).then_inc(x_in_s, 16)
            with sp.Fori(0, B - 1) as b:
                sp.wait_ge(ln.turned, 1 + HC * b + HC)
                load_rows(b + 1)
                sp.wait_ge(scores, 1 + TT * b + TT)
                load_columns(b + 1)
                sp.wait_ge(o_ready, 1 + TT * b + TT)
                load_memory(b + 1)
                sp.wait_ge(added, 1 + TT * b + TT)
                sp.dma_start(rows_of(x_out, b), x[:, :, :]).then_inc(x_out_s, 16)
                sp.wait_ge(x_out_s, 1 + 16 * b + 16)
                sp.dma_start(x[:, :, :], rows_of(x_in, b + 1)).then_inc(x_in_s, 16)
            sp.wait_ge(added, 1 + TT * B)
            sp.dma_start(rows_of(x_out, B - 1), x[:, :, :]).then_inc(x_out_s, 16)
            sp.wait_ge(x_out_s, 1 + 16 * B)

        @block.scalar
        def _(act):
            def batch(b, last_one=False):
                for i in range(TT):
                    act.wait_ge(tops, 1 + TT * b + i + 1)
                    act.wait_ge(pT_psum, 1 + TT * b + max(i - 1, 0))
                    act.activation(prob[:, i % 2, :], ps[:, 2 + i % 2, :], ACT.Exp, bias=ntop[:, i:i + 1],
                                   scale=SCALE, accum_out=total[:, i:i + 1]).then_inc(probs, 1)
                    act.wait_ge(pT_psum, 1 + TT * b + i + 1)
                    act.wait_ge(o_ready, 1 + TT * b + max(i - 1, 0))
                    act.activation(probT[:, i % 2, :, :], ps[:, 4 + i % 2, :], ACT.Identity).then_inc(pT_ready, 1)
                    if i == 1 and not last_one:
                        ln.scalar_sd(act, b + 1)

            ln.scalar_sd(act, 0)
            ln.scalar_move(act, 0)
            with act.Fori(0, B - 1) as b:
                batch(b)
                ln.scalar_move(act, b + 1)
            batch(B - 1, True)

        @block.tensor
        def _(pe):
            pe.wait_ge(set_up, 2)

            def batch(b):
                pe.wait_ge(memT_in, 1 + 16 * b + 16)
                pe.wait_ge(neg_ready, 1 + b + 1)
                pe.wait_ge(ln.xT_ready, 1 + HC * b + HC)

                def score(i):
                    pe.wait_ge(probs, 1 + TT * b + max(i - 1, 0))
                    pe.matmul(ps[:, 2 + i % 2, :], one_row[:, :], neg[0:1, :], start=True, stop=False)
                    for c in range(HC):
                        last = pe.matmul(ps[:, 2 + i % 2, :], xT[:, c, i * P:(i + 1) * P], memoryT[:, c, :],
                                         start=False, stop=(c == HC - 1))
                    last.then_inc(scores, 1)

                score(0)
                for i in range(TT):
                    if i + 1 < TT:
                        score(i + 1)
                    pe.wait_ge(probs, 1 + TT * b + i + 1)
                    pe.wait_ge(pT_ready, 1 + TT * b + max(i - 1, 0))
                    for m in range(MC):
                        last = pe.transpose(ps[:, 4 + i % 2, m * P:(m + 1) * P],
                                            prob[:, i % 2, m * P:(m + 1) * P], ident)
                    last.then_inc(pT_psum, 1)
                    pe.wait_ge(pT_ready, 1 + TT * b + i + 1)
                    pe.wait_ge(mem_in, 1 + 16 * b + 16)
                    pe.wait_ge(added, 1 + TT * b + max(i - 1, 0))
                    for m in range(MC):
                        last = pe.matmul(ps[:, 6 + i % 2, :], probT[:, i % 2, m, :], memory[:, m, :],
                                         start=(m == 0), stop=(m == MC - 1))
                    last.then_inc(o_ready, 1)

            ln.tensor(pe, 0)
            with pe.Fori(0, B - 1) as b:
                batch(b)
                ln.tensor(pe, b + 1)
            batch(B - 1)

        @block.vector
        def _(dve):
            own = Chain(dve, v_own, 19)
            dve.memset(one_row[:, :], 1.0).then_inc(set_up, 1)
            def layer_norm_start(b):
                dve.wait_ge(rows_in, 1 + 16 * b + 16)
                ln.statistics(dve, own, ln.xn).then_inc(ln.var_ready, 1)

            def layer_norm_end(b):
                dve.wait_ge(ln.sd_ready, 1 + b + 1)
                ln.normalise(dve, own, ln.xn, ln.xn).then_inc(ln.xn_ready, 1)

            def mask_row(b):
                dve.wait_ge(mask_in, 1 + 16)
                own.inc(dve.tensor_copy(maskf[:, :], mask8[:, b, :]))
                own.wait()
                dve.wait_ge(scores, 1 + TT * b)
                own.inc(dve.tensor_scalar(neg[:, :], maskf[:, :], -NEG, NEG, ALU.mult, ALU.add))
                dve.tensor_reduce(valid[:, :], maskf[:, :], AX.X, ALU.max).then_inc(neg_ready, 1)

            def batch(b, last_one=False):
                def finish(i):
                    dve.wait_ge(probs, 1 + TT * b + i + 1)
                    own.inc(dve.reciprocal(inv[:, i:i + 1], total[:, i:i + 1]))
                    own.wait()
                    own.inc(dve.tensor_scalar(inv[:, i:i + 1], inv[:, i:i + 1], valid[:, 0:1], None, ALU.mult))
                    own.wait()
                    dve.wait_ge(o_ready, 1 + TT * b + i + 1)
                    dve.wait_ge(x_in_s, 1 + 16 * b + 16)
                    dve.scalar_tensor_tensor(x[:, i, :], ps[:, 6 + i % 2, :], inv[:, i:i + 1], x[:, i, :],
                                             ALU.mult, ALU.add).then_inc(added, 1)

                for i in range(TT):
                    dve.wait_ge(scores, 1 + TT * b + i + 1)
                    own.inc(dve.tensor_reduce(top[:, i:i + 1], ps[:, 2 + i % 2, :], AX.X, ALU.max))
                    own.wait()
                    dve.tensor_scalar(ntop[:, i:i + 1], top[:, i:i + 1], -SCALE, None, ALU.mult).then_inc(tops, 1)
                    if i:
                        finish(i - 1)
                    if i == 1 and not last_one:
                        layer_norm_start(b + 1)
                    if i == TT - 1 and not last_one:
                        layer_norm_end(b + 1)
                finish(TT - 1)
                if not last_one:
                    mask_row(b + 1)

            layer_norm_start(0)
            layer_norm_end(0)
            mask_row(0)
            with dve.Fori(0, B - 1) as b:
                own.turn(b)
                batch(b)
                own.end()
            own.turn(B - 1)
            batch(B - 1, True)


F_IN = 2048
FC = F_IN // P


def ffn_inputs(i):
    return {
        "w1T": i["L0_ffn_w1"].T,
        "w2T": i["L0_ffn_w2"].T,
        "ffn_rows": np.stack([i["L0_ffn_b1"], i["L0_ffn_ln_g"], i["L0_ffn_ln_b"]]),
        "ffn_b2": i["L0_ffn_b2"].reshape(1, H),
    }


def ternary_ffn(nc, ps, ident, identb, ones, eps, x_in, x_out, dram):
    with ExitStack() as ctx:
        st = Stage(nc, ctx, "ff")
        tern = {"w1T": st.sb("tern_w1T", [P, HC, F_IN], BF16), "w2T": st.sb("tern_w2T", [P, FC, H], BF16)}
        mean_w = st.sb("mean_w", [P, 2])
        inv_w = st.sb("inv_w", [P, 2])
        w1_sums = st.sb("w1_sums", [P, HC])
        w_sums = st.sb("w_sums", [P, 2])
        x = st.sb("x", [P, TT, H])
        rows = st.sb("rows", [P, 3, F_IN])
        b2 = st.sb("b2", [P, H])
        h = st.sb("h", [P, TT, F_IN])
        g = st.sb("g", [P, TT, F_IN])
        raw = {"w1T": h[:, :, :], "w2T": g[:, :, :].rearrange("p i (c o) -> p (i c) o", o=H)}
        q1 = st.sb("q1", [P, TT, H], BF16)
        q1T = st.sb("q1T", [P, HC, T], BF16)
        q2 = st.sb("q2", [P, 2, F_IN], BF16)
        q2T = st.sb("q2T", [P, 2, FC, P], BF16)
        stats = st.sb("stats", [P, TT, F_IN // 512, 6])
        mv = st.sb("mv", [P, TT, 2])
        pause = st.sb("pause", [P, 1])
        sd, rstd = st.sb("sd", [P, TT]), st.sb("rstd", [P, TT])
        ln = Columns(st, ps, ident, eps, None)
        x_in_s, x_out_s, rows_in = st.sem("x_in"), st.sem("x_out"), st.sem("rows_in")
        ln_in = st.sem("ln_in")

        class Quantiser:
            def __init__(self, k, n, mean):
                name = st.name + f"_quant{k}"
                q = Stage(nc, ctx, name, st.sems)
                self.n, self.mean = n, mean
                self.scrap = q.sb("scrap", [P, n], BF16)
                self.ss, self.rms, self.amax, self.step, self.f, self.c = (
                    q.sb(v, [P, TT]) for v in ("ss", "rms", "amax", "step", "f", "c"))
                self.squares = q.sem("squares")
                self.rms_ready = q.sem("rms_ready")
                self.clipped = q.sem("clipped")
                self.q_ready = q.sem("q_ready")
                self.turned = q.sem("turned")
                self.moved = q.sem("moved")

            def square(self, act, b, v, i):
                act.wait_ge(self.squares, 1 + TT * b + i)
                act.activation(self.scrap[:, :], v[:, i, :], ACT.Square,
                               accum_out=self.ss[:, i:i + 1]).then_inc(self.squares, 1)

            def root(self, act, b):
                act.wait_ge(self.squares, 1 + TT * b + TT)
                act.activation(self.rms[:, :], self.ss[:, :], ACT.Sqrt, bias=eps,
                               scale=1.0 / self.n).then_inc(self.rms_ready, 1)

            def largest(self, dve, own, v, i):
                own.inc(dve.tensor_reduce(self.amax[:, i:i + 1], v[:, i, :], AX.X, ALU.max,
                                          apply_absolute_value=True))

            def factors(self, dve, own, b):
                dve.wait_ge(self.rms_ready, 1 + b + 1)
                own.inc(dve.reciprocal(self.rms[:, :], self.rms[:, :]))
                own.wait()
                own.inc(dve.tensor_tensor(self.step[:, :], self.amax[:, :], self.rms[:, :], ALU.mult))
                own.wait()
                own.inc(dve.tensor_scalar(self.step[:, :], self.step[:, :], 1e-5, 1.0 / 127.0, ALU.max, ALU.mult))
                own.wait()
                own.inc(dve.reciprocal(self.f[:, :], self.step[:, :]))
                own.inc(dve.tensor_scalar(self.c[:, :], self.step[:, :], self.mean, None, ALU.mult))
                own.wait()
                own.inc(dve.tensor_tensor(self.f[:, :], self.f[:, :], self.rms[:, :], ALU.mult))
                own.wait()

            def to_grid(self, dve, own, v, i):
                own.inc(dve.tensor_scalar(v[:, i, :], v[:, i, :], self.f[:, i:i + 1], ROUND, ALU.mult, ALU.add))
                own.wait()
                dve.tensor_scalar(v[:, i, :], v[:, i, :], ROUND - 128.0, ROUND + 127.0,
                                  ALU.max, ALU.min).then_inc(self.clipped, 1)

        first = Quantiser(1, H, mean_w[:, 0:1])
        second = Quantiser(2, F_IN, mean_w[:, 1:2])
        w_in = [st.sem("w1_in"), st.sem("w2_in")]
        w1_summed = st.sem("w1_summed")
        w_summed = [st.sem("w1_all"), st.sem("w2_all")]
        w_total = [st.sem("w1_total"), st.sem("w2_total")]
        w_rounded = [st.sem("w1_rounded"), st.sem("w2_rounded")]
        w_done = [st.sem("w1_done"), st.sem("w2_done")]
        b2_added = st.sem("b2_added")
        h_psum = st.sem("h_psum")
        h_raw = st.sem("h_raw")
        silu_done = st.sem("silu_done")
        h_act = st.sem("h_act")
        var2 = st.sem("var2")
        sd2 = st.sem("sd2")
        h_norm = st.sem("h_norm")
        h_ln = st.sem("h_ln")
        o_ready, added = st.sem("o_ready"), st.sem("added")
        v_own, g_own = st.sem("v_own"), st.sem("g_own")
        block = st.block()
        HALF = F_IN // 2


        @block.sync
        def _(sp):
            sp.dma_start(ln.xn[:, :, :], rows_of(x_in, 0)).then_inc(ln_in, 16)
            sp.dma_start(raw["w1T"], dram["w1T"].rearrange("(c p) o -> p c o", p=P)).then_inc(w_in[0], 16)
            sp.dma_start(raw["w2T"], dram["w2T"].rearrange("(c p) o -> p c o", p=P)).then_inc(w_in[1], 16)
            sp.dma_start(rows[:, :, :], dram["ffn_rows"].rearrange("(a r) o -> a r o", a=1)
                         .to_broadcast([P, 3, F_IN])).then_inc(rows_in, 16)
            sp.dma_start(b2[:, :], dram["ffn_b2"].to_broadcast([P, H])).then_inc(rows_in, 16)
            sp.dma_start(x[:, :, :], rows_of(x_in, 0)).then_inc(x_in_s, 16)

            def load_rows(b):
                sp.wait_ge(first.q_ready, 1 + TT * b)
                sp.dma_start(ln.xn[:, :, :], rows_of(x_in, b)).then_inc(ln_in, 16)

            def renew_x(b):
                sp.wait_ge(added, 1 + TT * b + TT)
                sp.dma_start(rows_of(x_out, b), x[:, :, :]).then_inc(x_out_s, 16)
                sp.wait_ge(x_out_s, 1 + 16 * b + 16)
                sp.dma_start(x[:, :, :], rows_of(x_in, b + 1)).then_inc(x_in_s, 16)

            load_rows(1)
            with sp.Fori(0, B - 2) as b:
                load_rows(b + 2)
                renew_x(b)
            renew_x(B - 2)
            sp.wait_ge(added, 1 + TT * B)
            sp.dma_start(rows_of(x_out, B - 1), x[:, :, :]).then_inc(x_out_s, 16)
            sp.wait_ge(x_out_s, 1 + 16 * B)

        @block.gpsimd
        def _(pool):
            own = Chain(pool, g_own, TT)
            pool.wait_ge(rows_in, 33)
            with pool.Fori(0, B) as b:
                own.turn(b)
                for i in range(TT):
                    pool.wait_ge(h_norm, 1 + TT * b + i + 1)
                    own.inc(pool.tensor_tensor(g[:, i, :], g[:, i, :], rows[:, 1, :], ALU.mult))
                    own.wait()
                    pool.tensor_tensor(g[:, i, :], g[:, i, :], rows[:, 2, :], ALU.add).then_inc(h_ln, 1)
                pool.wait_ge(x_in_s, 1 + 16 * b + 16)
                for i in range(TT):
                    pool.tensor_tensor(x[:, i, :], x[:, i, :], b2[:, :], ALU.add).then_inc(b2_added, 1)
                own.end()

        @block.scalar
        def _(act):
            def ternary(k, n):
                act.wait_ge(w_rounded[k], 2)
                act.activation(tern[n][:, :, :], raw[n], ACT.Copy, bias=-ROUND).then_inc(w_done[k], 1)

            def quantise_rows(b):
                ln.scalar_sd(act, b)
                if isinstance(b, int) and b == 0:
                    act.wait_ge(w_in[0], 17)
                    for c in range(HC):
                        act.wait_ge(w1_summed, 1 + c)
                        act.activation(second.scrap[:, :], raw["w1T"][:, c, :], ACT.Abs,
                                       accum_out=w1_sums[:, c:c + 1]).then_inc(w1_summed, 1)
                act.wait_ge(ln.xn_ready, 1 + b + 1)
                for i in range(TT):
                    first.square(act, b, ln.xn, i)
                first.root(act, b)
                for i in range(TT):
                    act.wait_ge(first.clipped, 1 + TT * b + i + 1)
                    act.wait_ge(first.turned, 1 + 2 * b)
                    act.activation(q1[:, i, :], ln.xn[:, i, :], ACT.Copy, bias=-ROUND).then_inc(first.q_ready, 1)
                if isinstance(b, int) and b == 0:
                    ternary(0, "w1T")
                for k in range(2):
                    act.wait_ge(first.turned, 1 + 2 * b + k + 1)
                    act.wait_ge(h_psum, 1 + 2 * TT * b)
                    act.activation(q1T[:, 2 * k:2 * k + 2, :], ps[:, 4 + k, :].bitcast(BF16),
                                   ACT.Copy).then_inc(first.moved, 1)

            def first_half(b):
                for i in range(TT):
                    act.wait_ge(h_raw, 1 + 2 * TT * b + 2 * i + 2)
                    act.activation(h[:, i, :], h[:, i, :], ACT.Silu).then_inc(silu_done, 1)
                for i in range(TT):
                    act.wait_ge(silu_done, 1 + TT * b + i + 1)
                    act.activation(h[:, i, :], h[:, i, :], ACT.Gelu).then_inc(h_act, 1)
                if isinstance(b, int) and b == 0:
                    ternary(1, "w2T")
                act.wait_ge(var2, 1 + b + 1)
                act.activation(sd[:, :], mv[:, :, 1], ACT.Sqrt, bias=eps).then_inc(sd2, 1)

            def second_half(b):
                for i in range(TT):
                    act.wait_ge(h_ln, 1 + TT * b + i + 1)
                    second.square(act, b, g, i)
                second.root(act, b)
                for i in range(TT):
                    act.wait_ge(second.clipped, 1 + TT * b + i + 1)
                    act.wait_ge(second.turned, 1 + 2 * TT * b + max(2 * (i - 1), 0))
                    act.activation(q2[:, i % 2, :], g[:, i, :], ACT.Copy, bias=-ROUND).then_inc(second.q_ready, 1)
                    for k in range(2):
                        act.wait_ge(second.turned, 1 + 2 * TT * b + 2 * i + k + 1)
                        act.wait_ge(o_ready, 1 + TT * b + max(i - 1, 0))
                        act.activation(q2T[:, i % 2, 8 * k:8 * k + 8, :], ps[:, 4 + k, :].bitcast(BF16),
                                       ACT.Copy).then_inc(second.moved, 1)

            quantise_rows(0)
            first_half(0)
            quantise_rows(1)
            with act.Fori(0, B - 2) as b:
                first_half(b + 1)
                second_half(b)
                quantise_rows(b + 2)
            first_half(B - 1)
            second_half(B - 2)
            second_half(B - 1)

        @block.tensor
        def _(pe):
            def total(k):
                pe.wait_ge(w_summed[k], 2)
                pe.matmul(ps[:, 6 + k, 0:1], ones, w_sums[:, k:k + 1], start=True, stop=True).then_inc(w_total[k], 1)

            def quantise_rows(b, second_done):
                if isinstance(b, int) and b == 0:
                    total(0)
                pe.wait_ge(first.q_ready, 1 + TT * b + TT)
                pe.wait_ge(second.moved, 1 + 2 * TT * second_done)
                for k in range(2):
                    for c in range(2 * k, 2 * k + 2):
                        for i in range(TT):
                            last = pe.transpose(
                                ps[:, 4 + k, :].bitcast(BF16)[:, (c % 2 * TT + i) * P:(c % 2 * TT + i + 1) * P],
                                q1[:, i, c * P:(c + 1) * P], identb)
                    last.then_inc(first.turned, 1)

            def first_half(b):
                pe.wait_ge(first.moved, 1 + 2 * b + 2)
                if isinstance(b, int) and b == 0:
                    total(1)
                    pe.wait_ge(w_done[0], 2)
                for i in range(TT):
                    for k in range(2):
                        pe.wait_ge(h_raw, 1 + 2 * TT * b + max(2 * i + k - 1, 0))
                        for n in range(2 * k, 2 * k + 2):
                            for c in range(HC):
                                last = pe.matmul(ps[:, n, :], q1T[:, c, i * P:(i + 1) * P],
                                                 tern["w1T"][:, c, n * 512:(n + 1) * 512],
                                                 start=(c == 0), stop=(c == HC - 1))
                        last.then_inc(h_psum, 1)

            def second_half(b, first_done):
                for i in range(TT):
                    pe.wait_ge(second.q_ready, 1 + TT * b + i + 1)
                    for k in range(2):
                        pe.wait_ge(first.moved, 1 + 2 * first_done)
                        pe.wait_ge(second.moved, 1 + 2 * TT * b + max(2 * i + k - 1, 0))
                        for c in range(8):
                            last = pe.transpose(ps[:, 4 + k, :].bitcast(BF16)[:, c * P:(c + 1) * P],
                                                q2[:, i % 2, (8 * k + c) * P:(8 * k + c + 1) * P], identb)
                        last.then_inc(second.turned, 1)
                    pe.wait_ge(second.moved, 1 + 2 * TT * b + 2 * i + 2)
                    pe.wait_ge(added, 1 + TT * b + max(i - 1, 0))
                    for c in range(FC):
                        last = pe.matmul(ps[:, 6 + i % 2, :], q2T[:, i % 2, c, :], tern["w2T"][:, c, :],
                                         start=(c == 0), stop=(c == FC - 1))
                    last.then_inc(o_ready, 1)

            quantise_rows(0, 0)
            first_half(0)
            pe.wait_ge(w_done[1], 2)
            quantise_rows(1, 0)
            with pe.Fori(0, B - 2) as b:
                first_half(b + 1)
                second_half(b, b + 2)
                quantise_rows(b + 2, b + 1)
            first_half(B - 1)
            second_half(B - 2, B)
            second_half(B - 1, B)

        @block.vector
        def _(dve):
            own = Chain(dve, v_own, 50)

            def ternary_grid(k, n):
                dve.wait_ge(w_total[k], 2)
                m = mean_w[:, k:k + 1]
                own.inc(dve.tensor_scalar(m, ps[:, 6 + k, 0:1], 1.0 / (F_IN * H), 1e-5, ALU.mult, ALU.max))
                own.wait()
                own.inc(dve.reciprocal(inv_w[:, k:k + 1], m))
                own.wait()
                own.inc(dve.tensor_scalar(raw[n], raw[n], inv_w[:, k:k + 1], ROUND, ALU.mult, ALU.add))
                own.wait()
                dve.tensor_scalar(raw[n], raw[n], ROUND - 1.0, ROUND + 1.0, ALU.max, ALU.min).then_inc(w_rounded[k], 1)

            def statistics(b):
                dve.wait_ge(ln_in, 1 + 16 * b + 16)
                ln.statistics(dve, own, ln.xn).then_inc(ln.var_ready, 1)

            def quantise_rows(b):
                dve.wait_ge(ln.sd_ready, 1 + b + 1)
                ln.normalise(dve, own, ln.xn, ln.xn).then_inc(ln.xn_ready, 1)
                dve.wait_ge(ln.xn_ready, 1 + b + 1)
                for i in range(TT):
                    first.largest(dve, own, ln.xn, i)
                if isinstance(b, int) and b == 0:
                    dve.wait_ge(w1_summed, 1 + HC)
                    dve.tensor_reduce(w_sums[:, 0:1], w1_sums[:, :], AX.X, ALU.add).then_inc(w_summed[0], 1)
                    ternary_grid(0, "w1T")
                    dve.wait_ge(w_in[1], 17)
                    dve.tensor_reduce(w_sums[:, 1:2], g[:, :, :].rearrange("p i o -> p (i o)"), AX.X, ALU.add,
                                      apply_absolute_value=True).then_inc(w_summed[1], 1)
                first.factors(dve, own, b)
                for i in range(TT):
                    first.to_grid(dve, own, ln.xn, i)

            def first_half(b, between):
                dve.wait_ge(rows_in, 33)
                for i in range(TT):
                    for k in range(2):
                        dve.wait_ge(h_psum, 1 + 2 * TT * b + 2 * i + k + 1)
                        dve.scalar_tensor_tensor(h[:, i, k * HALF:(k + 1) * HALF],
                                                 ps[:, 2 * k:2 * k + 2, :].rearrange("p a n -> p (a n)"),
                                                 first.c[:, i:i + 1], rows[:, 0, k * HALF:(k + 1) * HALF],
                                                 ALU.mult, ALU.add).then_inc(h_raw, 1)
                    between(i)
                for i in range(TT):
                    dve.wait_ge(h_act, 1 + TT * b + i + 1)
                    for n in range(F_IN // 512):
                        own.inc(dve.bn_stats(stats[:, i, n, :], h[:, i, n * 512:(n + 1) * 512]))
                own.wait()
                dve.memset(pause[:, :], 0.0)
                for i in range(TT):
                    last = dve.bn_aggr(mv[:, i, :], stats[:, i, :, :].rearrange("p a s -> p (a s)"))
                last.then_inc(var2, 1)

            def normalise(b):
                dve.wait_ge(sd2, 1 + b + 1)
                own.inc(dve.reciprocal(rstd[:, :], sd[:, :]))
                own.wait()
                for i in range(TT):
                    dve.wait_ge(second.q_ready, 1 + TT * b - TT + i + 1 if not isinstance(b, int) or b else 1)
                    dve.tensor_scalar(g[:, i, :], h[:, i, :], mv[:, i, 0:1], rstd[:, i:i + 1],
                                      ALU.subtract, ALU.mult).then_inc(h_norm, 1)

            def largest(b, i):
                dve.wait_ge(h_ln, 1 + TT * b + i + 1)
                second.largest(dve, own, g, i)

            def quantise(b):
                second.factors(dve, own, b)
                for i in range(TT):
                    second.to_grid(dve, own, g, i)

            def add(b):
                for i in range(TT):
                    dve.wait_ge(o_ready, 1 + TT * b + i + 1)
                    dve.wait_ge(b2_added, 1 + TT * b + TT)
                    dve.scalar_tensor_tensor(x[:, i, :], ps[:, 6 + i % 2, :], second.c[:, i:i + 1], x[:, i, :],
                                             ALU.mult, ALU.add).then_inc(added, 1)

            statistics(0)
            quantise_rows(0)
            first_half(0, lambda i: ternary_grid(1, "w2T") if i == TT - 1 else None)
            dve.wait_ge(w_done[1], 2)
            normalise(0)
            statistics(1)
            quantise_rows(1)
            with dve.Fori(0, B - 2) as b:
                own.turn(b)
                first_half(b + 1, lambda i: largest(b, i))
                quantise(b)
                normalise(b + 1)
                statistics(b + 2)
                add(b)
                quantise_rows(b + 2)
                own.end()
            own.turn(B - 2)
            first_half(B - 1, lambda i: largest(B - 2, i))
            quantise(B - 2)
            normalise(B - 1)
            add(B - 2)
            for i in range(TT):
                largest(B - 1, i)
            quantise(B - 1)
            add(B - 1)


DI, NS, RK, KC = 1024, 16, 128, 4
DC = DI // P


def mamba_inputs(i):
    per_channel = np.concatenate(
        [i["L1_attn_Wconv"].reshape(DI, KC)] + [i[f"L1_attn_{n}"].reshape(DI, 1) for n in ("bconv", "D", "bdt")]
        + [i["L1_attn_A_log"]], axis=1)
    return {
        "mb_cols": per_channel.reshape(DC, P, KC + 3 + NS).transpose(1, 0, 2),
        "WinT": i["L1_attn_Win"].T,
        "WxT": i["L1_attn_Wx"].T,
        "WdtT": i["L1_attn_Wdt"].T,
        "WoutT": i["L1_attn_Wout"].T,
    }


def mamba(nc, ps, ident, eps, x_in, x_out, dram):
    with ExitStack() as ctx:
        st = Stage(nc, ctx, "mb")
        xT = st.sb("xT", [P, HC, T])
        ln = Columns(st, ps, ident, eps, xT)
        w_in = st.sb("w_in", [P, HC, 2 * DI])
        w_x = st.sb("w_x", [P, DC, RK + 2 * NS])
        w_dt = st.sb("w_dt", [P, DI])
        w_out = st.sb("w_out", [P, DC, H])
        col = st.sb("col", [P, DC, KC + 3 + NS])
        taps, bconv, skip, bdt = col[:, :, 0:KC], col[:, :, KC], col[:, :, KC + 1], col[:, :, KC + 2]
        neg_a = st.sb("neg_a", [P, DC, NS])
        hs = st.sb("hs", [P, DC, T])
        gate = st.sb("gate", [P, DC, T])
        bcs = st.sb("bcs", [P, 2 * NS, T])
        dt = st.sb("dt", [P, DC, T])
        u = st.sb("u", [P, 2, T])
        dt_in, bc = u[:, 0, :], u[0:2 * NS, 1, :]
        db = [st.sb("db0", [P, 4, T]), st.sb("db1", [P, 4, T])]
        soft = db
        x = db[0]
        hc = ln.xn
        col_in, x_in_s, x_out_s = st.sem("col_in"), st.sem("x_in"), st.sem("x_out")
        w_in_in, w_x_in, w_out_in = st.sem("w_in_in"), st.sem("w_x_in"), st.sem("w_out_in")
        rows_in = st.sem("rows_in")
        a_exp, a_ready = st.sem("a_exp"), st.sem("a_ready")
        hs_psum, conv_done, hs_ready = st.sem("hs_psum"), st.sem("conv_done"), st.sem("hs_ready")
        gate_psum = st.sem("gate_psum")
        gate_moved = st.sem("gate_moved")
        gate_ready = st.sem("gate_ready")
        ssm_psum = st.sem("ssm_psum")
        ssm_moved = st.sem("ssm_moved")
        dt_psum = st.sem("dt_psum")
        dt_z = st.sem("dt_z")
        dt_abs = st.sem("dt_abs")
        dt_e = st.sem("dt_e")
        dt_log = st.sem("dt_log")
        dt_ready = st.sem("dt_ready")
        u_ready = st.sem("u_ready")
        db_ready = st.sem("db_ready")
        da_ready = st.sem("da_ready")
        scanned = st.sem("scanned")
        hc_ready = st.sem("hc_ready")
        summed = st.sem("summed")
        y_read = st.sem("y_read")
        yg_ready = st.sem("yg_ready")
        o_ready, added, v_own = st.sem("o_ready"), st.sem("added"), st.sem("v_own")
        block = st.block()
        NU = DC * NS
        NB = 2 + 2 * NS

        @block.sync
        def _(sp):
            sp.dma_start(ln.xn[:, :, :], rows_of(x_in, 0)).then_inc(rows_in, 16)
            sp.dma_start(col[:, :, :], dram["mb_cols"]).then_inc(col_in, 16)
            sp.dma_start(w_in[:, :, :], dram["WinT"].rearrange("(c p) e -> p c e", p=P)).then_inc(w_in_in, 16)
            sp.dma_start(w_x[:, :, :], dram["WxT"].rearrange("(c p) e -> p c e", p=P)).then_inc(w_x_in, 16)
            sp.dma_start(w_dt[:, :], dram["WdtT"]).then_inc(w_x_in, 16)
            sp.dma_start(w_out[:, :, :], dram["WoutT"].rearrange("(c p) e -> p c e", p=P)).then_inc(w_out_in, 16)
            with sp.Fori(0, B - 1) as b:
                sp.wait_ge(summed, 1 + NU * (b + 1))
                sp.dma_start(ln.xn[:, :, :], rows_of(x_in, b + 1)).then_inc(rows_in, 16)
                sp.dma_start(x[:, :, :], rows_of(x_in, b)).then_inc(x_in_s, 16)
                sp.wait_ge(added, 1 + TT * b + TT)
                sp.dma_start(rows_of(x_out, b), x[:, :, :]).then_inc(x_out_s, 16)
            sp.wait_ge(summed, 1 + NU * B)
            sp.dma_start(x[:, :, :], rows_of(x_in, B - 1)).then_inc(x_in_s, 16)
            sp.wait_ge(added, 1 + TT * B)
            sp.dma_start(rows_of(x_out, B - 1), x[:, :, :]).then_inc(x_out_s, 16)
            sp.wait_ge(x_out_s, 1 + 16 * B)

        @block.gpsimd
        def _(pool):
            with pool.Fori(0, B) as b:
                pool.wait_ge(ssm_moved, 1 + NB * b + NB)
                for d in range(DC):
                    pool.wait_ge(u_ready, 1 + DC * b + d + 1)
                    for g in range(NS // 4):
                        k = 4 * d + g
                        pool.wait_ge(scanned, 1 + NU * b + max(4 * (k - 1), 0))
                        pool.tensor_tensor(db[k % 2][:, :, :],
                                           u[:, d % 2, :].rearrange("p (a t) -> p a t", a=1).to_broadcast([P, 4, T]),
                                           bcs[:, 4 * g:4 * g + 4, :], ALU.mult).then_inc(db_ready, 1)

        @block.scalar
        def _(act):
            act.wait_ge(col_in, 17)
            act.activation(neg_a[:, :, :], col[:, :, KC + 3:], ACT.Exp).then_inc(a_exp, 1)

            def columns(b):
                ln.scalar_sd(act, b)
                act.wait_ge(gate_psum, 1 + DC * b)
                ln.scalar_move(act, b)

            def batch(b):
                for c in range(DC):
                    act.wait_ge(conv_done, 1 + DC * b + c + 1)
                    act.activation(hs[:, c, :], hs[:, c, :], ACT.Silu, bias=bconv[:, c:c + 1]).then_inc(hs_ready, 1)
                act.wait_ge(hc_ready, 1 + NU * b)
                act.wait_ge(scanned, 1 + NU * b)
                act.wait_ge(x_out_s, 1 + 16 * b)
                for k in range(NB):
                    act.wait_ge(ssm_psum, 1 + NB * b + k + 1)
                    bank = ps[:, 2 + k % 4, :]
                    src, dst = ((bank, dt_in), (bank[0:2 * NS, :], bc), (bank, bcs[:, max(k - 2, 0), :]))[min(k, 2)]
                    act.activation(dst, src, ACT.Copy).then_inc(ssm_moved, 1)
                    if k >= 3 and k % 2 == 1 and (k - 3) // 2 < DC:
                        d = (k - 3) // 2
                        act.wait_ge(dt_psum, 1 + DC * b + d + 1)
                        act.activation(dt[:, d, :], ps[:, 6 + d % 2, :], ACT.Identity,
                                       bias=bdt[:, d:d + 1]).then_inc(dt_z, 1)
                    if k in (20, 24):
                        g = (k - 20) // 4
                        act.wait_ge(dt_z, 1 + DC * b + DC)
                        act.activation(soft[g][:, :, :], dt[:, 4 * g:4 * g + 4, :], ACT.Abs).then_inc(dt_abs, 1)
                        act.wait_ge(dt_abs, 1 + 2 * b + g + 1)
                        act.activation(soft[g][:, :, :], soft[g][:, :, :], ACT.Exp, scale=-1.0).then_inc(dt_e, 1)
                    if k in (28, 31):
                        g = (k - 28) // 3
                        act.wait_ge(dt_e, 1 + 2 * b + g + 1)
                        act.activation(soft[g][:, :, :], soft[g][:, :, :], ACT.Ln, bias=1.0).then_inc(dt_log, 1)
                act.wait_ge(ssm_moved, 1 + NB * b + NB)
                act.wait_ge(dt_ready, 1 + 2 * b + 2)
                for d in range(DC):
                    for n in range(NS):
                        k = NS * d + n
                        act.wait_ge(scanned, 1 + NU * b + max(k - 1, 0))
                        act.activation(ps[:, 2 + k % 2, :], dt[:, d, :], ACT.Exp,
                                       scale=neg_a[:, d, n:n + 1]).then_inc(da_ready, 1)
                        if n == 8:
                            act.wait_ge(gate_psum, 1 + DC * b + d + 1)
                            act.activation(gate[:, d, :], ps[:, 7, :], ACT.Copy).then_inc(gate_moved, 1)
                for g in range(2):
                    act.wait_ge(gate_moved, 1 + DC * b + DC)
                    act.activation(gate[:, 4 * g:4 * g + 4, :], gate[:, 4 * g:4 * g + 4, :], ACT.Silu).then_inc(gate_ready, 1)

            columns(0)
            with act.Fori(0, B - 1) as b:
                batch(b)
                columns(b + 1)
            batch(B - 1)

        @block.tensor
        def _(pe):

            def in_projection(b):
                pe.wait_ge(w_in_in, 17)
                pe.wait_ge(ln.xT_ready, 1 + HC * b + HC)
                pe.wait_ge(added, 1 + TT * b)
                for c in range(DC):
                    pe.wait_ge(conv_done, 1 + DC * b + max(c - 5, 0))
                    for h in range(HC):
                        last = pe.matmul(ps[:, 2 + c % 6, :], w_in[:, h, c * P:(c + 1) * P], xT[:, h, :],
                                         start=(h == 0), stop=(h == HC - 1))
                    last.then_inc(hs_psum, 1)

            def batch(b):
                in_projection(b)
                pe.wait_ge(hs_ready, 1 + DC * b + DC)
                pe.wait_ge(w_x_in, 33)
                for k in range(NB):
                    pe.wait_ge(ssm_moved, 1 + NB * b + max(k - 3, 0))
                    bank = ps[:, 2 + k % 4, :]
                    if k < 2:
                        for c in range(DC):
                            last = pe.matmul((bank, bank[0:2 * NS, :])[k],
                                             (w_x[:, c, 0:RK], w_x[:, c, RK:])[k], hs[:, c, :],
                                             start=(c == 0), stop=(c == DC - 1))
                    else:
                        pe.wait_ge(ssm_moved, 1 + NB * b + 2)
                        last = pe.matmul(bank, ident[0:2 * NS, k - 2:k - 1].to_broadcast([2 * NS, P]), bc,
                                         start=True, stop=True)
                    last.then_inc(ssm_psum, 1)
                    if k >= 3 and k % 2 == 1 and (k - 3) // 2 < DC:
                        d = (k - 3) // 2
                        pe.wait_ge(dt_z, 1 + DC * b + max(d - 1, 0))
                        pe.matmul(ps[:, 6 + d % 2, :], w_dt[:, d * P:(d + 1) * P], dt_in,
                                  start=True, stop=True).then_inc(dt_psum, 1)
                pe.wait_ge(ssm_moved, 1 + NB * b + NB)
                for d in range(DC):
                    pe.wait_ge(y_read, 1 + DC * b + max(d - 1, 0))
                    for n in range(NS):
                        if n == 4:
                            pe.wait_ge(gate_moved, 1 + DC * b + d)
                            pe.wait_ge(dt_z, 1 + DC * b + DC)
                            for h in range(HC):
                                last = pe.matmul(ps[:, 7, :], w_in[:, h, DI + d * P:DI + (d + 1) * P], xT[:, h, :],
                                                 start=(h == 0), stop=(h == HC - 1))
                            last.then_inc(gate_psum, 1)
                        k = NS * d + n
                        pe.wait_ge(hc_ready, 1 + NU * b + k + 1)
                        pe.matmul(ps[:, d % 2, :], ident, hc[:, k % 4, :],
                                  start=(n == 0), stop=(n == NS - 1)).then_inc(summed, 1)
                pe.wait_ge(w_out_in, 17)
                for i in range(TT):
                    for d in range(DC):
                        pe.wait_ge(yg_ready, 1 + 2 * b + d // 4 + 1)
                        last = pe.matmul(ps[:, 4 + i, :], gate[:, d, i * P:(i + 1) * P], w_out[:, d, :],
                                         start=(d == 0), stop=(d == DC - 1))
                    last.then_inc(o_ready, 1)

            def turn_rows(b):
                pe.wait_ge(y_read, 1 + DC * b)
                ln.tensor(pe, b)

            turn_rows(0)
            with pe.Fori(0, B - 1) as b:
                batch(b)
                turn_rows(b + 1)
            batch(B - 1)

        @block.vector
        def _(dve):
            own = Chain(dve, v_own, 29)
            dve.wait_ge(a_exp, 2)
            dve.tensor_scalar(neg_a[:, :, :], neg_a[:, :, :], -1.0, None, ALU.mult).then_inc(a_ready, 1)

            def times_hs(b, d):
                dve.tensor_tensor(u[:, d % 2, :], dt[:, d, :], hs[:, d, :], ALU.mult).then_inc(u_ready, 1)

            def scan(b, k):
                dve.wait_ge(da_ready, 1 + NU * b + k + 1)
                dve.wait_ge(db_ready, 1 + NU // 4 * b + k // 4 + 1)
                dve.wait_ge(hc_ready, 1 + NU * b + max(k - 2, 0))
                dve.tensor_tensor_scan(ps[:, 4 + k % 3, :], ps[:, 2 + k % 2, :], db[k // 4 % 2][:, k % 4, :], 0.0,
                                       ALU.mult, ALU.add).then_inc(scanned, 1)

            def times_c(b, k):
                dve.wait_ge(scanned, 1 + NU * b + k + 1)
                dve.wait_ge(summed, 1 + NU * b + max(k - 3, 0))
                dve.tensor_tensor(hc[:, k % 4, :], ps[:, 4 + k % 3, :], bcs[:, NS + k % NS, :],
                                  ALU.mult).then_inc(hc_ready, 1)

            def finish(b, d):
                dve.wait_ge(summed, 1 + NU * b + NS * (d + 1))
                dve.scalar_tensor_tensor(hs[:, d, :], hs[:, d, :], skip[:, d:d + 1], ps[:, d % 2, :],
                                         ALU.mult, ALU.add).then_inc(y_read, 1)

            def layer_norm(b):
                dve.wait_ge(rows_in, 1 + 16 * b + 16)
                ln.vector(dve, own, b, ln.xn)

            def batch(b, last_one=False):
                for c in range(DC):
                    dve.wait_ge(hs_psum, 1 + DC * b + c + 1)
                    dve.wait_ge(yg_ready, 1 + 2 * b)
                    src = ps[:, 2 + c % 6, :]
                    own.inc(dve.tensor_scalar(hs[:, c, :], src, taps[:, c, KC - 1:KC], None, ALU.mult))
                    for j in range(1, KC):
                        own.wait()
                        last = dve.scalar_tensor_tensor(hs[:, c, j:], src[:, 0:T - j], taps[:, c, KC - 1 - j:KC - j],
                                                        hs[:, c, j:], ALU.mult, ALU.add)
                        if j < KC - 1:
                            own.inc(last)
                    last.then_inc(conv_done, 1)
                for g in range(2):
                    dve.wait_ge(dt_log, 1 + 2 * b + g + 1)
                    dve.scalar_tensor_tensor(dt[:, 4 * g:4 * g + 4, :], dt[:, 4 * g:4 * g + 4, :], 0.0,
                                             soft[g][:, :, :], ALU.max, ALU.add).then_inc(dt_ready, 1)
                dve.wait_ge(dt_ready, 1 + 2 * b + 2)
                dve.wait_ge(ssm_moved, 1 + NB * b + NB)
                times_hs(b, 0)
                for k in range(NU):
                    scan(b, k)
                    if k:
                        times_c(b, k - 1)
                    if k % NS == 8 and k // NS + 1 < DC:
                        times_hs(b, k // NS + 1)
                    if k % NS == 3 and k >= NS:
                        finish(b, k // NS - 1)
                times_c(b, NU - 1)
                finish(b, DC - 1)
                dve.wait_ge(y_read, 1 + DC * b + DC)
                for g in range(2):
                    dve.wait_ge(gate_ready, 1 + 2 * b + g + 1)
                    dve.tensor_tensor(gate[:, 4 * g:4 * g + 4, :], gate[:, 4 * g:4 * g + 4, :],
                                      hs[:, 4 * g:4 * g + 4, :], ALU.mult).then_inc(yg_ready, 1)
                if not last_one:
                    layer_norm(b + 1)
                dve.wait_ge(x_in_s, 1 + 16 * b + 16)
                for i in range(TT):
                    dve.wait_ge(o_ready, 1 + TT * b + i + 1)
                    dve.tensor_tensor(x[:, i, :], ps[:, 4 + i, :], x[:, i, :], ALU.add).then_inc(added, 1)

            layer_norm(0)
            with dve.Fori(0, B - 1) as b:
                own.turn(b)
                batch(b)
                own.end()
            own.turn(B - 1)
            batch(B - 1, True)


NH, NKV, DH = 16, 4, 128
MEM = T
KT = (MEM + T) // P


def attention_inputs(i):
    f32 = np.float32
    inv_freq = (f32(1) / f32(10000) ** (np.arange(0, DH, 2, dtype=f32) / f32(DH))).astype(f32)
    angle = np.outer(np.arange(T, dtype=f32), inv_freq).astype(f32)
    half = np.cos(angle), np.sin(angle)
    rope = np.stack([np.concatenate([half[0], half[0]], 1), np.concatenate([-half[1], half[1]], 1)])
    late = np.where(np.arange(P)[None, :] > np.arange(P)[:, None], f32(NEG), f32(0))
    norm_rows = np.stack([i["L1_xattn_q_norm_w"], np.roll(i["L1_xattn_q_norm_w"], DH // 2),
                          i["L1_xattn_k_norm_w"], np.roll(i["L1_xattn_k_norm_w"], DH // 2)])
    return {
        "rope": rope.astype(f32),
        "late": late.astype(f32),
        "norm_rows": norm_rows,
        **{n: i[f"L1_xattn_{n}"] for n in ("wq", "wk", "wv", "wo", "wk_ctx", "wv_ctx")},
    }


def context_attention(nc, ps, ident, identb, eps, eps6, x_in, x_out, dram):
    SCALE = float(DH) ** -0.5
    HG = NH // NKV
    with ExitStack() as ctx:
        st = Stage(nc, ctx, "ca")
        x = st.sb("x", [P, TT, H])
        xT = st.sb("xT", [P, HC, T])
        ln = Columns(st, ps, ident, eps, xT)
        wq = st.sb("wq", [P, HC, NH * DH])
        wo = st.sb("wo", [P, NH, H])
        qT = st.sb("qT", [P, NH, T])
        kT = st.sb("kT", [P, NKV, MEM + T])
        v = st.sb("v", [P, KT, NKV * DH])
        tables = st.sb("tables", [P, 4, TT, DH])
        norm_rows = st.sb("norm_rows", [P, 4, DH])
        late = st.sb("late", [P, P])
        lateb = st.sb("lateb", [P, P], BF16)
        prob = st.sb("prob", [P, 2, MEM + T])
        pT = [st.sb("pT0", [P, KT, T]), st.sb("pT1", [P, KT, T])]
        memT = pT[0][:, 0:HC, :]
        w_kv = [pT[1][:, HC * s:HC * (s + 1), :] for s in range(2)]
        raw, sq, rot = ln.xn[:, 0:2, :], ln.xn[:, 2, :], ln.xn[:, 3, :]
        roped = prob[:, :, 0:512]
        ssq = st.sb("ssq", [P, TT, NH])
        q_scale = st.sb("q_scale", [P, TT, NH])
        ssk = st.sb("ssk", [P, 2, NKV])
        rk = st.sb("rk", [P, 2, NKV])
        top = st.sb("top", [P, 2])
        ntop = st.sb("ntop", [P, 2])
        total = st.sb("total", [P, 2])
        inv = st.sb("inv", [P, 2])

        x_in_s, x_out_s, mem_in = (st.sem(n) for n in ("x_in", "x_out", "mem_in"))
        tables_in, wq_in, wo_in = st.sem("tables_in"), st.sem("wq_in"), st.sem("wo_in")
        kv_in = [st.sem("wk_in"), st.sem("wkc_in"), st.sem("wv_in"), st.sem("wvc_in")]
        rows_in = st.sem("rows_in")
        tables_ready = st.sem("tables_ready")
        proj = st.sem("proj")
        moved = st.sem("moved")
        squared = st.sem("squared")
        reduced = st.sem("reduced")
        rms_k = st.sem("rms_k")
        rope_done = st.sem("rope_done")
        qk_turned = st.sem("qk_turned")
        qk_moved = st.sem("qk_moved")
        rms_q = st.sem("rms_q")
        scale_ready = st.sem("scale_ready")
        scores = st.sem("scores")
        tops = st.sem("tops")
        exps = st.sem("exps")
        normed = st.sem("normed")
        turned = st.sem("turned")
        pT_moved = st.sem("pT_moved")
        pv_done = st.sem("pv_done")
        out_moved = st.sem("out_moved")
        o_ready, added, v_own = st.sem("o_ready"), st.sem("added"), st.sem("v_own")
        block = st.block()

        turning = [("q", i, g) for i in range(TT) for g in range(NH // 4)] \
            + [("k", i, 0) for i in range(TT)] + [("kc", i, 1) for i in range(TT)]
        groups = turning + [("v", i, 2) for i in range(TT)] + [("vc", i, 3) for i in range(TT)]
        NJ, NQ, NR = len(groups), TT * NH // 4, len(turning)
        units = [(h, i) for h in range(NH) for i in range(TT)]
        NU = len(units)

        @block.sync
        def _(sp):
            sp.dma_start(ln.xn[:, 0:2, :].rearrange("p a (i d) -> p a i d", i=TT),
                         dram["rope"].rearrange("a (i p) d -> p a i d", p=P)).then_inc(tables_in, 16)
            sp.dma_start(norm_rows[:, :, :], dram["norm_rows"].rearrange("(a r) d -> a r d", a=1)
                         .to_broadcast([P, 4, DH])).then_inc(tables_in, 16)
            sp.dma_start(late[:, :], dram["late"]).then_inc(tables_in, 16)

            def load_early(b):
                sp.dma_start(memT[:, :, :], dram["ctxT"].rearrange("b (c p) m -> b p c m", p=P)[b]).then_inc(mem_in, 16)
                for k, n in enumerate(("wk", "wk_ctx")):
                    sp.dma_start(w_kv[k], dram[n].rearrange("(c p) n -> p c n", p=P)).then_inc(kv_in[k], 16)

            def load_values(b):
                for k, n in ((2, "wv"), (3, "wv_ctx")):
                    sp.wait_ge(proj, 1 + NJ * b + NQ + TT * (k - 1))
                    sp.dma_start(w_kv[k % 2], dram[n].rearrange("(c p) n -> p c n", p=P)).then_inc(kv_in[k], 16)

            sp.wait_ge(tables_ready, 2)
            sp.dma_start(ln.xn[:, :, :], rows_of(x_in, 0)).then_inc(rows_in, 16)
            sp.dma_start(wq[:, :, :], dram["wq"].rearrange("(c p) n -> p c n", p=P)).then_inc(wq_in, 16)
            load_early(0)
            sp.dma_start(wo[:, :, :], dram["wo"].rearrange("(h p) n -> p h n", p=P)).then_inc(wo_in, 16)
            sp.dma_start(x[:, :, :], rows_of(x_in, 0)).then_inc(x_in_s, 16)
            with sp.Fori(0, B - 1) as b:
                load_values(b)
                sp.wait_ge(rope_done, 1 + NR * b + NR)
                sp.dma_start(ln.xn[:, :, :], rows_of(x_in, b + 1)).then_inc(rows_in, 16)
                sp.wait_ge(pv_done, 1 + NH * b + NH)
                load_early(b + 1)
                sp.wait_ge(added, 1 + TT * b + TT)
                sp.dma_start(rows_of(x_out, b), x[:, :, :]).then_inc(x_out_s, 16)
                sp.wait_ge(x_out_s, 1 + 16 * b + 16)
                sp.dma_start(x[:, :, :], rows_of(x_in, b + 1)).then_inc(x_in_s, 16)
            load_values(B - 1)
            sp.wait_ge(added, 1 + TT * B)
            sp.dma_start(rows_of(x_out, B - 1), x[:, :, :]).then_inc(x_out_s, 16)
            sp.wait_ge(x_out_s, 1 + 16 * B)

        @block.scalar
        def _(act):
            def move_turned(b, j):
                act.wait_ge(qk_turned, 1 + NR * b + j + 1)
                n, i, g = groups[j]
                dst = {"q": qT[:, 4 * g:4 * g + 4, i * P:(i + 1) * P],
                       "k": kT[:, :, MEM + i * P:MEM + (i + 1) * P],
                       "kc": kT[:, :, i * P:(i + 1) * P]}[n]
                act.activation(dst, ps[:, 4 + j % 2, :].rearrange("p (a s) -> p a s", a=4),
                               ACT.Copy).then_inc(qk_moved, 1)

            def exp(b, k):
                h, i = units[k]
                w = MEM + (i + 1) * P
                act.wait_ge(tops, 1 + NU * b + k + 1)
                act.wait_ge(turned, 1 + 2 * NU * b + max(2 * (k - 1), 0))
                act.activation(prob[:, k % 2, 0:w],
                               ps[:, 2 * (k % 2):2 * (k % 2) + 2, :].rearrange("p a n -> p (a n)")[:, 0:w], ACT.Exp,
                               bias=ntop[:, k % 2:k % 2 + 1], scale=q_scale[:, i, h:h + 1],
                               accum_out=total[:, k % 2:k % 2 + 1]).then_inc(exps, 1)

            def move_p(b, k):
                h, i = units[k]
                if i == 0:
                    act.wait_ge(pv_done, 1 + NH * b + max(h - 1, 0))
                for half, n in ((0, TT), (1, i + 1)):
                    act.wait_ge(turned, 1 + 2 * NU * b + 2 * k + half + 1)
                    act.activation(pT[h % 2][:, TT * half:TT * half + n, i * P:(i + 1) * P],
                                   ps[:, 4 + half, 0:n * P].rearrange("p (a s) -> p a s", a=n),
                                   ACT.Copy).then_inc(pT_moved, 1)

            def columns(b):
                ln.scalar_sd(act, b)
                ln.scalar_move(act, b)

            def batch(b):
                for j, (n, i, g) in enumerate(groups):
                    act.wait_ge(proj, 1 + NJ * b + j + 1)
                    if j >= NR:
                        act.activation(v[:, i + (TT if n == "v" else 0), :], ps[:, j % 4, :], ACT.Copy).then_inc(moved, 1)
                        if j == NR:
                            move_turned(b, NR - 1)
                        continue
                    act.wait_ge(rope_done, 1 + NR * b + max(j - 1, 0))
                    act.activation(raw[:, j % 2, :], ps[:, j % 4, :], ACT.Copy).then_inc(moved, 1)
                    act.wait_ge(moved, 1 + NJ * b + j + 1)
                    act.wait_ge(reduced, 1 + NR * b + j)
                    act.activation(sq, raw[:, j % 2, :], ACT.Square).then_inc(squared, 1)
                    if n != "q":
                        act.wait_ge(reduced, 1 + NR * b + j + 1)
                        act.activation(rk[:, j % 2, :], ssk[:, j % 2, :], ACT.Sqrt, bias=eps6,
                                       scale=1.0 / DH).then_inc(rms_k, 1)
                    if j:
                        move_turned(b, j - 1)
                act.activation(q_scale[:, :, :], ssq[:, :, :], ACT.Sqrt, bias=eps6, scale=1.0 / DH).then_inc(rms_q, 1)
                exp(b, 0)
                exp(b, 1)
                for k in range(NU):
                    move_p(b, k)
                    if k + 2 < NU:
                        exp(b, k + 2)

            columns(0)
            with act.Fori(0, B - 1) as b:
                batch(b)
                columns(b + 1)
            batch(B - 1)

        @block.tensor
        def _(pe):

            def batch(b):
                pe.wait_ge(tables_ready, 2)
                pe.wait_ge(wq_in, 17)
                pe.wait_ge(added, 1 + TT * b)
                pe.wait_ge(ln.xT_ready, 1 + HC * b + HC)
                pe.wait_ge(mem_in, 1 + 16 * b + 16)

                def turn_qk(j):
                    pe.wait_ge(rope_done, 1 + NR * b + j + 1)
                    pe.wait_ge(qk_moved, 1 + NR * b + max(j - 1, 0))
                    for a in range(4):
                        last = pe.transpose(ps[:, 4 + j % 2, a * P:(a + 1) * P],
                                            roped[:, j % 2, a * P:(a + 1) * P], ident)
                    last.then_inc(qk_turned, 1)

                for j, (n, i, g) in enumerate(groups):
                    if n != "q" and i == 0:
                        pe.wait_ge(kv_in[g], 1 + 16 * b + 16)
                    pe.wait_ge(moved, 1 + NJ * b + max(j - 3, 0))
                    src = memT if n in ("kc", "vc") else xT
                    for c in range(HC):
                        w = wq[:, c, g * 512:(g + 1) * 512] if n == "q" else w_kv[g % 2][:, c, :]
                        last = pe.matmul(ps[:, j % 4, :], src[:, c, i * P:(i + 1) * P], w,
                                         start=(c == 0), stop=(c == HC - 1))
                    last.then_inc(proj, 1)
                    if 1 <= j <= NR:
                        turn_qk(j - 1)
                pe.wait_ge(qk_moved, 1 + NR * b + NR)
                pe.wait_ge(moved, 1 + NJ * b + NJ)

                def score(k):
                    h, i = units[k]
                    pe.wait_ge(exps, 1 + NU * b + max(k - 1, 0))
                    q = qT[:, h, i * P:(i + 1) * P]
                    pe.matmul(ps[:, 2 * (k % 2), :], q, kT[:, h // HG, 0:MEM], start=True, stop=True)
                    own = ps[:, 2 * (k % 2) + 1, :]
                    pe.matmul(own[:, 0:(i + 1) * P], q, kT[:, h // HG, MEM:MEM + (i + 1) * P],
                              start=True, stop=False, skip_group_check=True)
                    pe.matmul(own[:, i * P:(i + 1) * P], identb, lateb[:, :], start=False, stop=True,
                              skip_group_check=True).then_inc(scores, 1)

                def turn(k):
                    h, i = units[k]
                    pe.wait_ge(normed, 1 + NU * b + k + 1)
                    for half, n in ((0, TT), (1, i + 1)):
                        pe.wait_ge(pT_moved, 1 + 2 * NU * b + max(2 * k + half - 1, 0))
                        for a in range(n):
                            m = TT * half + a
                            last = pe.transpose(ps[:, 4 + half, a * P:(a + 1) * P], prob[:, k % 2, m * P:(m + 1) * P], ident)
                        last.then_inc(turned, 1)

                def pv(h, part):
                    if part == 0:
                        pe.wait_ge(pT_moved, 1 + 2 * NU * b + 2 * TT * (h + 1))
                        pe.wait_ge(out_moved, 1 + NH * b + max(h - 1, 0))
                    for m in (2 * part, 2 * part + 1):
                        s0 = max(m - TT, 0) * P
                        last = pe.matmul(ps[:, 6 + h % 2, s0:T], v[:, m, h // HG * DH:(h // HG + 1) * DH],
                                         pT[h % 2][:, m, s0:T], start=(m == 0), stop=(m == KT - 1),
                                         skip_group_check=True)
                    if part == TT - 1:
                        last.then_inc(pv_done, 1)

                score(0)
                score(1)
                for k in range(NU + 6):
                    if k < NU:
                        turn(k)
                    if k + 2 < NU:
                        score(k + 2)
                    if k >= TT + 0 and (k - TT) // TT < NH:
                        pv((k - TT) // TT, (k - TT) % TT)
                pe.wait_ge(out_moved, 1 + NH * b + NH)
                pe.wait_ge(wo_in, 17)
                for i in range(TT):
                    for h in range(NH):
                        last = pe.matmul(ps[:, 4 + i, :], qT[:, h, i * P:(i + 1) * P], wo[:, h, :],
                                         start=(h == 0), stop=(h == NH - 1))
                    last.then_inc(o_ready, 1)

            ln.tensor(pe, 0)
            with pe.Fori(0, B - 1) as b:
                batch(b)
                ln.tensor(pe, b + 1)
            batch(B - 1)

        @block.vector
        def _(dve):
            own = Chain(dve, v_own, 211)
            dve.wait_ge(tables_in, 49)
            dve.tensor_copy(lateb[:, :], late[:, :])
            for a in range(4):
                last = dve.tensor_tensor(tables[:, a, :, :], ln.xn[:, a % 2, :].rearrange("p (i d) -> p i d", i=TT),
                                         norm_rows[:, a:a + 1, :].to_broadcast([P, TT, DH]), ALU.mult)
            last.then_inc(tables_ready, 1)
            dve.wait_ge(tables_ready, 2)

            def by_head(t, lo=0, hi=DH):
                return t.rearrange("p (a d) -> p a d", d=DH)[:, :, lo:hi]

            def rope(b, j):
                n, i, g = groups[j]
                t = 0 if n == "q" else 2
                out, q = roped[:, j % 2, :], raw[:, j % 2, :]
                dve.wait_ge(squared, 1 + NR * b + j + 1)
                ss = ssq[:, i, 4 * g:4 * g + 4] if n == "q" else ssk[:, j % 2, :]
                dve.tensor_reduce(ss, by_head(sq), AX.X, ALU.add).then_inc(reduced, 1)
                dve.wait_ge(qk_turned, 1 + NR * b + max(j - 1, 0))
                if n == "kc":
                    own.inc(dve.tensor_tensor(by_head(out), by_head(q), norm_rows[:, 2:3, :].to_broadcast([P, 4, DH]),
                                              ALU.mult))
                    own.wait()
                else:
                    own.inc(dve.tensor_tensor(by_head(out), by_head(q),
                                              tables[:, t, i:i + 1, :].to_broadcast([P, 4, DH]), ALU.mult))
                    dve.wait_ge(rope_done, 1 + NR * b + j)
                    for lo in (0, DH // 2):
                        hi, other = lo + DH // 2, DH // 2 - lo
                        own.inc(dve.tensor_tensor(by_head(rot, lo, hi), by_head(q, other, other + DH // 2),
                                                  tables[:, t + 1, i:i + 1, lo:hi].to_broadcast([P, 4, DH // 2]),
                                                  ALU.mult))
                    own.wait()
                    last = dve.tensor_tensor(out, out, rot, ALU.add)
                    if n == "q":
                        last.then_inc(rope_done, 1)
                        return
                    own.inc(last)
                dve.wait_ge(rms_k, 1 + 2 * TT * b + j - NQ + 1)
                own.inc(dve.reciprocal(rk[:, j % 2, :], rk[:, j % 2, :]))
                own.wait()
                dve.tensor_tensor(by_head(out), by_head(out),
                                  rk[:, j % 2, :].rearrange("p (a o) -> p a o", o=1).to_broadcast([P, 4, DH]),
                                  ALU.mult).then_inc(rope_done, 1)

            def maximum(b, k):
                h, i = units[k]
                w = MEM + (i + 1) * P
                dve.wait_ge(scores, 1 + NU * b + k + 1)
                own.inc(dve.tensor_reduce(top[:, k % 2:k % 2 + 1],
                                          ps[:, 2 * (k % 2):2 * (k % 2) + 2, :].rearrange("p a n -> p (a n)")[:, 0:w],
                                          AX.X, ALU.max))
                own.wait()
                dve.tensor_scalar(ntop[:, k % 2:k % 2 + 1], top[:, k % 2:k % 2 + 1], q_scale[:, i, h:h + 1], -1.0,
                                  ALU.mult, ALU.mult).then_inc(tops, 1)

            def normalise(b, k):
                h, i = units[k]
                w = MEM + (i + 1) * P
                dve.wait_ge(exps, 1 + NU * b + k + 1)
                own.inc(dve.reciprocal(inv[:, k % 2:k % 2 + 1], total[:, k % 2:k % 2 + 1]))
                own.wait()
                dve.tensor_scalar(prob[:, k % 2, 0:w], prob[:, k % 2, 0:w], inv[:, k % 2:k % 2 + 1], None,
                                  ALU.mult).then_inc(normed, 1)

            def move_out(b, h):
                dve.wait_ge(pv_done, 1 + NH * b + h + 1)
                dve.tensor_copy(qT[:, h, :], ps[:, 6 + h % 2, :]).then_inc(out_moved, 1)

            def layer_norm(b):
                dve.wait_ge(rows_in, 1 + 16 * b + 16)
                ln.vector(dve, own, b, ln.xn)

            def batch(b, last_one=False):
                for j in range(NR):
                    rope(b, j)
                dve.wait_ge(rms_q, 1 + b + 1)
                own.inc(dve.reciprocal(q_scale[:, :, :], q_scale[:, :, :]))
                own.wait()
                own.inc(dve.tensor_scalar(q_scale[:, :, :], q_scale[:, :, :], SCALE, None, ALU.mult))
                own.wait()
                maximum(b, 0)
                for k in range(NU):
                    normalise(b, k)
                    if k + 1 < NU:
                        maximum(b, k + 1)
                    if k >= 2 * TT + 1 and k % TT == 1:
                        move_out(b, k // TT - 2)
                move_out(b, NH - 2)
                move_out(b, NH - 1)
                if not last_one:
                    layer_norm(b + 1)
                dve.wait_ge(x_in_s, 1 + 16 * b + 16)
                for i in range(TT):
                    dve.wait_ge(o_ready, 1 + TT * b + i + 1)
                    dve.tensor_tensor(x[:, i, :], ps[:, 4 + i, :], x[:, i, :], ALU.add).then_inc(added, 1)

            layer_norm(0)
            with dve.Fori(0, B - 1) as b:
                own.turn(b)
                batch(b)
                own.end()
            own.turn(B - 1)
            batch(B - 1, True)



NE, TOP, SEL, FI = 64, 8, 4, 192
NT = B * TT
SLOT_TILES = B * T * TOP // P + NE


def expert_inputs(i):
    return {
        "gateT": i["L1_ffn_gate_weight"].T,
        "similarity": i["L1_ffn_similarity"],
        "guT": i["L1_ffn_gate_up_proj"].transpose(0, 2, 1),
        "downT": i["L1_ffn_down_proj"].transpose(0, 2, 1),
        "count_row": np.arange(SLOT_TILES, dtype=np.float32).reshape(1, SLOT_TILES),
        "before": np.triu(np.ones((P, P), np.float32), 1),
        "choice_before": np.tril(np.ones((TOP, TOP), np.float32), -1).reshape(1, TOP * TOP),
        "token_numbers": 1 + np.arange(B * T, dtype=np.float32).reshape(NT, P).T,
        "spare_numbers": 1 + B * T + np.arange(P, dtype=np.float32).reshape(P, 1),
    }


def route(nc, ps, ident, ones, eps, x_in, dram, keep):
    xn_rows, out_rows = keep["xn_rows"], keep["out_rows"]
    tokens, slot_share = keep["tokens"], keep["slot_share"]
    tile_expert, tile_ring, expert_end = keep["tile_expert"], keep["tile_ring"], keep["expert_end"]
    with ExitStack() as ctx:
        st = Stage(nc, ctx, "rt")
        x = st.sb("x", [P, NT, H])
        xT = st.sb("xT", [P, HC, T])
        ln = Columns(st, ps, ident, eps, None)
        gateT = st.sb("gateT", [P, HC, NE])
        sim = st.sb("sim", [NE, NE])
        count = st.sb("count", [P, SLOT_TILES])
        before = st.sb("before", [P, P])
        upto = st.sb("upto", [NE, NE])
        token_numbers = st.sb("token_numbers", [P, NT])
        spare_numbers = st.sb("spare_numbers", [P, 1])
        choice_before = st.sb("choice_before", [P, TOP, TOP])
        again = st.sb("again", [P, NT, TOP])
        share = st.sb("share", [P, NT, TOP])
        entry = st.sb("entry", [P, 2, NT, TOP])
        slot_tile = st.sb("slot_tile", [P, NT, TOP])
        slot_row = st.sb("slot_row", [P, NT, TOP])
        RING = 4
        at_row = st.sb("at_row", [P, RING, P])
        at_tile = st.sb("at_tile", [P, RING, 2, SLOT_TILES])
        taken = st.sb("taken", [P, 3, SLOT_TILES])
        prob = st.sb("prob", [P, NT, NE])
        top, total = st.sb("top", [P, NT]), st.sb("total", [P, NT])
        index = st.sb("index", [P, NT, TOP], U32)
        indexf = st.sb("indexf", [P, NT, TOP])
        hot = st.sb("hot", [P, NT, TOP, NE])
        chosen = st.sb("chosen", [P, 2, NT, NE])
        turned_sb = st.sb("turned_sb", [NE, 2, P])
        primary = st.sb("primary", [NE, NE])
        cand = st.sb("cand", [NE, NE])
        cbest = st.sb("cbest", [NE, TOP])
        cindex = st.sb("cindex", [NE, TOP], U32)
        cindexf = st.sb("cindexf", [NE, TOP])
        moves = st.sb("moves", [NE, 3])
        to = st.sb("to", [NE, NE])
        toT = st.sb("toT", [NE, NE])
        member = st.sb("member", [P, NT, NE])
        earlier = st.sb("earlier", [P, NT + 1, NE])
        tiles = st.sb("tiles", [NE, 1])
        end = st.sb("end", [NE, 1])
        base = st.sb("base", [P, NE])
        place = st.sb("place", [P, 2, NT, NE])
        past = st.sb("past", [NE, SLOT_TILES])
        slotf = st.sb("slotf", [P, NT, TOP])
        expertf = st.sb("expertf", [1, SLOT_TILES])
        fours = st.sb("fours", [1, SLOT_TILES])
        zero = st.sb("zero", [P, H])
        const_in, x_in_s, xn_out = st.sem("const_in"), st.sem("x_in"), st.sem("xn_out")
        x_rest_in = st.sem("x_rest_in")
        logits, logits_moved = st.sem("logits"), st.sem("logits_moved")
        shifted, exps = st.sem("shifted"), st.sem("exps")
        zero_set = st.sem("zero_set")
        x_stored = st.sem("x_stored")
        chosen_ready, counts = st.sem("chosen_ready"), st.sem("counts")
        to_ready = st.sem("to_ready")
        to_turned, to_moved = st.sem("to_turned"), st.sem("to_moved")
        later_turned, later_moved = st.sem("later_turned"), st.sem("later_moved")
        sent = st.sem("sent")
        member_ready, ranked = st.sem("member_ready"), st.sem("ranked")
        tiles_ready, based = st.sem("tiles_ready"), st.sem("based")
        past_ready, past_summed = st.sem("past_ready"), st.sem("past_summed")
        place_ready = st.sem("place_ready")
        slots_ready = st.sem("slots_ready")
        at_row_ready, at_tile_ready = st.sem("at_row_ready"), st.sem("at_tile_ready")
        entered = st.sem("entered")
        v_own = st.sem("v_own")
        block = st.block()

        @block.sync
        def _(sp):
            tiles_of_x = x_in.rearrange("(n p) h -> p n h", p=P)
            sp.dma_start(x[:, 0:TT, :], tiles_of_x[:, 0:TT]).then_inc(x_in_s, 16)
            sp.dma_start(x[:, TT:, :], tiles_of_x[:, TT:]).then_inc(x_rest_in, 16)
            sp.dma_start(gateT[:, :, :], dram["gateT"].rearrange("(c p) e -> p c e", p=P)).then_inc(const_in, 16)
            sp.dma_start(sim[:, :], dram["similarity"]).then_inc(const_in, 16)
            sp.dma_start(count[:, :], dram["count_row"].to_broadcast([P, SLOT_TILES])).then_inc(const_in, 16)
            sp.dma_start(before[:, :], dram["before"]).then_inc(const_in, 16)
            sp.dma_start(token_numbers[:, :], dram["token_numbers"]).then_inc(const_in, 16)
            sp.dma_start(spare_numbers[:, :], dram["spare_numbers"]).then_inc(const_in, 16)
            sp.dma_start(choice_before[:, :, :].rearrange("p r q -> p (r q)"),
                         dram["choice_before"].to_broadcast([P, TOP * TOP])).then_inc(const_in, 16)
            sp.wait_ge(zero_set, 2)
            sp.dma_start(xn_rows[B * T:B * T + P], zero[:, :]).then_inc(x_stored, 16)
            sp.dma_start(out_rows[B * T:B * T + P], zero[:, :]).then_inc(x_stored, 16)
            with sp.Fori(0, B) as b:
                sp.wait_ge(ln.xn_ready, 1 + b + 1)
                sp.dma_start(rows_of(xn_rows[0:B * T], b), ln.xn[:, :, :]).then_inc(xn_out, 16)
            sp.wait_ge(x_in_s, 17)
            sp.wait_ge(x_rest_in, 17)
            sp.dma_start(out_rows[0:B * T].rearrange("(n p) h -> p n h", p=P), x[:, :, :]).then_inc(x_stored, 16)
            sp.wait_ge(xn_out, 1 + 16 * B)
            sp.wait_ge(x_stored, 1 + 16 * 3)

        @block.gpsimd
        def _(pool):
            pool.wait_ge(slots_ready, 2)
            for k in range(NT * TOP):
                n, r = k // TOP, k % TOP
                if k >= RING:
                    pool.wait_ge(entered, 1 + k - RING + 1)
                pool.tensor_scalar(at_row[:, k % RING, :], count[:, 0:P], slot_row[:, n, r:r + 1], None,
                                   ALU.is_equal).then_inc(at_row_ready, 1)

        @block.scalar
        def _(act):
            with act.Fori(0, B) as b:
                ln.scalar_sd(act, b)
                act.wait_ge(logits, 1 + b)
                for c in range(HC):
                    act.wait_ge(ln.turned, 1 + HC * b + c + 1)
                    act.activation(xT[:, c, :], ps[:, c % 2, :], ACT.Copy).then_inc(ln.xT_ready, 1)
            act.wait_ge(logits, 1 + B)
            act.activation(prob[:, :, :].rearrange("p n e -> p (n e)"),
                           ps[:, 2:4, :].rearrange("p a n -> p (a n)"), ACT.Copy).then_inc(logits_moved, 1)
            act.wait_ge(shifted, 2)
            act.activation(prob[:, :, :], prob[:, :, :], ACT.Exp).then_inc(exps, 1)
            act.wait_ge(to_turned, 2)
            act.activation(toT[:, :], ps[0:NE, 0, 0:NE], ACT.Copy).then_inc(to_moved, 1)
            for k in range(2 * NT):
                act.wait_ge(later_turned, 1 + k + 1)
                if k >= 2:
                    act.wait_ge(sent, 1 + k - 1)
                act.activation(turned_sb[:, k % 2, :], ps[0:NE, k % 2, 0:P], ACT.Copy).then_inc(later_moved, 1)

        @block.tensor
        def _(pe):
            pe.wait_ge(const_in, 1 + 16 * 7)
            every_logit = ps[:, 2:4, :].rearrange("p a n -> p (a n)")
            with pe.Fori(0, B) as b:
                ln.tensor(pe, b)
                pe.wait_ge(ln.xT_ready, 1 + HC * b + HC)
                for i in range(TT):
                    for c in range(HC):
                        last = pe.matmul(every_logit[:, bass.ds(TT * NE * b + i * NE, NE)],
                                         xT[:, c, i * P:(i + 1) * P], gateT[:, c, :],
                                         start=(c == 0), stop=(c == HC - 1))
                last.then_inc(logits, 1)
            pe.wait_ge(chosen_ready, 1 + B)
            for s in range(2):
                for n in range(NT):
                    pe.matmul(ps[:, 4, s * NE:(s + 1) * NE], ones, chosen[:, s, n, :],
                              start=(n == 0), stop=(n == NT - 1))
            for s in range(2):
                for n in range(NT):
                    last = pe.matmul(ps[0:NE, 5, s:s + 1], chosen[:, s, n, :], ones[:, 0:1],
                                     start=(n == 0), stop=(n == NT - 1))
            last.then_inc(counts, 1)
            pe.wait_ge(to_ready, 2)
            pe.transpose(ps[0:NE, 0, 0:NE], to[:, :], ident[0:NE, 0:NE]).then_inc(to_turned, 1)
            pe.wait_ge(to_moved, 2)

            def times(k, rows, right):
                n = k % NT
                if k >= 2:
                    pe.wait_ge(later_moved, 1 + k - 1)
                pe.transpose(ps[0:NE, k % 2, 0:P], rows, ident).then_inc(later_turned, 1)
                pe.wait_ge(later_moved, 1 + k + 1)
                pe.matmul(ps[:, 6 + n // 8, n % 8 * NE:(n % 8 + 1) * NE], turned_sb[:, k % 2, :], right,
                          start=True, stop=True).then_inc(sent, 1)

            for n in range(NT):
                times(n, chosen[:, 1, n, :], to[:, :])
            pe.wait_ge(member_ready, 2)
            for n in range(NT):
                out = ps[:, 2 + n // 8, n % 8 * NE:(n % 8 + 1) * NE]
                pe.matmul(out, before[:, :], member[:, n, :], start=True, stop=False)
                pe.matmul(out, ones, earlier[:, n, :], start=False, stop=True)
            pe.matmul(ps[0:NE, 5, 4:5], earlier[:, NT, :], ones[:, 0:1], start=True, stop=True).then_inc(ranked, 1)
            pe.wait_ge(tiles_ready, 2)
            pe.matmul(ps[:, 4, 0:NE], tiles[:, 0:1].to_broadcast([NE, P]), before[0:NE, 0:NE], start=True, stop=True)
            pe.matmul(ps[0:NE, 4, NE:NE + 1], upto[:, :], tiles[:, :], start=True, stop=True)
            pe.matmul(ps[0:1, 4, 2 * NE:3 * NE], tiles[:, 0:1], upto[:, :], start=True, stop=True).then_inc(based, 1)
            pe.wait_ge(past_ready, 2)
            pe.matmul(ps[:, 5, 0:SLOT_TILES], ones[0:NE, :], past[:, :], start=True, stop=True).then_inc(past_summed, 1)
            pe.wait_ge(place_ready, 2)
            for n in range(NT):
                times(NT + n, place[:, 0, n, :], toT[:, :])
            pe.wait_ge(slots_ready, 2)
            for k in range(NT * TOP):
                pe.wait_ge(at_row_ready, 1 + k + 1)
                pe.wait_ge(at_tile_ready, 1 + k + 1)
                pe.matmul(ps[:, 0, 0:2 * SLOT_TILES], at_row[:, k % RING, :],
                          at_tile[:, k % RING, :, :].rearrange("p a j -> p (a j)"),
                          start=(k == 0), stop=(k == NT * TOP - 1)).then_inc(entered, 1)

        @block.vector
        def _(dve):
            own = Chain(dve, v_own, 5)
            dve.memset(zero[:, :], 0.0).then_inc(zero_set, 1)

            def layer_norm(b):
                own.turn(b)
                dve.wait_ge(xn_out, 1 + 16 * b)
                ln.vector(dve, own, b, x[:, :, :].rearrange("p (b i) h -> p b i h", b=B)[:, b])
                own.end()

            dve.wait_ge(x_in_s, 17)
            layer_norm(0)
            dve.wait_ge(x_rest_in, 17)
            with dve.Fori(1, B) as b:
                layer_norm(b)

            def step(instruction):
                own.inc(instruction)
                own.wait()

            def bc(t, shape):
                return t.rearrange("p (n o) -> p n o", o=1).to_broadcast(shape)

            def flat(t):
                return t.rearrange("p n e -> p (n e)")

            own.turn(B)
            dve.wait_ge(logits_moved, 2)
            step(dve.tensor_reduce(top[:, :], prob[:, :, :], AX.X, ALU.max))
            dve.tensor_tensor(prob[:, :, :], prob[:, :, :], bc(top[:, :], [P, NT, NE]), ALU.subtract).then_inc(shifted, 1)
            dve.wait_ge(exps, 2)
            step(dve.tensor_reduce(total[:, :], prob[:, :, :], AX.X, ALU.add))
            step(dve.reciprocal(total[:, :], total[:, :]))
            step(dve.tensor_tensor(prob[:, :, :], prob[:, :, :], bc(total[:, :], [P, NT, NE]), ALU.mult))
            for n in range(NT):
                own.inc(dve.max(share[:, n, :], prob[:, n, :]))
            own.wait()
            for n in range(NT):
                own.inc(dve.max_index(index[:, n, :], share[:, n, :], prob[:, n, :]))
            own.wait()
            step(dve.tensor_copy(indexf[:, :, :], index[:, :, :]))
            step(dve.tensor_reduce(total[:, :], share[:, :, :], AX.X, ALU.add))
            step(dve.tensor_scalar(total[:, :], total[:, :], 1e-12, None, ALU.max))
            step(dve.reciprocal(total[:, :], total[:, :]))
            step(dve.tensor_tensor(share[:, :, :], share[:, :, :], bc(total[:, :], [P, NT, TOP]), ALU.mult))
            dve.wait_ge(const_in, 1 + 16 * 7)
            for b in range(B):
                for n in range(TT * b, TT * b + TT):
                    own.inc(dve.tensor_tensor(hot[:, n, :, :], bc(indexf[:, n, :], [P, TOP, NE]),
                                              count[:, 0:NE].rearrange("p (o e) -> p o e", o=1)
                                              .to_broadcast([P, TOP, NE]), ALU.is_equal))
                own.wait()
                for s in range(2):
                    for n in range(TT * b, TT * b + TT):
                        last = dve.tensor_reduce(chosen[:, s, n, :],
                                                 hot[:, n, s * SEL:(s + 1) * SEL, :].rearrange("p r e -> p e r"),
                                                 AX.X, ALU.add)
                last.then_inc(chosen_ready, 1)

            eye = ident[0:NE, 0:NE]
            step(dve.tensor_tensor(upto[:, :], before[0:NE, 0:NE], eye, ALU.add))
            step(dve.tensor_tensor(cand[:, :], sim[:, :], eye, ALU.mult))
            step(dve.tensor_tensor(sim[:, :], sim[:, :], cand[:, :], ALU.subtract))
            step(dve.tensor_tensor(sim[:, :], sim[:, :], eye, ALU.add))
            dve.wait_ge(counts, 2)
            step(dve.tensor_scalar(primary[:, :], ps[0:NE, 4, 0:NE], 0.5, None, ALU.is_ge))
            step(dve.tensor_tensor(cand[:, :], sim[:, :], primary[:, :], ALU.mult))
            step(dve.tensor_scalar(primary[:, :], primary[:, :], -NEG, NEG, ALU.mult, ALU.add))
            step(dve.tensor_tensor(cand[:, :], cand[:, :], primary[:, :], ALU.add))
            step(dve.max(cbest[:, :], cand[:, :]))
            step(dve.max_index(cindex[:, :], cbest[:, :], cand[:, :]))
            step(dve.tensor_copy(cindexf[:, :], cindex[:, :]))
            step(dve.tensor_scalar(moves[:, 0:1], ps[0:NE, 5, 0:1], 0.5, None, ALU.is_lt))
            step(dve.tensor_scalar(moves[:, 1:2], ps[0:NE, 5, 1:2], 0.5, None, ALU.is_ge))
            step(dve.tensor_scalar(moves[:, 2:3], cbest[:, 0:1], 0.5, None, ALU.is_ge))
            step(dve.tensor_tensor(moves[:, 0:1], moves[:, 0:1], moves[:, 1:2], ALU.mult))
            step(dve.tensor_tensor(moves[:, 0:1], moves[:, 0:1], moves[:, 2:3], ALU.mult))
            step(dve.tensor_scalar(to[:, :], count[0:NE, 0:NE], cindexf[:, 0:1], None, ALU.is_equal))
            step(dve.tensor_tensor(to[:, :], to[:, :], eye, ALU.subtract))
            step(dve.tensor_scalar(to[:, :], to[:, :], moves[:, 0:1], None, ALU.mult))
            dve.tensor_tensor(to[:, :], to[:, :], eye, ALU.add).then_inc(to_ready, 1)

            both = ps[:, 6:8, :].rearrange("p a n -> p (a n)")
            own.inc(dve.memset(earlier[:, 0, :], 0.0))
            dve.wait_ge(sent, 1 + NT)
            step(dve.tensor_tensor(flat(member[:, :, :]), both, flat(chosen[:, 0, :, :]), ALU.add))
            step(dve.tensor_scalar(member[:, :, :], member[:, :, :], 0.5, None, ALU.is_ge))
            for n in range(NT):
                last = dve.tensor_tensor(earlier[:, n + 1, :], earlier[:, n, :], member[:, n, :], ALU.add)
                if n < NT - 1:
                    step(last)
            last.then_inc(member_ready, 1)
            dve.wait_ge(ranked, 2)
            step(dve.tensor_scalar(tiles[:, :], ps[0:NE, 5, 4:5], 1.0 / P, (P - 1) / (2.0 * P), ALU.mult, ALU.add))
            step(dve.tensor_scalar(tiles[:, :], tiles[:, :], ROUND, None, ALU.add))
            dve.tensor_scalar(tiles[:, :], tiles[:, :], ROUND, 1.0, ALU.subtract, ALU.max).then_inc(tiles_ready, 1)
            dve.wait_ge(based, 2)
            step(dve.tensor_scalar(base[:, :], ps[:, 4, 0:NE], float(P), None, ALU.mult))
            step(dve.tensor_copy(end[:, :], ps[0:NE, 4, NE:NE + 1]))
            own.inc(dve.tensor_copy(expert_end[:, :], ps[0:1, 4, 2 * NE:3 * NE]))
            dve.tensor_scalar(past[:, :], count[0:NE, :], end[:, 0:1], None, ALU.is_ge).then_inc(past_ready, 1)
            dve.tensor_tensor(place[:, 0, :, :], ps[:, 2:4, :].rearrange("p a (n e) -> p (a n) e", e=NE),
                              base[:, :].rearrange("p (o e) -> p o e", o=1).to_broadcast([P, NT, NE]),
                              ALU.add).then_inc(place_ready, 1)
            dve.wait_ge(past_summed, 2)
            step(dve.tensor_scalar(expertf[:, :], ps[0:1, 5, 0:SLOT_TILES], float(NE - 1), None, ALU.min))
            own.inc(dve.tensor_copy(tile_expert[:, :], expertf[:, :]))
            step(dve.tensor_scalar(fours[:, :], expertf[:, :], 0.25, -0.375, ALU.mult, ALU.add))
            step(dve.tensor_scalar(fours[:, :], fours[:, :], ROUND, None, ALU.add))
            step(dve.tensor_scalar(fours[:, :], fours[:, :], ROUND, None, ALU.subtract))
            own.inc(dve.scalar_tensor_tensor(tile_ring[:, :], fours[:, :], -4.0, expertf[:, :], ALU.mult, ALU.add))
            dve.wait_ge(sent, 1 + 2 * NT)
            step(dve.tensor_copy(flat(place[:, 1, :, :]), both))
            for s in range(2):
                for n in range(NT):
                    part = hot[:, n, s * SEL:(s + 1) * SEL, :]
                    own.inc(dve.tensor_tensor(part, part, place[:, s, n:n + 1, :].to_broadcast([P, SEL, NE]), ALU.mult))
            own.wait()
            step(dve.tensor_reduce(slotf[:, :, :], hot[:, :, :, :], AX.X, ALU.add))
            same = hot[:, :, :, 0:TOP]
            for n in range(NT):
                own.inc(dve.tensor_tensor(same[:, n, :, :], bc(slotf[:, n, :], [P, TOP, TOP]),
                                          slotf[:, n:n + 1, :].to_broadcast([P, TOP, TOP]), ALU.is_equal))
            own.wait()
            weighed = hot[:, :, :, TOP:2 * TOP]
            for n in range(NT):
                own.inc(dve.tensor_tensor(weighed[:, n, :, :], same[:, n, :, :],
                                          share[:, n:n + 1, :].to_broadcast([P, TOP, TOP]), ALU.mult))
                own.inc(dve.tensor_copy(entry[:, 0, n, :], token_numbers[:, n:n + 1].to_broadcast([P, TOP])))
            own.wait()
            own.inc(dve.tensor_reduce(entry[:, 1, :, :], weighed, AX.X, ALU.add))
            for n in range(NT):
                own.inc(dve.tensor_tensor(same[:, n, :, :], same[:, n, :, :], choice_before[:, :, :], ALU.mult))
            own.wait()
            step(dve.tensor_reduce(again[:, :, :], same, AX.X, ALU.max))
            own.inc(dve.tensor_scalar(again[:, :, :], again[:, :, :], -1.0, 1.0, ALU.mult, ALU.add))
            step(dve.tensor_scalar(slot_tile[:, :, :], slotf[:, :, :], 1.0 / P, (1 - P) / (2.0 * P), ALU.mult, ALU.add))
            step(dve.tensor_scalar(slot_tile[:, :, :], slot_tile[:, :, :], ROUND, None, ALU.add))
            step(dve.tensor_scalar(slot_tile[:, :, :], slot_tile[:, :, :], ROUND, None, ALU.subtract))
            own.inc(dve.scalar_tensor_tensor(slot_row[:, :, :], slot_tile[:, :, :], -float(P), slotf[:, :, :],
                                             ALU.mult, ALU.add))
            for a in range(2):
                last = dve.tensor_tensor(entry[:, a, :, :], entry[:, a, :, :], again[:, :, :], ALU.mult)
                if a == 0:
                    own.inc(last)
            last.then_inc(slots_ready, 1)
            dve.wait_ge(slots_ready, 2)
            for k in range(NT * TOP):
                n, r = k // TOP, k % TOP
                if k >= RING:
                    dve.wait_ge(entered, 1 + k - RING + 1)
                for a in range(2):
                    last = dve.tensor_scalar(at_tile[:, k % RING, a, :], count[:, :], slot_tile[:, n, r:r + 1],
                                             entry[:, a, n, r:r + 1], ALU.is_equal, ALU.mult)
                last.then_inc(at_tile_ready, 1)
            dve.wait_ge(entered, 1 + NT * TOP)
            number, free, spare = (taken[:, a, :] for a in range(3))
            own.inc(dve.tensor_scalar(number, ps[:, 0, 0:SLOT_TILES], 1.0, None, ALU.subtract))
            own.inc(dve.tensor_copy(slot_share[:, :], ps[:, 0, SLOT_TILES:2 * SLOT_TILES]))
            own.wait()
            step(dve.tensor_scalar(free, number, 0.0, spare_numbers[:, 0:1], ALU.is_lt, ALU.mult))
            step(dve.tensor_tensor(spare, number, free, ALU.add))
            step(dve.tensor_copy(tokens[:, :], spare))


def experts(nc, ps, ident, ones, eps, x_in, x_out, dram):
    xn_rows = nc.dram_tensor("xn_rows", (B * T + P, H), F32, kind="Internal").ap()
    out_rows = nc.dram_tensor("out_rows", (B * T + P, H), F32, kind="Internal").ap()
    with ExitStack() as outer:
        held = Stage(nc, outer, "ex")
        keep = {
            "xn_rows": xn_rows, "out_rows": out_rows,
            "tile_expert": held.sb("tile_expert", [1, SLOT_TILES], I32),
            "tile_ring": held.sb("tile_ring", [1, SLOT_TILES], I32),
            "expert_end": held.sb("expert_end", [1, NE], I32),
            "tokens": held.sb("tokens", [P, SLOT_TILES], U32),
            "slot_share": held.sb("slot_share", [P, SLOT_TILES]),
        }
        route(nc, ps, ident, ones, eps, x_in, dram, keep)
        slot_products(nc, ps, ident, dram, x_out, keep)


def slot_products(nc, ps, ident, dram, x_out, keep):
    xn_rows, out_rows, tokens, slot_share = (keep[n] for n in ("xn_rows", "out_rows", "tokens", "slot_share"))
    tile_expert, tile_ring, expert_end = keep["tile_expert"], keep["tile_ring"], keep["expert_end"]
    FH = FI // 2
    D = 4
    with ExitStack() as ctx:
        st = Stage(nc, ctx, "sp")
        R = 4
        w_gu = st.sb("w_gu", [P, R * HC, 2 * FI])
        w_d = st.sb("w_d", [FH, R * 2, H])
        idx = [st.sb(f"idx{s}", [P, 1], U32) for s in range(D)]
        out_idx = [st.sb(f"out_idx{s}", [P, 1], U32) for s in range(D)]
        xg = [st.sb(f"xg{s}", [P, H]) for s in range(D)]
        y = [st.sb(f"y{s}", [P, H]) for s in range(D)]
        xgT = st.sb("xgT", [P, 2, HC, P])
        act_g = st.sb("act_g", [P, 2, FI])
        hid = st.sb("hid", [P, 2, FI])
        hidT = st.sb("hidT", [FH, 2, 2, P])
        w_in = [st.sem(f"w_in{s}") for s in range(R)]
        experts_in = st.sem("experts_in")
        gathered = [st.sem(f"gathered{s}", True) for s in range(D)]
        y_added = st.sem("y_added", True)
        out_idx_ready = st.sem("out_idx_ready")
        x_out_s = st.sem("x_out")
        idx_ready = st.sem("idx_ready")
        x_turned = st.sem("x_turned")
        x_moved = st.sem("x_moved")
        gu_done = st.sem("gu_done")
        silu = st.sem("silu")
        hid_ready = st.sem("hid_ready")
        h_turned = st.sem("h_turned")
        h_moved = st.sem("h_moved")
        o_done = st.sem("o_done")
        y_ready = st.sem("y_ready")
        passed = st.sem("passed")
        block = st.block()

        def pipeline(eng, steps, peeled=D):
            for j in range(peeled):
                steps(j, j % D)
            with eng.Fori(peeled, SLOT_TILES - D, D) as j0:
                j0 = nc.s_assert_within(j0, peeled, SLOT_TILES - 2 * D)
                for s in range(D):
                    steps(j0 + s, s)
            for s in range(D):
                steps(SLOT_TILES - D + s, s)

        def exists(j):
            return not isinstance(j, int) or 0 <= j < SLOT_TILES

        def ring(eng, sem, per, j, s, start=1):
            eng.wait_ge(sem[s], start + per // D * (j - s) + per)

        def reused(j):
            return not isinstance(j, int) or j >= D

        def reused2(j):
            return not isinstance(j, int) or j >= 2

        @block.sync
        def _(sp):
            def load(e, s, end):
                if end is not None:
                    sp.wait_ge(o_done, 1 + end)
                sp.dma_start(w_gu[:, HC * s:HC * (s + 1), :],
                             dram["guT"].rearrange("e (c p) n -> e p c n", p=P)[e]).then_inc(w_in[s], 16)
                sp.dma_start(w_d[:, 2 * s:2 * s + 2, :],
                             dram["downT"].rearrange("e (c p) n -> e p c n", p=FH)[e]).then_inc(w_in[s], 16)

            def tell(e, s):
                sp.wait_ge(w_in[s], 1 + 32 * ((e - s) // R) + 32 if isinstance(e, int) else 1 + 32 // R * (e - s) + 32)
                sp.sem_inc(experts_in, 1)

            for e in range(R):
                load(e, e, None)
            for e in range(R - 1):
                tell(e, e)
            with sp.Fori(R, NE, R) as e0:
                e0 = nc.s_assert_within(e0, R, NE - R)
                for s in range(R):
                    end = sp.value_load(expert_end[0:1, bass.ds(e0 + (s - R), 1)], min_val=0, max_val=SLOT_TILES)
                    tell(e0 + (s - 1), (s - 1) % R)
                    load(e0 + s, s, end)
            tell(NE - 1, R - 1)
            sp.wait_ge(y_added, 16 * SLOT_TILES)
            sp.dma_start(x_out.rearrange("(p n) h -> p (n h)", p=P),
                         out_rows[0:B * T].rearrange("(p n) h -> p (n h)", p=P)).then_inc(x_out_s, 16)
            sp.wait_ge(x_out_s, 1 + 16)
        @block.gpsimd
        def _(pool):
            def gather(j, s):
                if not exists(j):
                    return
                if reused(j):
                    pool.wait_ge(x_turned, 1 + j - D + 1)
                pool.tensor_copy(idx[s][:, :], tokens[:, j:j + 1] if isinstance(j, int)
                                 else tokens[:, bass.ds(j, 1)]).then_inc(idx_ready, 1)
                pool.wait_ge(idx_ready, 1 + j + 1)
                pool.sem_inc(passed, 1)
                pool.indirect_dma_start(xg[s][:, :], None, xn_rows,
                                        bass.IndirectOffsetOnAxis(ap=idx[s][:, 0:1], axis=0)).then_inc(gathered[s], 16)

            def add_rows(j, s):
                pool.wait_ge(y_ready, 1 + j + 1)
                pool.tensor_copy(out_idx[s][:, :], tokens[:, j:j + 1] if isinstance(j, int)
                                 else tokens[:, bass.ds(j, 1)]).then_inc(out_idx_ready, 1)
                pool.wait_ge(out_idx_ready, 1 + j + 1)
                if not isinstance(j, int) or j:
                    pool.wait_ge(y_added, 16 * j)
                pool.sem_inc(passed, 1)
                pool.indirect_dma_start(out_rows, bass.IndirectOffsetOnAxis(ap=out_idx[s][:, 0:1], axis=0),
                                        y[s][:, :], None, compute_op=ALU.add).then_inc(y_added, 16)

            def steps(j, s):
                gather(j + 3, (s + 3) % D)
                if not isinstance(j, int) or j >= 3:
                    add_rows(j - 3, (s + 1) % D)

            for j in range(3):
                gather(j, j)
            pipeline(pool, steps)
            for j in range(SLOT_TILES - 3, SLOT_TILES):
                add_rows(j, j % D)

        @block.scalar
        def _(act):
            def move_x(j, s):
                if not exists(j):
                    return
                act.wait_ge(x_turned, 1 + j + 1)
                if reused2(j):
                    act.wait_ge(gu_done, 1 + j - 1)
                act.activation(xgT[:, s % 2, :, :], ps[:, s % 2, :], ACT.Copy).then_inc(x_moved, 1)

            def steps(j, s):
                if isinstance(j, int) and j == 0:
                    move_x(0, 0)
                move_x(j + 1, s + 1)
                act.wait_ge(gu_done, 1 + j + 1)
                if reused2(j):
                    act.wait_ge(hid_ready, 1 + j - 1)
                act.activation(act_g[:, s % 2, :], ps[:, 2 + s % 2, 0:FI], ACT.Silu).then_inc(silu, 1)
                if isinstance(j, int) and j == 0:
                    return
                move_h(j - 1, s + 1)

            def move_h(j, s):
                act.wait_ge(h_turned, 1 + j + 1)
                if reused2(j):
                    act.wait_ge(o_done, 1 + j - 1)
                act.activation(hidT[:, s % 2, :, :], ps[0:FH, 4 + s % 2, 0:2 * P], ACT.Copy).then_inc(h_moved, 1)

            pipeline(act, steps)
            move_h(SLOT_TILES - 1, 1)

        @block.tensor
        def _(pe):
            def at(table, j):
                return table[0:1, j:j + 1] if isinstance(j, int) else table[0:1, bass.ds(j, 1)]

            def place(j):
                return pe.value_load(at(tile_ring, j), min_val=0, max_val=R - 1)

            def turn_x(j, s):
                if not exists(j):
                    return
                ring(pe, gathered, 16, j, s, start=0)
                if reused2(j):
                    pe.wait_ge(x_moved, 1 + j - 1)
                for c in range(HC):
                    last = pe.transpose(ps[:, s % 2, c * P:(c + 1) * P], xg[s][:, c * P:(c + 1) * P], ident)
                last.then_inc(x_turned, 1)

            def gate_up(j, s):
                expert = pe.value_load(at(tile_expert, j), min_val=0, max_val=NE - 1)
                w = place(j)
                pe.wait_ge(experts_in, 2 + expert)
                pe.wait_ge(x_moved, 1 + j + 1)
                if reused2(j):
                    pe.wait_ge(hid_ready, 1 + j - 1)
                for c in range(HC):
                    last = pe.matmul(ps[:, 2 + s % 2, 0:2 * FI], xgT[:, s % 2, c, :], w_gu[:, w * HC + c, :],
                                     start=(c == 0), stop=(c == HC - 1))
                last.then_inc(gu_done, 1)

            def turn_h(j, s):
                pe.wait_ge(hid_ready, 1 + j + 1)
                if reused2(j):
                    pe.wait_ge(h_moved, 1 + j - 1)
                for a in range(2):
                    last = pe.transpose(ps[0:FH, 4 + s % 2, a * P:(a + 1) * P], hid[:, s % 2, a * FH:(a + 1) * FH], ident)
                last.then_inc(h_turned, 1)

            def down(j, s):
                w = place(j)
                pe.wait_ge(h_moved, 1 + j + 1)
                if reused2(j):
                    pe.wait_ge(y_ready, 1 + j - 1)
                for a in range(2):
                    last = pe.matmul(ps[:, 6 + s % 2, :], hidT[:, s % 2, a, :], w_d[:, w * 2 + a, :],
                                     start=(a == 0), stop=(a == 1))
                last.then_inc(o_done, 1)

            def steps(j, s):
                turn_x(j + 1, (s + 1) % D)
                gate_up(j, s)
                if not isinstance(j, int) or j >= 1:
                    turn_h(j - 1, (s + 3) % D)
                if not isinstance(j, int) or j >= 2:
                    down(j - 2, (s + 2) % D)

            turn_x(0, 0)
            pipeline(pe, steps)
            turn_h(SLOT_TILES - 1, D - 1)
            down(SLOT_TILES - 2, D - 2)
            down(SLOT_TILES - 1, D - 1)

        @block.vector
        def _(dve):
            def move_y(j, s):
                dve.wait_ge(o_done, 1 + j + 1)
                if reused(j):
                    dve.wait_ge(y_added, 16 * (j - D + 1))
                dve.tensor_scalar(y[s][:, :], ps[:, 6 + s % 2, :],
                                  slot_share[:, j:j + 1] if isinstance(j, int) else slot_share[:, bass.ds(j, 1)],
                                  None, ALU.mult).then_inc(y_ready, 1)

            def steps(j, s):
                dve.wait_ge(silu, 1 + j + 1)
                if reused2(j):
                    dve.wait_ge(h_turned, 1 + j - 1)
                dve.tensor_tensor(hid[:, s % 2, :], ps[:, 2 + s % 2, FI:2 * FI], act_g[:, s % 2, :],
                                  ALU.mult).then_inc(hid_ready, 1)
                if not isinstance(j, int) or j >= 2:
                    move_y(j - 2, (s + 2) % D)

            pipeline(dve, steps, 2 * D)
            move_y(SLOT_TILES - 2, D - 2)
            move_y(SLOT_TILES - 1, D - 1)


STAGES = "ABCDEF"


def columns_of(*vectors):
    return np.ascontiguousarray(np.concatenate([np.asarray(v).reshape(-1, P).T for v in vectors], axis=1))


def build(nc, dram, out):
    res = nc.dram_tensor("residual", (B * T, H), F32, kind="Internal").ap()
    with ExitStack() as ctx:
        ps = ctx.enter_context(nc.psum_tensor("ps", [P, 8, 512], F32))
        ident_t = ctx.enter_context(nc.sbuf_tensor("ident", [P, P], F32))
        ones_t = ctx.enter_context(nc.sbuf_tensor("ones", [P, P], F32))
        identb_t = ctx.enter_context(nc.sbuf_tensor("identb", [P, P], BF16))
        eps_t = ctx.enter_context(nc.sbuf_tensor("eps", [P, 2], F32))
        const_in = ctx.enter_context(nc.semaphore("const_in"))
        const_set = ctx.enter_context(nc.semaphore("const_set"))
        with nc.Block() as block:
            @block.sync
            def _(sp):
                sp.dma_start(ident_t[:, :], dram["identity"]).then_inc(const_in, 16)
                sp.wait_ge(const_in, 16)

            @block.vector
            def _(dve):
                dve.memset(ones_t[:, :], 1.0)
                dve.memset(eps_t[:, 0:1], 1e-5)
                dve.memset(eps_t[:, 1:2], 1e-6)
                dve.wait_ge(const_in, 16)
                dve.tensor_copy(identb_t[:, :], ident_t[:, :]).then_inc(const_set, 1)
                dve.wait_ge(const_set, 1)
        ident, identb, ones = ident_t[:, :], identb_t[:, :], ones_t[:, :]
        eps, eps6 = eps_t[:, 0:1], eps_t[:, 1:2]
        at = dram["x"]
        for s in STAGES:
            to = out if s == STAGES[-1] else res
            if s == "A":
                time_mix(nc, ps, ident, eps, at, to, dram["tm_cols"],
                         {"r": dram["Wr"], "k": dram["Wk"], "v": dram["Wv"], "o": dram["Wo"]})
            elif s == "B":
                memory_attention(nc, ps, ident, eps, at, to, dram["ctx"], dram["ctxT"], dram["mask"])
            elif s == "C":
                ternary_ffn(nc, ps, ident, identb, ones, eps, at, to, dram)
            elif s == "D":
                mamba(nc, ps, ident, eps, at, to, dram)
            elif s == "E":
                context_attention(nc, ps, ident, identb, eps, eps6, at, to, dram)
            elif s == "F":
                experts(nc, ps, ident, ones, eps, at, to, dram)
            at = to


def laid_out(i):
    i = {k: np.asarray(v) for k, v in i.items()}
    d = {
        "x": i["x"].reshape(B * T, H),
        "identity": np.eye(P, dtype=np.float32),
    }
    if "A" in STAGES:
        d["tm_cols"] = columns_of(*(i[f"L0_attn_{n}"] for n in (
            "ln_scale", "ln_bias", "mix_k", "mix_v", "mix_r", "time_first", "time_decay")))
        for n in "rkvo":
            d[f"W{n}"] = i[f"L0_attn_W{n}"]
    if "B" in STAGES or "E" in STAGES:
        d["ctx"] = i["ctx_2048"]
        d["ctxT"] = i["ctx_2048"].transpose(0, 2, 1)
        d["mask"] = i["mask_BxS2_bk0"]
    if "C" in STAGES:
        d |= ffn_inputs(i)
    if "D" in STAGES:
        d |= mamba_inputs(i)
    if "E" in STAGES:
        d |= attention_inputs(i)
    if "F" in STAGES:
        d |= expert_inputs(i)
    return {k: np.ascontiguousarray(v) for k, v in d.items()}


def kernel(**inputs):
    import concourse.bacc as bacc
    from concourse.bass_utils import run_bass_kernel_spmd

    nc = bacc.Bacc("TRN2", target_bir_lowering=False, num_devices=1)
    arrays = laid_out(inputs)
    dram = {n: nc.dram_tensor(f"in_{n}", a.shape, mybir.dt.from_np(a.dtype), kind="ExternalInput").ap()
            for n, a in arrays.items()}
    out = nc.dram_tensor("out", (B * T, H), F32, kind="ExternalOutput").ap()
    build(nc, dram, out)
    r = run_bass_kernel_spmd(nc, [{f"in_{n}": a for n, a in arrays.items()}], core_ids=[0])
    return r.results[0]["out"].reshape(B, T, H)
```
